# Optimizing a Trainium2 kernel written in Bass

```python
import numpy as np
import jax
import jax.numpy as jnp

def _softmax(x, axis=-1):
    return jax.nn.softmax(x, axis=axis)

def _gelu(x):
    return jax.nn.gelu(x, approximate=True)

def _silu(x):
    return jax.nn.silu(x)

def _sigmoid(x):
    return jax.nn.sigmoid(x)

def _layernorm(x, axis=-1, eps=1e-05):
    m = jnp.mean(x, axis=axis, keepdims=True)
    v = jnp.var(x, axis=axis, keepdims=True)
    return (x - m) / jnp.sqrt(v + eps)

def _scatter_add(tgt, idx, src, axis=0):
    return tgt.at[idx].add(src)

def _segment_sum(src, seg, n):
    return jax.ops.segment_sum(src, seg, n)
kernel_name = 'mk_audio_tower_d4_tok_aud1d512_r4_e3b573'

def setup_inputs(seed: int=0):
    np.random.seed(seed)
    _w = jnp.asarray

    def _rec_inputs():
        import jax
        import jax.numpy as jnp
        _rk = jax.random.key(seed)
        x = -0.00238186 + 1.00146 * jax.random.normal(jax.random.fold_in(_rk, 1), (64, 5000), jnp.float32)
        return x
    x = _rec_inputs()

    def _L0_tok_setup():
        import jax, jax.numpy as jnp
        import numpy as np
        B, E, G, P = (8, 16, 5000, 128)
        MASK_DENSITY = 0.1
        key = jax.random.key(seed)
        k_x, k_w, k_m = jax.random.split(key, 3)
        x = jax.random.normal(k_x, (B, G), dtype=jnp.float32)
        weight = jax.random.normal(k_w, (E, G, P), dtype=jnp.float32) * 0.01
        bias = jnp.zeros((E, P), dtype=jnp.float32)
        mask = (jax.random.uniform(k_m, (G, P)) < MASK_DENSITY).astype(jnp.float32)
        return {'x': x, 'weight': weight, 'bias': bias, 'mask': mask}
    _L0_tok_all = _L0_tok_setup()
    _L0_tok_in = {k: v for k, v in _L0_tok_all.items() if k in ('weight', 'bias', 'mask')}
    del _L0_tok_all

    def _L0_attn_setup():
        import jax, jax.numpy as jnp
        import numpy as np
        B, L, D_IN, H, N, R = (8, 512, 128, 256, 16, 64)
        EPS = 1e-05

        def _mamba(x, ln_gamma, ln_beta, W_in, conv_w, A, D, dt_W1, dt_b1, dt_W2, dt_b2, W_out):
            residual = x
            mu = jnp.mean(x, axis=-1, keepdims=True)
            var = jnp.mean((x - mu) ** 2, axis=-1, keepdims=True)
            xn = (x - mu) * jax.lax.rsqrt(var + EPS) * ln_gamma + ln_beta
            h = jnp.einsum('bld,hd->blh', xn, W_in)
            hc = jnp.transpose(h, (0, 2, 1))
            hc = jax.lax.conv_general_dilated(hc, conv_w, window_strides=(1,), padding=((1, 1),), feature_group_count=H, dimension_numbers=('NCH', 'OIH', 'NCH'))
            h = jnp.transpose(jax.nn.silu(hc), (0, 2, 1))
            dt = jax.nn.relu(jnp.einsum('blh,rh->blr', h, dt_W1) + dt_b1)
            dt = jax.nn.softplus(jnp.einsum('blr,hr->blh', dt, dt_W2) + dt_b2)
            A_neg = -jnp.exp(A)
            safe_A = jnp.where(jnp.abs(A_neg) < 1e-05, jnp.ones_like(A_neg), A_neg)

            def step(state, inp):
                x_t, dt_t = inp
                dA = A_neg * dt_t[..., None]
                discrete_A = jnp.exp(dA)
                discrete_B = (discrete_A - 1.0) / safe_A * dt_t[..., None]
                state = discrete_A * state + discrete_B * x_t[..., None]
                y = jnp.einsum('bhc,hc->bh', state, A) + D * x_t
                return (state, y)
            state0 = jnp.zeros((x.shape[0], H, N), x.dtype)
            xs = (jnp.transpose(h, (1, 0, 2)), jnp.transpose(dt, (1, 0, 2)))
            _, ys = jax.lax.scan(step, state0, xs)
            y = jnp.transpose(ys, (1, 0, 2))
            out = jnp.einsum('blh,dh->bld', y, W_out)
            return residual + out
        key = jax.random.key(seed)
        ks = jax.random.split(key, 12)
        s = lambda k, shape, sc=0.02: jax.random.normal(k, shape, dtype=jnp.float32) * sc
        return {'x': jax.random.normal(ks[0], (B, L, D_IN), dtype=jnp.float32), 'ln_gamma': jnp.ones((D_IN,), jnp.float32), 'ln_beta': jnp.zeros((D_IN,), jnp.float32), 'W_in': s(ks[1], (H, D_IN)), 'conv_w': s(ks[2], (H, 1, 3)), 'A': s(ks[3], (H, N), 0.01), 'D': jnp.ones((H,), jnp.float32), 'dt_W1': s(ks[4], (R, H)), 'dt_b1': jnp.zeros((R,), jnp.float32), 'dt_W2': s(ks[5], (H, R)), 'dt_b2': jnp.zeros((H,), jnp.float32), 'W_out': s(ks[6], (D_IN, H))}
    _L0_attn_all = _L0_attn_setup()
    _L0_attn_in = {k: v for k, v in _L0_attn_all.items() if k in ('ln_gamma', 'ln_beta', 'W_in', 'conv_w', 'A', 'D', 'dt_W1', 'dt_b1', 'dt_W2', 'dt_b2', 'W_out')}
    del _L0_attn_all

    def _L0_ffn_setup():
        import jax, jax.numpy as jnp
        import numpy as np
        CAPACITY_FACTOR = 1.2
        key = jax.random.key(seed)
        k1, k2, k3 = jax.random.split(key, 3)
        B, S, D, E = (8, 1024, 128, 16)
        x = jax.random.normal(k1, (B, S, D), dtype=jnp.float32)
        switch_w = jax.random.normal(k2, (E, D), dtype=jnp.float32) * 0.02
        switch_b = jnp.zeros((E,), dtype=jnp.float32)
        expert_w = jax.random.normal(k3, (E, D, D), dtype=jnp.float32) * 0.02
        expert_b = jnp.zeros((E, D), dtype=jnp.float32)
        return {'x': x, 'switch_w': switch_w, 'switch_b': switch_b, 'expert_w': expert_w, 'expert_b': expert_b}
    _L0_ffn_all = _L0_ffn_setup()
    _L0_ffn_in = {k: v for k, v in _L0_ffn_all.items() if k in ('switch_w', 'switch_b', 'expert_w', 'expert_b')}
    del _L0_ffn_all

    def _L1_attn_setup():
        import jax, jax.numpy as jnp
        import numpy as np
        N_HEAD = 8
        D_MODEL = 128
        D_HEAD = 64
        N_ROLL = 2
        SLEN = 512
        BSZ = 8
        EPS = 1e-05
        SCALE = D_HEAD ** (-0.5)

        def _dpfp(x):
            x = jnp.concatenate([jax.nn.relu(x), jax.nn.relu(-x)], axis=-1)
            x = jnp.concatenate([x * jnp.roll(x, i, axis=-1) for i in range(1, N_ROLL + 1)], axis=-1)
            return x / x.sum(-1, keepdims=True)
        key = jax.random.key(seed)
        k1, k2, k3 = jax.random.split(key, 3)
        h = jax.random.normal(k1, (SLEN, BSZ, D_MODEL), dtype=jnp.float32)
        W_qkvb = jax.random.normal(k2, (N_HEAD * (3 * D_HEAD + 1), D_MODEL), dtype=jnp.float32) * 0.02
        W_o = jax.random.normal(k3, (D_MODEL, N_HEAD * D_HEAD), dtype=jnp.float32) * 0.02
        ln_g = jnp.ones((D_MODEL,), dtype=jnp.float32)
        ln_b = jnp.zeros((D_MODEL,), dtype=jnp.float32)
        return {'h': h, 'W_qkvb': W_qkvb, 'W_o': W_o, 'ln_g': ln_g, 'ln_b': ln_b}
    _L1_attn_all = _L1_attn_setup()
    _L1_attn_in = {k: v for k, v in _L1_attn_all.items() if k in ('W_qkvb', 'W_o', 'ln_g', 'ln_b')}
    del _L1_attn_all

    def _L1_ffn_setup():
        import jax, jax.numpy as jnp
        import numpy as np
        S, B, I, O, H, E, K = (128, 32, 128, 128, 128, 8, 2)

        def _expert(x_seq, Wi, Wh, b, Wo, bo):
            Bsz = x_seq.shape[1]
            Hd = Wh.shape[0]

            def step(carry, xt):
                h, c = carry
                gates = xt @ Wi + h @ Wh + b
                i_, f_, g_, o_ = jnp.split(gates, 4, axis=-1)
                c = jax.nn.sigmoid(f_) * c + jax.nn.sigmoid(i_) * jnp.tanh(g_)
                h = jax.nn.sigmoid(o_) * jnp.tanh(c)
                return ((h, c), h @ Wo + bo)
            init = (jnp.zeros((Bsz, Hd), x_seq.dtype), jnp.zeros((Bsz, Hd), x_seq.dtype))
            _, ys = jax.lax.scan(step, init, x_seq)
            return ys
        key = jax.random.key(seed)
        ks = jax.random.split(key, 6)
        s = 0.02
        return {'x': jax.random.normal(ks[0], (S, B, I), dtype=jnp.float32), 'router_w': jax.random.normal(ks[1], (I, E), dtype=jnp.float32) * s, 'router_b': jnp.zeros((E,), dtype=jnp.float32), 'Wi': jax.random.normal(ks[2], (E, I, 4 * H), dtype=jnp.float32) * s, 'Wh': jax.random.normal(ks[3], (E, H, 4 * H), dtype=jnp.float32) * s, 'b': jnp.zeros((E, 4 * H), dtype=jnp.float32), 'Wo': jax.random.normal(ks[4], (E, H, O), dtype=jnp.float32) * s, 'bo': jnp.zeros((E, O), dtype=jnp.float32)}
    _L1_ffn_all = _L1_ffn_setup()
    _L1_ffn_in = {k: v for k, v in _L1_ffn_all.items() if k in ('router_w', 'router_b', 'Wi', 'Wh', 'b', 'Wo', 'bo')}
    del _L1_ffn_all

    def _L2_attn_setup():
        import jax, jax.numpy as jnp
        import numpy as np
        D_MODEL = 128
        D_QK = 128
        H = 8
        HEAD_DIM = D_QK // H
        V_DIM = D_MODEL // H
        PROJ_OUT = D_MODEL + 2 * D_QK + H
        key = jax.random.key(seed)
        k1, k2, k3, k4, k5 = jax.random.split(key, 5)
        B, S = (2, 512)
        x = jax.random.normal(k1, (B, S, D_MODEL), dtype=jnp.float32)
        s_in = 1.0 / np.sqrt(D_MODEL)
        Wvqkn_w = jax.random.uniform(k2, (PROJ_OUT, D_MODEL), jnp.float32, -s_in, s_in)
        Wvqkn_b = jax.random.uniform(k3, (PROJ_OUT,), jnp.float32, -s_in, s_in)
        out_w = jax.random.uniform(k4, (D_MODEL, D_MODEL), jnp.float32, -s_in, s_in)
        out_b = jax.random.uniform(k5, (D_MODEL,), jnp.float32, -s_in, s_in)
        return {'x': x, 'Wvqkn_w': Wvqkn_w, 'Wvqkn_b': Wvqkn_b, 'out_w': out_w, 'out_b': out_b}
    _L2_attn_all = _L2_attn_setup()
    _L2_attn_in = {k: v for k, v in _L2_attn_all.items() if k in ('Wvqkn_w', 'Wvqkn_b', 'out_w', 'out_b')}
    del _L2_attn_all

    def _L2_ffn_setup():
        import jax, jax.numpy as jnp
        import numpy as np
        BINS = jnp.array([-1.5, -1.0, -0.5, 0.0, 0.5, 1.0, 1.5], dtype=jnp.float32)
        N_BINS = BINS.shape[0] + 1
        INDEX = 0
        key = jax.random.key(seed)
        k1, k2 = jax.random.split(key)
        x = jax.random.normal(k1, (8, 1024, 128), dtype=jnp.float32)
        W = jax.random.normal(k2, (N_BINS, 128, 128), dtype=jnp.float32) * 0.02
        return {'x': x, 'W': W}
    _L2_ffn_all = _L2_ffn_setup()
    _L2_ffn_in = {k: v for k, v in _L2_ffn_all.items() if k in ('W',)}
    del _L2_ffn_all

    def _L3_attn_setup():
        import jax, jax.numpy as jnp
        import numpy as np
        import math
        key = jax.random.key(seed)
        k_x, k_q, k_k, k_v, k_o = jax.random.split(key, 5)
        B, S, D_IN, H, D_K, D_V, D_OUT = (1, 1024, 128, 8, 64, 64, 128)
        scale = 0.02
        return {'x': jax.random.normal(k_x, (B, S, D_IN), dtype=jnp.float32), 'W_q': jax.random.uniform(k_q, (H, D_IN, D_K), dtype=jnp.float32) * scale, 'W_k': jax.random.uniform(k_k, (H, D_IN, D_K), dtype=jnp.float32) * scale, 'W_v': jax.random.uniform(k_v, (H, D_IN, D_V), dtype=jnp.float32) * scale, 'W_o': jax.random.uniform(k_o, (H, D_V, D_OUT), dtype=jnp.float32) * scale}
    _L3_attn_all = _L3_attn_setup()
    _L3_attn_in = {k: v for k, v in _L3_attn_all.items() if k in ('W_q', 'W_k', 'W_v', 'W_o')}
    del _L3_attn_all

    def _L3_ffn_setup():
        import jax, jax.numpy as jnp
        import numpy as np
        G, H, DQK, DV, L, D_IN = (8, 16, 128, 128, 100, 128)
        FF = D_IN
        LSW = 1.0

        def _l2norm(x, d):
            n = jnp.maximum(jnp.linalg.norm(x, axis=-1, keepdims=True), 1e-12)
            return x / n * d ** 0.5
        key = jax.random.key(seed)
        ks = jax.random.split(key, 16)
        s = 0.02
        inp = {'x': jax.random.normal(ks[0], (4, 512, D_IN), dtype=jnp.float32), 'gamma_norm': jnp.ones((D_IN,), jnp.float32), 'Wq_w': jax.random.normal(ks[1], (D_IN, G * H * DQK), jnp.float32) * s, 'Wq_b': jnp.zeros((G * H * DQK,), jnp.float32), 'Wkv_w': jax.random.normal(ks[2], (D_IN, G * (DQK + DV)), jnp.float32) * s, 'Wkv_b': jnp.zeros((G * (DQK + DV),), jnp.float32), 'aw1_w': jax.random.normal(ks[3], (G * DQK, L), jnp.float32) * s, 'aw1_b': jnp.zeros((L,), jnp.float32), 'aw2_w': jax.random.normal(ks[4], (L, L), jnp.float32) * s, 'aw2_b': jnp.zeros((L,), jnp.float32), 'wz_g1': jnp.ones((G * H * DV,), jnp.float32), 'wz_w1': jax.random.normal(ks[5], (G * H * DV, 2 * FF), jnp.float32) * s, 'wz_b1': jnp.zeros((2 * FF,), jnp.float32), 'wz_g2': jnp.ones((2 * FF,), jnp.float32), 'wz_w2': jax.random.normal(ks[6], (2 * FF, FF), jnp.float32) * s, 'wz_b2': jnp.zeros((FF,), jnp.float32)}
        return inp
    _L3_ffn_all = _L3_ffn_setup()
    _L3_ffn_in = {k: v for k, v in _L3_ffn_all.items() if k in ('gamma_norm', 'Wq_w', 'Wq_b', 'Wkv_w', 'Wkv_b', 'aw1_w', 'aw1_b', 'aw2_w', 'aw2_b', 'wz_g1', 'wz_w1', 'wz_b1', 'wz_g2', 'wz_w2', 'wz_b2')}
    del _L3_ffn_all
    return {'x': x, 'L0_tok_weight': _L0_tok_in['weight'], 'L0_tok_bias': _L0_tok_in['bias'], 'L0_tok_mask': _L0_tok_in['mask'], 'L0_attn_ln_gamma': _L0_attn_in['ln_gamma'], 'L0_attn_ln_beta': _L0_attn_in['ln_beta'], 'L0_attn_W_in': _L0_attn_in['W_in'], 'L0_attn_conv_w': _L0_attn_in['conv_w'], 'L0_attn_A': _L0_attn_in['A'], 'L0_attn_D': _L0_attn_in['D'], 'L0_attn_dt_W1': _L0_attn_in['dt_W1'], 'L0_attn_dt_b1': _L0_attn_in['dt_b1'], 'L0_attn_dt_W2': _L0_attn_in['dt_W2'], 'L0_attn_dt_b2': _L0_attn_in['dt_b2'], 'L0_attn_W_out': _L0_attn_in['W_out'], 'L0_ffn_switch_w': _L0_ffn_in['switch_w'], 'L0_ffn_switch_b': _L0_ffn_in['switch_b'], 'L0_ffn_expert_w': _L0_ffn_in['expert_w'], 'L0_ffn_expert_b': _L0_ffn_in['expert_b'], 'L1_attn_W_qkvb': _L1_attn_in['W_qkvb'], 'L1_attn_W_o': _L1_attn_in['W_o'], 'L1_attn_ln_g': _L1_attn_in['ln_g'], 'L1_attn_ln_b': _L1_attn_in['ln_b'], 'L1_ffn_router_w': _L1_ffn_in['router_w'], 'L1_ffn_router_b': _L1_ffn_in['router_b'], 'L1_ffn_Wi': _L1_ffn_in['Wi'], 'L1_ffn_Wh': _L1_ffn_in['Wh'], 'L1_ffn_b': _L1_ffn_in['b'], 'L1_ffn_Wo': _L1_ffn_in['Wo'], 'L1_ffn_bo': _L1_ffn_in['bo'], 'L2_attn_Wvqkn_w': _L2_attn_in['Wvqkn_w'], 'L2_attn_Wvqkn_b': _L2_attn_in['Wvqkn_b'], 'L2_attn_out_w': _L2_attn_in['out_w'], 'L2_attn_out_b': _L2_attn_in['out_b'], 'L2_ffn_W': _L2_ffn_in['W'], 'L3_attn_W_q': _L3_attn_in['W_q'], 'L3_attn_W_k': _L3_attn_in['W_k'], 'L3_attn_W_v': _L3_attn_in['W_v'], 'L3_attn_W_o': _L3_attn_in['W_o'], 'L3_ffn_gamma_norm': _L3_ffn_in['gamma_norm'], 'L3_ffn_Wq_w': _L3_ffn_in['Wq_w'], 'L3_ffn_Wq_b': _L3_ffn_in['Wq_b'], 'L3_ffn_Wkv_w': _L3_ffn_in['Wkv_w'], 'L3_ffn_Wkv_b': _L3_ffn_in['Wkv_b'], 'L3_ffn_aw1_w': _L3_ffn_in['aw1_w'], 'L3_ffn_aw1_b': _L3_ffn_in['aw1_b'], 'L3_ffn_aw2_w': _L3_ffn_in['aw2_w'], 'L3_ffn_aw2_b': _L3_ffn_in['aw2_b'], 'L3_ffn_wz_g1': _L3_ffn_in['wz_g1'], 'L3_ffn_wz_w1': _L3_ffn_in['wz_w1'], 'L3_ffn_wz_b1': _L3_ffn_in['wz_b1'], 'L3_ffn_wz_g2': _L3_ffn_in['wz_g2'], 'L3_ffn_wz_w2': _L3_ffn_in['wz_w2'], 'L3_ffn_wz_b2': _L3_ffn_in['wz_b2']}

def reference(x, L0_tok_weight, L0_tok_bias, L0_tok_mask, L0_attn_ln_gamma, L0_attn_ln_beta, L0_attn_W_in, L0_attn_conv_w, L0_attn_A, L0_attn_D, L0_attn_dt_W1, L0_attn_dt_b1, L0_attn_dt_W2, L0_attn_dt_b2, L0_attn_W_out, L0_ffn_switch_w, L0_ffn_switch_b, L0_ffn_expert_w, L0_ffn_expert_b, L1_attn_W_qkvb, L1_attn_W_o, L1_attn_ln_g, L1_attn_ln_b, L1_ffn_router_w, L1_ffn_router_b, L1_ffn_Wi, L1_ffn_Wh, L1_ffn_b, L1_ffn_Wo, L1_ffn_bo, L2_attn_Wvqkn_w, L2_attn_Wvqkn_b, L2_attn_out_w, L2_attn_out_b, L2_ffn_W, L3_attn_W_q, L3_attn_W_k, L3_attn_W_v, L3_attn_W_o, L3_ffn_gamma_norm, L3_ffn_Wq_w, L3_ffn_Wq_b, L3_ffn_Wkv_w, L3_ffn_Wkv_b, L3_ffn_aw1_w, L3_ffn_aw1_b, L3_ffn_aw2_w, L3_ffn_aw2_b, L3_ffn_wz_g1, L3_ffn_wz_w1, L3_ffn_wz_b1, L3_ffn_wz_g2, L3_ffn_wz_w2, L3_ffn_wz_b2):
    import jax
    import jax.numpy as jnp

    def _L0_tok_ref(x, weight, bias, mask):
        import jax, jax.numpy as jnp
        import numpy as np
        B, E, G, P = (8, 16, 5000, 128)
        MASK_DENSITY = 0.1
        W = weight * mask[None, :, :]
        out = jnp.einsum('bg,egp->bep', x, W)
        return out + bias[None, :, :]

    def _L0_attn_ref(x, ln_gamma, ln_beta, W_in, conv_w, A, D, dt_W1, dt_b1, dt_W2, dt_b2, W_out):
        import jax, jax.numpy as jnp
        import numpy as np
        B, L, D_IN, H, N, R = (8, 512, 128, 256, 16, 64)
        EPS = 1e-05

        def _mamba(x, ln_gamma, ln_beta, W_in, conv_w, A, D, dt_W1, dt_b1, dt_W2, dt_b2, W_out):
            residual = x
            mu = jnp.mean(x, axis=-1, keepdims=True)
            var = jnp.mean((x - mu) ** 2, axis=-1, keepdims=True)
            xn = (x - mu) * jax.lax.rsqrt(var + EPS) * ln_gamma + ln_beta
            h = jnp.einsum('bld,hd->blh', xn, W_in)
            hc = jnp.transpose(h, (0, 2, 1))
            hc = jax.lax.conv_general_dilated(hc, conv_w, window_strides=(1,), padding=((1, 1),), feature_group_count=H, dimension_numbers=('NCH', 'OIH', 'NCH'))
            h = jnp.transpose(jax.nn.silu(hc), (0, 2, 1))
            dt = jax.nn.relu(jnp.einsum('blh,rh->blr', h, dt_W1) + dt_b1)
            dt = jax.nn.softplus(jnp.einsum('blr,hr->blh', dt, dt_W2) + dt_b2)
            A_neg = -jnp.exp(A)
            safe_A = jnp.where(jnp.abs(A_neg) < 1e-05, jnp.ones_like(A_neg), A_neg)

            def step(state, inp):
                x_t, dt_t = inp
                dA = A_neg * dt_t[..., None]
                discrete_A = jnp.exp(dA)
                discrete_B = (discrete_A - 1.0) / safe_A * dt_t[..., None]
                state = discrete_A * state + discrete_B * x_t[..., None]
                y = jnp.einsum('bhc,hc->bh', state, A) + D * x_t
                return (state, y)
            state0 = jnp.zeros((x.shape[0], H, N), x.dtype)
            xs = (jnp.transpose(h, (1, 0, 2)), jnp.transpose(dt, (1, 0, 2)))
            _, ys = jax.lax.scan(step, state0, xs)
            y = jnp.transpose(ys, (1, 0, 2))
            out = jnp.einsum('blh,dh->bld', y, W_out)
            return residual + out
        return _mamba(x, ln_gamma, ln_beta, W_in, conv_w, A, D, dt_W1, dt_b1, dt_W2, dt_b2, W_out)

    def _L0_ffn_ref(x, switch_w, switch_b, expert_w, expert_b):
        import jax, jax.numpy as jnp
        import numpy as np
        CAPACITY_FACTOR = 1.2
        B, S, D = x.shape
        E = switch_w.shape[0]
        N = B * S
        xf = x.reshape(N, D)
        logits = xf @ switch_w.T + switch_b
        probs = jax.nn.softmax(logits, axis=-1)
        route_probs = jnp.max(probs, axis=-1)
        routes = jnp.argmax(probs, axis=-1)
        oh = jax.nn.one_hot(routes, E, dtype=jnp.int32)
        pos = jnp.take_along_axis(jnp.cumsum(oh, axis=0), routes[:, None], axis=1)[:, 0] - 1
        capacity = int(CAPACITY_FACTOR * N / E)
        keep = pos < capacity
        buf = jnp.zeros((E, capacity, D), dtype=xf.dtype).at[routes, pos].set(xf)
        y = jnp.einsum('ecd,efd->ecf', buf, expert_w) + expert_b[:, None, :]
        gathered = y[routes, jnp.minimum(pos, capacity - 1)]
        out = jnp.where(keep[:, None], gathered, xf) * route_probs[:, None]
        return out.reshape(B, S, D)

    def _L1_attn_ref(h, W_qkvb, W_o, ln_g, ln_b):
        import jax, jax.numpy as jnp
        import numpy as np
        N_HEAD = 8
        D_MODEL = 128
        D_HEAD = 64
        N_ROLL = 2
        SLEN = 512
        BSZ = 8
        EPS = 1e-05
        SCALE = D_HEAD ** (-0.5)

        def _dpfp(x):
            x = jnp.concatenate([jax.nn.relu(x), jax.nn.relu(-x)], axis=-1)
            x = jnp.concatenate([x * jnp.roll(x, i, axis=-1) for i in range(1, N_ROLL + 1)], axis=-1)
            return x / x.sum(-1, keepdims=True)
        slen, bsz, _ = h.shape
        qkvb = jnp.einsum('lbd,ed->lbe', h, W_qkvb).reshape(slen, bsz, N_HEAD, 3 * D_HEAD + 1)
        q, k, v, beta = jnp.split(qkvb, [D_HEAD, 2 * D_HEAD, 3 * D_HEAD], axis=-1)
        beta = jax.nn.sigmoid(beta)
        q = _dpfp(q)
        k = _dpfp(k)
        denom_acc = jnp.cumsum(k, axis=0)
        denominator = jnp.einsum('lbhd,lbhd->lbh', denom_acc, q)[..., None]
        dk = 2 * N_ROLL * D_HEAD
        W0 = jnp.zeros((bsz, N_HEAD, dk, D_HEAD), dtype=h.dtype)

        def step(W, inp):
            qt, kt, vt, bt = inp
            v_old = jnp.einsum('bhd,bhde->bhe', kt, W)
            delta = bt * (vt - v_old)
            W = W + jnp.einsum('bhd,bhe->bhde', kt, delta)
            out = jnp.einsum('bhd,bhde->bhe', qt, W)
            return (W, out)
        _, out = jax.lax.scan(step, W0, (q, k, v, beta))
        out = SCALE * out / (denominator + EPS)
        out = out.reshape(slen, bsz, N_HEAD * D_HEAD)
        attn_out = jnp.einsum('lbe,de->lbd', out, W_o)
        x = h + attn_out
        mu = x.mean(-1, keepdims=True)
        var = x.var(-1, keepdims=True)
        return (x - mu) * jax.lax.rsqrt(var + EPS) * ln_g + ln_b

    def _L1_ffn_ref(x, router_w, router_b, Wi, Wh, b, Wo, bo):
        import jax, jax.numpy as jnp
        import numpy as np
        S, B, I, O, H, E, K = (128, 32, 128, 128, 128, 8, 2)

        def _expert(x_seq, Wi, Wh, b, Wo, bo):
            Bsz = x_seq.shape[1]
            Hd = Wh.shape[0]

            def step(carry, xt):
                h, c = carry
                gates = xt @ Wi + h @ Wh + b
                i_, f_, g_, o_ = jnp.split(gates, 4, axis=-1)
                c = jax.nn.sigmoid(f_) * c + jax.nn.sigmoid(i_) * jnp.tanh(g_)
                h = jax.nn.sigmoid(o_) * jnp.tanh(c)
                return ((h, c), h @ Wo + bo)
            init = (jnp.zeros((Bsz, Hd), x_seq.dtype), jnp.zeros((Bsz, Hd), x_seq.dtype))
            _, ys = jax.lax.scan(step, init, x_seq)
            return ys
        S_, B_, I_ = x.shape
        N = S_ * B_
        flat_x = x.reshape(N, I_)
        logits = flat_x @ router_w + router_b
        top_vals, top_idx = jax.lax.top_k(logits, K)
        rw = jax.nn.softmax(top_vals, axis=1)
        mask = (top_idx.T[:, None, :] == jnp.arange(E)[None, :, None]).astype(x.dtype)
        expert_x = (mask[..., None] * flat_x[None, None]).reshape(K, E, S_, B_, I_)
        run_e = jax.vmap(_expert, in_axes=(0, 0, 0, 0, 0, 0))
        run_ke = jax.vmap(run_e, in_axes=(0, None, None, None, None, None))
        out = run_ke(expert_x, Wi, Wh, b, Wo, bo)
        out = out.reshape(K, E, N, -1)
        y = jnp.einsum('ken,nk,keno->no', mask, rw, out)
        return y.reshape(S_, B_, -1)

    def _L2_attn_ref(x, Wvqkn_w, Wvqkn_b, out_w, out_b):
        import jax, jax.numpy as jnp
        import numpy as np
        D_MODEL = 128
        D_QK = 128
        H = 8
        HEAD_DIM = D_QK // H
        V_DIM = D_MODEL // H
        PROJ_OUT = D_MODEL + 2 * D_QK + H
        B, S, _ = x.shape
        vqkn = jnp.einsum('bsd,od->bso', x, Wvqkn_w) + Wvqkn_b
        v = vqkn[..., :D_MODEL]
        qk = vqkn[..., D_MODEL:D_MODEL + 2 * D_QK]
        n = vqkn[..., D_MODEL + 2 * D_QK:]
        qk = qk.reshape(B, S, 2, H, HEAD_DIM)
        v = v.reshape(B, S, H, V_DIM)
        q, k = (qk[:, :, 0], qk[:, :, 1])
        kv = jnp.einsum('bshd,bsht->bshdt', k, v)
        kv = jnp.cumsum(kv, axis=1)
        out = jnp.einsum('bshd,bshdt->bsht', q, kv)
        gate = jnp.exp(-jnp.exp(n))
        ctx = gate[..., None] * out
        ctx = ctx.reshape(B, S, D_MODEL)
        return jnp.einsum('bsd,od->bso', ctx, out_w) + out_b

    def _L2_ffn_ref(x, W):
        import jax, jax.numpy as jnp
        import numpy as np
        BINS = jnp.array([-1.5, -1.0, -0.5, 0.0, 0.5, 1.0, 1.5], dtype=jnp.float32)
        N_BINS = BINS.shape[0] + 1
        INDEX = 0
        y = x[..., INDEX]
        mem = jnp.sum(y[..., None] > BINS, axis=-1)
        B, T, D = x.shape
        xf = x.reshape(B * T, D)
        memf = mem.reshape(B * T)
        out = jnp.zeros((B * T, W.shape[-1]), dtype=x.dtype)
        for k in range(N_BINS):
            sel = (memf == k)[:, None].astype(x.dtype)
            out = out + sel * (xf @ W[k])
        return out.reshape(B, T, W.shape[-1])

    def _L3_attn_ref(x, W_q, W_k, W_v, W_o):
        import jax, jax.numpy as jnp
        import numpy as np
        import math
        S = x.shape[-2]
        d_key = W_k.shape[-1]
        Q = jnp.einsum('hjk,blj->bhlk', W_q, x)
        K = jnp.einsum('hjk,blj->bhlk', W_k, x)
        V = jnp.einsum('hjk,blj->bhlk', W_v, x)
        mask = jnp.triu(jnp.ones((S, S), dtype=bool), k=1)
        scores = jnp.einsum('bhik,bhjk->bhij', Q, K)
        scores = jnp.where(mask, -jnp.inf, scores)
        weights = jax.nn.softmax(scores / math.sqrt(d_key), axis=-1)
        weights = jnp.where(mask, 0.0, weights)
        values = jnp.einsum('bhij,bhjv->bhiv', weights, V)
        return jnp.einsum('hvk,bhlv->blk', W_o, values)

    def _L3_ffn_ref(x, gamma_norm, Wq_w, Wq_b, Wkv_w, Wkv_b, aw1_w, aw1_b, aw2_w, aw2_b, wz_g1, wz_w1, wz_b1, wz_g2, wz_w2, wz_b2):
        import jax, jax.numpy as jnp
        import numpy as np
        G, H, DQK, DV, L, D_IN = (8, 16, 128, 128, 100, 128)
        FF = D_IN
        LSW = 1.0

        def _l2norm(x, d):
            n = jnp.maximum(jnp.linalg.norm(x, axis=-1, keepdims=True), 1e-12)
            return x / n * d ** 0.5
        b, s, d = x.shape
        xn = _l2norm(x, d) * gamma_norm
        q = (xn @ Wq_w + Wq_b).reshape(b, s, G, H, DQK)
        kv = xn @ Wkv_w + Wkv_b
        k, v = (kv[..., :G * DQK], kv[..., G * DQK:])
        w = jax.nn.silu(k @ aw1_w + aw1_b) @ aw2_w + aw2_b
        w1 = jax.nn.softmax(w, axis=-1) / s
        w2 = jax.nn.softmax(w, axis=-2) / L * LSW
        w = (w1 + w2) / (1.0 + LSW)
        kc = jnp.einsum('bsd,bsl->bld', k, w).reshape(b, L, G, DQK)
        vc = jnp.einsum('bsd,bsl->bld', v, w).reshape(b, L, G, DV)
        qk = jnp.einsum('bsghd,blgd->bghsl', q, kc) * (1.0 / DQK ** 0.5)
        att = jax.nn.softmax(qk, axis=-1)
        z = jnp.einsum('bghsl,blgd->bsghd', att, vc).reshape(b, s, G * H * DV)
        zn = _l2norm(z, G * H * DV) * wz_g1
        h1 = jax.nn.silu(zn @ wz_w1 + wz_b1)
        h1n = _l2norm(h1, 2 * FF) * wz_g2
        out = jax.nn.silu(h1n @ wz_w2 + wz_b2)
        return out
    h = _L0_tok_ref(x, L0_tok_weight, L0_tok_bias, L0_tok_mask)
    h = h + _L0_attn_ref(_layernorm(h, axis=-1), L0_attn_ln_gamma, L0_attn_ln_beta, L0_attn_W_in, L0_attn_conv_w, L0_attn_A, L0_attn_D, L0_attn_dt_W1, L0_attn_dt_b1, L0_attn_dt_W2, L0_attn_dt_b2, L0_attn_W_out)
    h = h + _L0_ffn_ref(_layernorm(h, axis=-1), L0_ffn_switch_w, L0_ffn_switch_b, L0_ffn_expert_w, L0_ffn_expert_b)
    h = h + _L1_attn_ref(_layernorm(h, axis=-1), L1_attn_W_qkvb, L1_attn_W_o, L1_attn_ln_g, L1_attn_ln_b)
    h = h + _L1_ffn_ref(_layernorm(h, axis=-1), L1_ffn_router_w, L1_ffn_router_b, L1_ffn_Wi, L1_ffn_Wh, L1_ffn_b, L1_ffn_Wo, L1_ffn_bo)
    h = h + _L2_attn_ref(_layernorm(h, axis=-1), L2_attn_Wvqkn_w, L2_attn_Wvqkn_b, L2_attn_out_w, L2_attn_out_b)
    h = h + _L2_ffn_ref(_layernorm(h, axis=-1), L2_ffn_W)
    h = h + _L3_attn_ref(_layernorm(h, axis=-1), L3_attn_W_q, L3_attn_W_k, L3_attn_W_v, L3_attn_W_o)
    h = h + _L3_ffn_ref(_layernorm(h, axis=-1), L3_ffn_gamma_norm, L3_ffn_Wq_w, L3_ffn_Wq_b, L3_ffn_Wkv_w, L3_ffn_Wkv_b, L3_ffn_aw1_w, L3_ffn_aw1_b, L3_ffn_aw2_w, L3_ffn_aw2_b, L3_ffn_wz_g1, L3_ffn_wz_w1, L3_ffn_wz_b1, L3_ffn_wz_g2, L3_ffn_wz_w2, L3_ffn_wz_b2)
    return h

_drawn_inputs = setup_inputs


def setup_inputs(seed=0):
    import zlib

    import numpy as np

    out = dict(_drawn_inputs(seed))
    spreads = {'L0_tok_bias': (0.0, 0.1),
     'L0_attn_ln_gamma': (1.0, 0.6),
     'L0_attn_ln_beta': (0.0, 0.8),
     'L0_attn_D': (1.0, 0.6),
     'L0_attn_dt_b1': (0.0, 0.8),
     'L0_attn_dt_b2': (0.0, 0.8),
     'L0_ffn_switch_b': (0.0, 0.1),
     'L0_ffn_expert_b': (0.0, 1.621),
     'L1_attn_ln_g': (1.0, 0.2),
     'L1_attn_ln_b': (0.0, 0.1),
     'L1_ffn_router_b': (0.0, 0.1),
     'L1_ffn_b': (0.0, 0.8),
     'L1_ffn_bo': (0.0, 0.274),
     'L3_ffn_gamma_norm': (1.0, 0.6),
     'L3_ffn_Wq_b': (0.0, 2.0),
     'L3_ffn_Wkv_b': (0.0, 0.1),
     'L3_ffn_aw1_b': (0.0, 2.0),
     'L3_ffn_aw2_b': (0.0, 2.0),
     'L3_ffn_wz_g1': (1.0, 0.6),
     'L3_ffn_wz_b1': (0.0, 2.0),
     'L3_ffn_wz_g2': (1.0, 0.6),
     'L3_ffn_wz_b2': (0.0, 0.346)}
    factors = {'L0_attn_W_in': 8.0,
     'L0_attn_conv_w': 8.0,
     'L0_attn_A': 8.0,
     'L0_attn_dt_W1': 8.0,
     'L0_attn_dt_W2': 8.0,
     'L0_attn_W_out': 8.0,
     'L1_attn_W_qkvb': 8.0,
     'L1_attn_W_o': 8.0,
     'L1_ffn_Wi': 5.341,
     'L1_ffn_Wh': 8.0,
     'L1_ffn_Wo': 4.699,
     'L3_attn_W_q': 8.0,
     'L3_attn_W_k': 8.0,
     'L3_attn_W_v': 8.0,
     'L3_attn_W_o': 8.0,
     'L3_ffn_Wq_w': 200.0,
     'L3_ffn_aw1_w': 200.0,
     'L3_ffn_aw2_w': 200.0,
     'L0_ffn_expert_w': 4.373,
     'L2_attn_out_b': 3.539}
    for name, (base, spread) in spreads.items():
        noise = np.random.default_rng([zlib.crc32(name.encode()), seed]).standard_normal(out[name].shape)
        drawn = base * np.exp(spread * noise) if base else spread * noise
        out[name] = jnp.asarray(drawn.astype(out[name].dtype))
    for name, factor in factors.items():
        out[name] = (out[name] * factor).astype(out[name].dtype)
    return out
```

```python
from contextlib import ExitStack

import concourse.bass as bass
from concourse import mybir

F32 = mybir.dt.float32
ALU = mybir.AluOpType
ACT = mybir.ActivationFunctionType
AX = mybir.AxisListType.X

P = 128
ROWS, PLACES = 64, 16
TOKENS = ROWS * PLACES
TILES = TOKENS // P
HALF = 512
LN_EPS = 1e-5

LAYERS = [0, 1, 2, 3, 4, 5, 6, 7, 8]


class Chip:

    def __init__(self, nc, stack):
        self.nc, self.stack = nc, stack
        self.sems, self.used = ExitStack(), []

    def sem(self, name):
        h = self.sems.enter_context(self.nc.semaphore(name))
        self.used.append(h)
        return h

    def renew(self):
        nc, used = self.nc, self.used
        if used:
            with nc.Block() as block:
                @block.gpsimd
                def _(pool):
                    for h in used:
                        nc.gpsimd.sem_clear(h)
            self.sems.close()
        self.sems, self.used = ExitStack(), []

    def sb(self, name, shape, stack=None, dt=F32):
        return (stack or self.stack).enter_context(self.nc.sbuf_tensor(name, shape, dt))

    def ps(self, name, shape, stack):
        return stack.enter_context(self.nc.psum_tensor(name, shape, F32))


class Order:

    def __init__(self, eng, sem):
        self.eng, self.sem, self.n = eng, sem, 0

    def after(self, ins):
        self.n += 1
        ins.then_inc(self.sem, 1)
        self.eng.wait_ge(self.sem, self.n)


def start(c, hin):
    nc = c.nc
    s_zero, s_ident, s_hin = c.sem("zeroed"), c.sem("identity"), c.sem("stream_loaded")
    with nc.Block() as block:
        @block.gpsimd
        def _(pool):
            nc.gpsimd.memset(c.ident[:, :], 0.0).then_inc(s_zero, 1)
            nc.gpsimd.memset(c.half_neg[:, :], -0.5).then_inc(s_zero, 1)
            pool.wait_ge(s_zero, 2)
            nc.gpsimd.affine_select(out=c.ident[:, :], in_=c.ident[:, :], compare_op=ALU.not_equal, fill=1.0,
                                    base=0, pattern=[[-1, P]], channel_multiplier=1).then_inc(s_ident, 1)
            pool.wait_ge(s_ident, 1)

        if hin is not None:
            @block.sync
            def _(sp):
                sp.dma_start(c.H[:, :, :], hin.rearrange("(i q) e d -> (q e) i d", q=8)
                             if False else hin.rearrange("b e d -> (b e) d").rearrange("(i p) d -> p i d", p=P)
                             ).then_inc(s_hin, 16)
                sp.wait_ge(s_hin, 16)


def finish(c, out):
    nc = c.nc
    s_out = c.sem("stored")
    with nc.Block() as block:
        @block.sync
        def _(sp):
            sp.dma_start(out.rearrange("b e d -> (b e) d").rearrange("(i p) d -> p i d", p=P), c.H[:, :, :]
                         ).then_inc(s_out, 16)
            sp.wait_ge(s_out, 16)



class Norm:

    def __init__(self, c, name, stack):
        self.c = c
        self.stats = c.sb(name + "_stats", [P, TILES, 6], stack)
        self.mean_var = c.sb(name + "_mean_var", [P, TILES, 2], stack)
        self.var_eps = c.sb(name + "_var_eps", [P, TILES], stack)
        self.rstd = c.sb(name + "_rstd", [P, TILES], stack)
        self.s_var, self.s_rstd = c.sem(name + "_var"), c.sem(name + "_rstd")

    def statistics(self, o, src):
        v = self.c.nc.vector
        for i in range(TILES):
            last = v.bn_stats(self.stats[:, i, :], src[:, i, :])
        o.after(last)
        for i in range(TILES):
            last = v.bn_aggr(self.mean_var[:, i, :], self.stats[:, i, :])
        o.after(last)
        v.tensor_scalar_add(self.var_eps[:, :], self.mean_var[:, :, 1], LN_EPS).then_inc(self.s_var, 1)

    def power(self, pool):
        pool.wait_ge(self.s_var, 1)
        self.c.nc.gpsimd.tensor_tensor(self.rstd[:, :], self.var_eps[:, :], self.c.half_neg[:, 0:TILES],
                                       ALU.pow).then_inc(self.s_rstd, 1)

    def apply(self, dve, dst, src):
        dve.wait_ge(self.s_rstd, 1)
        for i in range(TILES):
            last = self.c.nc.vector.tensor_scalar(dst[:, i, :], src[:, i, :], self.mean_var[:, i, 0:1],
                                                  self.rstd[:, i:i + 1], ALU.subtract, ALU.mult)
        return last


def transpose_tokens(c, dst, src):
    for i in range(TILES):
        last = c.nc.tensor.transpose(dst[:, i * P:(i + 1) * P], src[:, i, :], c.ident[:, :])
    return last



GENES, GENE_P, SLOTS = 5000, 125, 5
GENE_TILES = GENES // GENE_P
EMB = PLACES * P
EMB_ROW = EMB + P + ROWS


def token_embedding(c, A):
    nc = c.nc
    s_load = [c.sem(f"genes_loaded{s}") for s in range(SLOTS)]
    s_masked, s_used, s_bias, s_sum = c.sem("masked"), c.sem("genes_used"), c.sem("emb_bias"), c.sem("emb_sum")
    s_swap, s_swapped, s_back = c.sem("emb_swap"), c.sem("emb_swapped"), c.sem("emb_back")
    with ExitStack() as st:
        ring = c.sb("gene_ring", [GENE_P, SLOTS, EMB_ROW], st)
        bias = c.sb("emb_bias_rows", [ROWS, EMB], st)
        summed = c.sb("emb_rows", [ROWS, PLACES, P], st)
        feat = c.sb("emb_feat", [P, ROWS, PLACES], st)
        acc = c.ps("emb_acc", [ROWS, EMB], st)
        swap = c.ps("emb_swap_ps", [P, PLACES, ROWS], st)
        back = c.ps("emb_back_ps", [P, TILES, P], st)
        genes = A["genes"]

        block = st.enter_context(nc.Block())

        @block.sync
        def _(sp):
            for s in range(SLOTS):
                sp.dma_start(ring[:, s, :], genes[s, :, :]).then_inc(s_load[s], 16)
            sp.dma_start(bias[:, :], A["tok_bias"].broadcast_to([ROWS, EMB])).then_inc(s_bias, 16)
            with sp.Fori(1, GENE_TILES // SLOTS) as it:
                for s in range(SLOTS):
                    sp.wait_ge(s_used, it * SLOTS + (s + 1 - SLOTS))
                    sp.dma_start(ring[:, s, :], genes[bass.ds(it * SLOTS + s, 1), :, :].rearrange("a p n -> (a p) n")
                                 ).then_inc(s_load[s], 16)

        @block.vector
        def _(dve):
            with dve.Fori(0, GENE_TILES // SLOTS) as it:
                for s in range(SLOTS):
                    dve.wait_ge(s_load[s], it * 16 + 16)
                    w = ring[:, s, 0:EMB].rearrange("p (e f) -> p e f", f=P)
                    m = ring[:, s, EMB:EMB + P].unsqueeze(1).broadcast_to([GENE_P, PLACES, P])
                    nc.vector.tensor_tensor(w, w, m, ALU.mult).then_inc(s_masked, 1)
            dve.wait_ge(s_bias, 16)
            dve.wait_ge(s_used, GENE_TILES)
            nc.vector.tensor_tensor(summed[:, :, :].rearrange("p e f -> p (e f)"), acc[:, :], bias[:, :],
                                    ALU.add).then_inc(s_sum, 1)
            dve.wait_ge(s_swap, 1)
            nc.vector.tensor_copy(feat[:, :, :].rearrange("p b e -> p e b"), swap[:, :, :]).then_inc(s_swapped, 1)
            dve.wait_ge(s_back, 1)
            nc.vector.tensor_copy(c.H[:, :, :], back[:, :, :])

        @block.tensor
        def _(pe):
            def tile(s, first, last):
                for q in range(EMB // HALF):
                    ins = nc.tensor.matmul(acc[:, q * HALF:(q + 1) * HALF], ring[:, s, EMB + P:EMB_ROW],
                                           ring[:, s, q * HALF:(q + 1) * HALF], start=first, stop=last)
                ins.then_inc(s_used, 1)

            for s in range(SLOTS):
                pe.wait_ge(s_masked, s + 1)
                tile(s, s == 0, False)
            with pe.Fori(1, GENE_TILES // SLOTS - 1) as it:
                for s in range(SLOTS):
                    pe.wait_ge(s_masked, it * SLOTS + (s + 1))
                    tile(s, False, False)
            for s in range(SLOTS):
                pe.wait_ge(s_masked, GENE_TILES - SLOTS + s + 1)
                tile(s, False, s == SLOTS - 1)
            pe.wait_ge(s_sum, 1)
            for e in range(PLACES):
                ins = nc.tensor.transpose(swap[:, e, :], summed[:, e, :], c.ident[0:ROWS, 0:ROWS])
            ins.then_inc(s_swap, 1)
            pe.wait_ge(s_swapped, 1)
            for i in range(TILES):
                ins = nc.tensor.transpose(back[:, i, :],
                                          feat[:, :, :].rearrange("p b e -> p (b e)")[:, i * P:(i + 1) * P],
                                          c.ident[:, :])
            ins.then_inc(s_back, 1)



def columns(widths):
    at, n = {}, 0
    for name, w in widths:
        at[name] = (n, n + w)
        n += w
    return at, n


def pack(np, widths, parts):
    at, n = columns(widths)
    out = np.zeros((P, n), np.float32)
    for name, w in widths:
        a = parts[name].reshape(-1, w)
        out[:a.shape[0], at[name][0]:at[name][1]] = a
    return out



HID, STATES, RANK = 256, 16, 64
HH = HID // P
PAD = PLACES + 2
SEG = PLACES + 1
RING = 4
MAMBA = [("w_in", HID), ("w1", HH * RANK), ("w2", HID), ("w_out", HH * P), ("conv", HH * 3), ("a", HH * STATES),
         ("d", HH), ("b2", HH), ("gamma", 1), ("beta", 1), ("b1", 1)]


def halves(np, a):
    return np.transpose(a.reshape(HH, P, -1), (1, 0, 2)).reshape(P, -1)


def lay_mamba(np, x, A):
    g = {k[len("L0_attn_"):]: v for k, v in x.items() if k.startswith("L0_attn_")}
    A["mamba"] = pack(np, MAMBA, {
        "w_in": g["W_in"].T, "w1": halves(np, g["dt_W1"].T), "w2": g["dt_W2"].T, "w_out": halves(np, g["W_out"].T),
        "conv": halves(np, g["conv_w"].reshape(HID, 3)), "a": halves(np, g["A"]), "d": halves(np, g["D"]),
        "b2": halves(np, g["dt_b2"]), "gamma": g["ln_gamma"], "beta": g["ln_beta"], "b1": g["dt_b1"]})


def mamba(c, A):
    nc = c.nc
    at, n_cols = columns(MAMBA)
    with ExitStack() as st:
        W = c.sb("mamba_w", [P, n_cols], st)

        def w(name, rows=P):
            return W[0:rows, at[name][0]:at[name][1]]

        n1, n2 = Norm(c, "mamba_n1", st), Norm(c, "mamba_n2", st)
        X1 = c.sb("mamba_x1", [P, TILES, P], st)
        X2 = c.sb("mamba_x2", [P, TILES, P], st)
        xnT = c.sb("mamba_xnT", [P, TOKENS], st)
        hpad = c.sb("mamba_hpad", [P, HH, ROWS, PAD], st)
        conv = c.sb("mamba_conv", [P, HH, ROWS, PLACES], st)
        hs = c.sb("mamba_hs", [P, HH, TOKENS], st)
        d1 = c.sb("mamba_d1", [RANK, TOKENS], st)
        z = c.sb("mamba_z", [P, HH, TOKENS], st)
        mag = c.sb("mamba_mag", [P, HH, TOKENS], st)
        dt = c.sb("mamba_dt", [P, HH, TOKENS], st)
        U = c.sb("mamba_u", [P, HH, ROWS, PAD], st)
        dU = c.sb("mamba_du", [P, HH, ROWS, SEG], st)
        Y = c.sb("mamba_y", [P, HH, ROWS, PLACES], st)
        dA = c.sb("mamba_dA", [P, RING, ROWS, SEG], st)
        S = c.sb("mamba_state", [P, RING, ROWS, SEG], st)
        WA = c.sb("mamba_wa", [P, HH, STATES, P], st)
        ea = c.sb("mamba_ea", [P, HH * STATES], st)
        aneg = c.sb("mamba_aneg", [P, HH * STATES], st)
        tiny = c.sb("mamba_tiny", [P, HH * STATES], st)
        safe = c.sb("mamba_safe", [P, HH * STATES], st)
        inv = c.sb("mamba_inv", [P, HH * STATES], st)
        coef = c.sb("mamba_coef", [P, HH, STATES], st)
        csum = c.sb("mamba_csum", [P, HH], st)
        outT = c.sb("mamba_outT", [P, TOKENS], st)
        psA = c.ps("mamba_psA", [P, TOKENS], st)
        psH = c.ps("mamba_psH", [P, HH, TOKENS], st)
        psO = c.ps("mamba_psO", [P, TOKENS], st)

        names = ("w", "x2", "xt", "xn", "h", "hcopy", "conv", "hs", "d1ps", "d1", "d2ps", "mag", "log", "dt", "expa",
                 "coef", "wa", "pads", "dA", "state", "used", "y", "outps", "outT", "back", "x1", "cord", "aord")
        s = {k: c.sem("mamba_" + k) for k in names}
        block = st.enter_context(nc.Block())

        @block.sync
        def _(sp):
            sp.dma_start(W[:, :], A["mamba"]).then_inc(s["w"], 16)

        @block.gpsimd
        def _(pool):
            nc.gpsimd.memset(hpad[:, :, :, :], 0.0).then_inc(s["pads"], 1)
            nc.gpsimd.memset(U[:, :, :, :], 0.0).then_inc(s["pads"], 1)
            nc.gpsimd.memset(dA[:, :, :, :], 0.0).then_inc(s["pads"], 1)
            n1.power(pool)
            n2.power(pool)
            pool.wait_ge(s["coef"], 1)
            for h in range(HH):
                wo = w("w_out")[:, h * P:(h + 1) * P].unsqueeze(1).broadcast_to([P, STATES, P])
                k = coef[:, h, :].unsqueeze(2).broadcast_to([P, STATES, P])
                nc.gpsimd.tensor_tensor(WA[:, h, :, :], wo, k, ALU.mult).then_inc(s["wa"], 1)

        @block.scalar
        def _(act):
            act.wait_ge(s["w"], 16)
            nc.scalar.activation(ea[:, :], w("a"), ACT.Exp).then_inc(s["expa"], 1)
            act.wait_ge(s["xt"], 1)
            nc.scalar.activation(xnT[:, :], psA[:, :], ACT.Identity, bias=w("beta"), scale=w("gamma")
                                 ).then_inc(s["xn"], 1)
            act.wait_ge(s["h"], 1)
            act.wait_ge(s["pads"], 1)
            for h in range(HH):
                nc.scalar.activation(hpad[:, h, :, 1:1 + PLACES],
                                     psH[:, h, :].rearrange("p (b l) -> p b l", l=PLACES), ACT.Copy
                                     ).then_inc(s["hcopy"], 1)
            for h in range(HH):
                act.wait_ge(s["conv"], h + 1)
                nc.scalar.activation(hs[:, h, :], conv[:, h, :, :].rearrange("p b l -> p (b l)"), ACT.Silu
                                     ).then_inc(s["hs"], 1)
            act.wait_ge(s["d1ps"], 1)
            nc.scalar.activation(d1[:, :], psA[0:RANK, :], ACT.Relu, bias=w("b1", RANK)).then_inc(s["d1"], 1)
            act.wait_ge(s["mag"], 1)
            nc.scalar.activation(mag[:, :, :], mag[:, :, :], ACT.Exp, scale=-1.0).then_inc(s["aord"], 1)
            act.wait_ge(s["aord"], 1)
            nc.scalar.activation(mag[:, :, :], mag[:, :, :], ACT.Ln, bias=1.0).then_inc(s["log"], 1)
            act.wait_ge(s["dt"], 1)
            act.wait_ge(s["pads"], 3)
            for k in range(HH * STATES):
                h, n = k % HH, k // HH
                if k >= RING:
                    act.wait_ge(s["state"], k - RING + 1)
                nc.scalar.activation(dA[:, k % RING, :, 1:SEG], dt[:, h, :].rearrange("p (b l) -> p b l", l=PLACES),
                                     ACT.Exp, scale=aneg[:, h * STATES + n:h * STATES + n + 1]).then_inc(s["dA"], 1)
            act.wait_ge(s["outps"], 1)
            nc.scalar.activation(outT[:, :], psO[:, :], ACT.Copy).then_inc(s["outT"], 1)

        @block.vector
        def _(dve):
            v = nc.vector
            o = Order(dve, s["cord"])
            n1.statistics(o, c.H)
            o.after(n1.apply(dve, X1, c.H))
            n2.statistics(o, X1)
            n2.apply(dve, X2, X1).then_inc(s["x2"], 1)
            o.after(v.tensor_tensor(c.H[:, :, :], c.H[:, :, :], X1[:, :, :], ALU.add))
            dve.wait_ge(s["expa"], 1)
            v.tensor_scalar_mul(aneg[:, :], ea[:, :], -1.0)
            o.after(v.tensor_scalar(tiny[:, :], ea[:, :], 1e-5, None, ALU.is_lt))
            o.after(v.tensor_scalar(safe[:, :], tiny[:, :], -1.0, 1.0, ALU.mult, ALU.add))
            o.after(v.tensor_tensor(safe[:, :], safe[:, :], aneg[:, :], ALU.mult))
            o.after(v.tensor_tensor(safe[:, :], safe[:, :], tiny[:, :], ALU.add))
            o.after(v.reciprocal(inv[:, :], safe[:, :]))
            o.after(v.tensor_tensor(coef[:, :, :].rearrange("p h n -> p (h n)"), inv[:, :], w("a"), ALU.mult))
            v.tensor_reduce(csum[:, :], coef[:, :, :], AX, ALU.add).then_inc(s["coef"], 1)
            for h in range(HH):
                k = w("conv")[:, 3 * h:3 * h + 3]
                dve.wait_ge(s["hcopy"], h + 1)
                o.after(v.tensor_scalar(conv[:, h, :, :], hpad[:, h, :, 1:1 + PLACES], k[:, 1:2], None, ALU.mult))
                o.after(v.scalar_tensor_tensor(conv[:, h, :, :], hpad[:, h, :, 0:PLACES], k[:, 0:1],
                                               conv[:, h, :, :], ALU.mult, ALU.add))
                v.scalar_tensor_tensor(conv[:, h, :, :], hpad[:, h, :, 2:PAD], k[:, 2:3], conv[:, h, :, :],
                                       ALU.mult, ALU.add).then_inc(s["conv"], 1)
            dve.wait_ge(s["d2ps"], 1)
            for h in range(HH):
                last = v.tensor_scalar(z[:, h, :], psH[:, h, :], w("b2")[:, h:h + 1], None, ALU.add)
            o.after(last)
            v.scalar_tensor_tensor(mag[:, :, :], z[:, :, :], -1.0, z[:, :, :], ALU.mult, ALU.max).then_inc(s["mag"], 1)
            dve.wait_ge(s["log"], 1)
            o.after(v.scalar_tensor_tensor(dt[:, :, :], z[:, :, :], 0.0, mag[:, :, :], ALU.max, ALU.add))
            dve.wait_ge(s["pads"], 2)
            for h in range(HH):
                last = v.tensor_tensor(U[:, h, :, 1:1 + PLACES], dt[:, h, :].rearrange("p (b l) -> p b l", l=PLACES),
                                       hs[:, h, :].rearrange("p (b l) -> p b l", l=PLACES), ALU.mult)
            last.then_inc(s["dt"], 1)
            dve.wait_ge(s["dt"], 1)
            for h in range(HH):
                last = v.tensor_tensor(dU[:, h, :, :], U[:, h, :, 1:PAD], U[:, h, :, 0:SEG], ALU.subtract)
            o.after(last)
            for k in range(HH * STATES):
                h = k % HH
                dve.wait_ge(s["dA"], k + 1)
                if k >= RING:
                    dve.wait_ge(s["used"], k - RING + 1)
                v.tensor_tensor_scan(S[:, k % RING, :, :].rearrange("p b l -> p (b l)"),
                                     dA[:, k % RING, :, :].rearrange("p b l -> p (b l)"),
                                     dU[:, h, :, :].rearrange("p b l -> p (b l)"), 0.0, ALU.mult, ALU.add
                                     ).then_inc(s["state"], 1)
            for h in range(HH):
                last = v.tensor_scalar(Y[:, h, :, :], U[:, h, :, 2:PAD], csum[:, h:h + 1], -1.0, ALU.mult, ALU.mult)
            o.after(last)
            for h in range(HH):
                last = v.scalar_tensor_tensor(Y[:, h, :, :].rearrange("p b l -> p (b l)"), hs[:, h, :],
                                              w("d")[:, h:h + 1], Y[:, h, :, :].rearrange("p b l -> p (b l)"),
                                              ALU.mult, ALU.add)
            last.then_inc(s["y"], 1)
            dve.wait_ge(s["back"], 1)
            v.tensor_tensor(c.H[:, :, :], c.H[:, :, :], psA[:, :].rearrange("p (i d) -> p i d", d=P), ALU.add)

        @block.tensor
        def _(pe):
            mm = nc.tensor.matmul
            pe.wait_ge(s["x2"], 1)
            transpose_tokens(c, psA, X2).then_inc(s["xt"], 1)
            pe.wait_ge(s["xn"], 1)
            for h in range(HH):
                for q in range(2):
                    ins = mm(psH[:, h, q * HALF:(q + 1) * HALF], w("w_in")[:, h * P:(h + 1) * P],
                             xnT[:, q * HALF:(q + 1) * HALF], start=True, stop=True)
            ins.then_inc(s["h"], 1)
            pe.wait_ge(s["hs"], HH)
            for q in range(2):
                for h in range(HH):
                    ins = mm(psA[0:RANK, q * HALF:(q + 1) * HALF], w("w1")[:, h * RANK:(h + 1) * RANK],
                             hs[:, h, q * HALF:(q + 1) * HALF], start=h == 0, stop=h == HH - 1)
            ins.then_inc(s["d1ps"], 1)
            pe.wait_ge(s["d1"], 1)
            for h in range(HH):
                for q in range(2):
                    ins = mm(psH[:, h, q * HALF:(q + 1) * HALF], w("w2", RANK)[:, h * P:(h + 1) * P],
                             d1[:, q * HALF:(q + 1) * HALF], start=True, stop=True)
            ins.then_inc(s["d2ps"], 1)
            pe.wait_ge(s["wa"], HH)
            for k in range(HH * STATES):
                h, n = k % HH, k // HH
                pe.wait_ge(s["state"], k + 1)
                for q in range(2):
                    ins = mm(psO[:, q * HALF:(q + 1) * HALF], WA[:, h, n, :],
                             S[:, k % RING, q * ROWS // 2:(q + 1) * ROWS // 2, 1:SEG], start=k == 0, stop=False)
                ins.then_inc(s["used"], 1)
            pe.wait_ge(s["y"], 1)
            for h in range(HH):
                for q in range(2):
                    ins = mm(psO[:, q * HALF:(q + 1) * HALF], w("w_out")[:, h * P:(h + 1) * P],
                             Y[:, h, q * ROWS // 2:(q + 1) * ROWS // 2, :], start=False, stop=h == HH - 1)
            ins.then_inc(s["outps"], 1)
            pe.wait_ge(s["outT"], 1)
            for i in range(TILES):
                ins = nc.tensor.transpose(psA[:, i * P:(i + 1) * P], outT[:, i * P:(i + 1) * P], c.ident[:, :])
            ins.then_inc(s["back"], 1)



SWITCH, BINS = 16, (-1.5, -1.0, -0.5, 0.0, 0.5, 1.0, 1.5)
CAPACITY = int(1.2 * TOKENS / SWITCH)
PER_BANK = HALF // P
BANKS = 4
SWITCH_COLS = [("w", SWITCH * P), ("gate", SWITCH), ("gate_b", SWITCH), ("rank", SWITCH), ("tri", P), ("ones", P),
               ("bias", P)]
BINNED_COLS = [("w", (len(BINS) + 1) * P)]


def lay_switch(np, x, A):
    A["switch"] = pack(np, SWITCH_COLS, {
        "w": np.transpose(x["L0_ffn_expert_w"], (2, 0, 1)).reshape(P, SWITCH * P), "gate": x["L0_ffn_switch_w"].T,
        "gate_b": np.tile(x["L0_ffn_switch_b"], (P, 1)),
        "rank": np.tile(np.arange(SWITCH, 0, -1, dtype=np.float32), (P, 1)),
        "tri": np.triu(np.ones((P, P), np.float32)), "ones": np.ones((P, P), np.float32),
        "bias": x["L0_ffn_expert_b"]})


def lay_binned(np, x, A):
    A["binned"] = np.transpose(x["L2_ffn_W"], (1, 0, 2)).reshape(P, (len(BINS) + 1) * P)


def picked_experts(c, name, W_dram, cols, n_exp, routed):
    nc = c.nc
    at, n_cols = columns(cols)
    groups = n_exp // PER_BANK
    with ExitStack() as st:
        W = c.sb(name + "_w", [P, n_cols], st)

        def w(part, rows=P):
            return W[0:rows, at[part][0]:at[part][1]]

        norm = Norm(c, name + "_n", st)
        X = c.sb(name + "_x", [P, TILES, P], st)
        XT = c.sb(name + "_xT", [P, TOKENS], st)
        K = c.sb(name + "_k", [P, TILES, n_exp], st)
        psT = c.ps(name + "_psT", [P, TOKENS], st)
        psE = c.ps(name + "_psE", [P, BANKS, HALF], st)
        psL = c.ps(name + "_psL", [P, TILES, n_exp], st)
        psC = c.ps(name + "_psC", [P, TILES, n_exp], st)
        s = {k: c.sem(f"{name}_{k}") for k in ("w", "x", "xps", "xT", "out", "taken", "ord", "ones")}
        if routed:
            s.update({k: c.sem(f"{name}_{k}") for k in ("logit", "shift", "exp", "hot", "count", "k", "kps", "kT",
                                                        "bias")})
            L, E, hot, score, before = (c.sb(f"{name}_{k}", [P, TILES, n_exp], st)
                                        for k in ("l", "e", "hot", "score", "before"))
            top, total, prob, rest = (c.sb(f"{name}_{k}", [P, TILES], st) for k in ("top", "total", "prob", "rest"))
            KT = c.sb(name + "_kT", [n_exp, TOKENS], st)
        else:
            above = c.sb(name + "_above", [P, TILES, n_exp + 1], st)
        block = st.enter_context(nc.Block())

        @block.sync
        def _(sp):
            sp.dma_start(W[:, :], W_dram).then_inc(s["w"], 16)

        @block.gpsimd
        def _(pool):
            if not routed:
                nc.gpsimd.memset(above[:, :, 0:1], 1.0).then_inc(s["ones"], 1)
                nc.gpsimd.memset(above[:, :, n_exp:n_exp + 1], 0.0).then_inc(s["ones"], 1)
            norm.power(pool)

        @block.scalar
        def _(act):
            act.wait_ge(s["xps"], 1)
            nc.scalar.activation(XT[:, :], psT[:, :], ACT.Copy).then_inc(s["xT"], 1)
            if routed:
                act.wait_ge(s["shift"], 1)
                nc.scalar.activation(E[:, :, :], L[:, :, :], ACT.Exp).then_inc(s["exp"], 1)
                act.wait_ge(s["kps"], 1)
                nc.scalar.activation(KT[:, :], psT[0:n_exp, :], ACT.Copy).then_inc(s["kT"], 1)

        @block.vector
        def _(dve):
            v = nc.vector
            o = Order(dve, s["ord"])
            norm.statistics(o, c.H)
            norm.apply(dve, X, c.H).then_inc(s["x"], 1)
            if routed:
                dve.wait_ge(s["w"], 16)
                dve.wait_ge(s["logit"], 1)
                o.after(v.tensor_tensor(L[:, :, :], psL[:, :, :],
                                        w("gate_b").unsqueeze(1).broadcast_to([P, TILES, n_exp]), ALU.add))
                o.after(v.tensor_reduce(top[:, :], L[:, :, :], AX, ALU.max))
                tops = top[:, :].unsqueeze(2).broadcast_to([P, TILES, n_exp])
                v.tensor_tensor(score[:, :, :], L[:, :, :], tops, ALU.is_equal)
                o.after(v.tensor_tensor(L[:, :, :], L[:, :, :], tops, ALU.subtract))
                v.tensor_tensor(score[:, :, :], score[:, :, :],
                                w("rank").unsqueeze(1).broadcast_to([P, TILES, n_exp]), ALU.mult
                                ).then_inc(s["shift"], 1)
                dve.wait_ge(s["shift"], 1)
                o.after(v.tensor_reduce(top[:, :], score[:, :, :], AX, ALU.max))
                o.after(v.tensor_tensor(hot[:, :, :], score[:, :, :],
                                        top[:, :].unsqueeze(2).broadcast_to([P, TILES, n_exp]), ALU.is_equal))
                o.after(v.memset(before[:, 0, :], 0.0))
                for i in range(1, TILES):
                    ins = v.tensor_tensor(before[:, i, :], before[:, i - 1, :], hot[:, i - 1, :], ALU.add)
                    if i < TILES - 1:
                        o.after(ins)
                ins.then_inc(s["hot"], 1)
                dve.wait_ge(s["exp"], 1)
                o.after(v.tensor_reduce(total[:, :], E[:, :, :], AX, ALU.add))
                o.after(v.reciprocal(prob[:, :], total[:, :]))
                dve.wait_ge(s["count"], 1)
                o.after(v.scalar_tensor_tensor(K[:, :, :].rearrange("p i e -> p (i e)"),
                                               psC[:, :, :].rearrange("p i e -> p (i e)"), float(CAPACITY),
                                               hot[:, :, :].rearrange("p i e -> p (i e)"), ALU.is_le, ALU.mult))
                o.after(v.tensor_tensor(K[:, :, :], K[:, :, :],
                                        prob[:, :].unsqueeze(2).broadcast_to([P, TILES, n_exp]), ALU.mult))
                v.tensor_reduce(total[:, :], K[:, :, :], AX, ALU.add).then_inc(s["k"], 1)
                dve.wait_ge(s["k"], 1)
                o.after(v.tensor_tensor(rest[:, :], prob[:, :], total[:, :], ALU.subtract))
                for i in range(TILES):
                    ins = v.scalar_tensor_tensor(c.H[:, i, :], X[:, i, :], rest[:, i:i + 1], c.H[:, i, :],
                                                 ALU.mult, ALU.add)
                o.after(ins)
            else:
                dve.wait_ge(s["x"], 1)
                dve.wait_ge(s["ones"], 2)
                for n, edge in enumerate(BINS):
                    ins = v.tensor_scalar(above[:, :, n + 1:n + 2], X[:, :, 0:1], edge, None, ALU.is_gt)
                o.after(ins)
                o.after(v.tensor_tensor(K[:, :, :], above[:, :, 0:n_exp], above[:, :, 1:n_exp + 1], ALU.subtract))
            for m in range(groups * TILES):
                g, i = m // TILES, m % TILES
                dve.wait_ge(s["out"], m + 1)
                for j in range(PER_BANK):
                    e = g * PER_BANK + j
                    ins = v.scalar_tensor_tensor(c.H[:, i, :], psE[:, m % BANKS, j * P:(j + 1) * P],
                                                 K[:, i, e:e + 1], c.H[:, i, :], ALU.mult, ALU.add)
                    if j < PER_BANK - 1:
                        o.after(ins)
                ins.then_inc(s["taken"], 1)
            if routed:
                dve.wait_ge(s["bias"], 1)
                dve.wait_ge(s["taken"], groups * TILES)
                v.tensor_tensor(c.H[:, :, :], c.H[:, :, :], psT[:, :].rearrange("p (i d) -> p i d", d=P), ALU.add)

        @block.tensor
        def _(pe):
            mm = nc.tensor.matmul

            def expert_bank(m):
                g, i = m // TILES, m % TILES
                if m >= BANKS:
                    pe.wait_ge(s["taken"], m - BANKS + 1)
                mm(psE[:, m % BANKS, :], XT[:, i * P:(i + 1) * P],
                   W[:, at["w"][0] + g * HALF:at["w"][0] + (g + 1) * HALF], start=True, stop=True
                   ).then_inc(s["out"], 1)

            pe.wait_ge(s["x"], 1)
            transpose_tokens(c, psT, X).then_inc(s["xps"], 1)
            pe.wait_ge(s["w"], 16)
            pe.wait_ge(s["xT"], 1)
            if routed:
                for i in range(TILES):
                    ins = mm(psL[:, i, :], XT[:, i * P:(i + 1) * P], w("gate"), start=True, stop=True)
                ins.then_inc(s["logit"], 1)
            for m in range(BANKS):
                expert_bank(m)
            if routed:
                pe.wait_ge(s["hot"], 1)
                mm(psC[:, :, :], w("tri"), hot[:, :, :], start=True, stop=False)
                mm(psC[:, :, :], w("ones"), before[:, :, :], start=False, stop=True).then_inc(s["count"], 1)
                pe.wait_ge(s["k"], 1)
                for i in range(TILES):
                    ins = nc.tensor.transpose(psT[0:n_exp, i * P:(i + 1) * P], K[:, i, :], c.ident[:, :])
                ins.then_inc(s["kps"], 1)
                pe.wait_ge(s["kT"], 1)
                for i in range(TILES):
                    ins = mm(psT[:, i * P:(i + 1) * P], KT[:, i * P:(i + 1) * P], w("bias", n_exp),
                             start=True, stop=True)
                ins.then_inc(s["bias"], 1)
            for m in range(BANKS, groups * TILES):
                expert_bank(m)


def switch_experts(c, A):
    picked_experts(c, "switch", A["switch"], SWITCH_COLS, SWITCH, True)


def binned_experts(c, A):
    picked_experts(c, "binned", A["binned"], BINNED_COLS, len(BINS) + 1, False)



LHEADS, LDIM = 8, 16
HEAD_SLOT = 32
LGROUPS = LHEADS * HEAD_SLOT // P
PER_GROUP = LHEADS // LGROUPS
VN = P + LHEADS
LINEAR_COLS = [("qk", 2 * LGROUPS * P), ("qk_b", 2 * LGROUPS), ("vn", VN), ("vn_b", VN), ("mask", P), ("out", P),
               ("out_b", P)]


def row_mask(np):
    t = np.arange(P)
    return ((t[:, None] // PLACES == t[None, :] // PLACES) & (t[:, None] <= t[None, :])).astype(np.float32)


def lay_linear(np, x, A):
    w, b = x["L2_attn_Wvqkn_w"], x["L2_attn_Wvqkn_b"]
    qk_w = np.zeros((2, LHEADS, HEAD_SLOT, P), np.float32)
    qk_b = np.zeros((2, LHEADS, HEAD_SLOT), np.float32)
    qk_w[:, :, :LDIM] = w[P:3 * P].reshape(2, LHEADS, LDIM, P)
    qk_b[:, :, :LDIM] = b[P:3 * P].reshape(2, LHEADS, LDIM)
    vn = np.concatenate([w[:P], w[3 * P:]])
    A["linear"] = pack(np, LINEAR_COLS, {
        "qk": qk_w.reshape(2 * LGROUPS * P, P).T, "qk_b": qk_b.reshape(2 * LGROUPS, P).T, "vn": vn.T,
        "vn_b": np.tile(np.concatenate([b[:P], b[3 * P:]]), (P, 1)), "mask": row_mask(np),
        "out": x["L2_attn_out_w"].T, "out_b": np.tile(x["L2_attn_out_b"], (P, 1))})


def linear_attention(c, A):
    nc = c.nc
    at, n_cols = columns(LINEAR_COLS)
    with ExitStack() as st:
        W = c.sb("linear_w", [P, n_cols], st)

        def w(part):
            return W[:, at[part][0]:at[part][1]]

        norm = Norm(c, "linear_n", st)
        X = c.sb("linear_x", [P, TILES, P], st)
        XT = c.sb("linear_xT", [P, TOKENS], st)
        QK = c.sb("linear_qk", [P, 2 * LGROUPS, TOKENS], st)
        V = c.sb("linear_v", [P, TILES, VN], st)
        gate = c.sb("linear_gate", [P, TILES, LHEADS], st)
        S = c.sb("linear_s", [P, 2, PER_GROUP, LGROUPS, P], st)
        ctx = c.sb("linear_ctx", [P, TILES, P], st)
        ctxT = c.sb("linear_ctxT", [P, TOKENS], st)
        psT = c.ps("linear_psT", [P, TOKENS], st)
        psS = c.ps("linear_psS", [P, PER_GROUP, HALF], st)
        psV = c.ps("linear_psV", [P, 2, HALF], st)
        names = ("w", "x", "xps", "xT", "qkps", "qk", "vps", "v", "gate", "sps", "s", "ops", "ctx", "cps", "cT",
                 "out", "ord", "aord")
        s = {k: c.sem("linear_" + k) for k in names}
        block = st.enter_context(nc.Block())

        @block.sync
        def _(sp):
            sp.dma_start(W[:, :], A["linear"]).then_inc(s["w"], 16)

        @block.gpsimd
        def _(pool):
            norm.power(pool)

        @block.scalar
        def _(act):
            act.wait_ge(s["xps"], 1)
            nc.scalar.activation(XT[:, :], psT[:, :], ACT.Copy).then_inc(s["xT"], 1)
            for u in range(2 * LGROUPS):
                act.wait_ge(s["qkps"], u + 1)
                nc.scalar.activation(QK[:, u, :], psS[:, 2 * (u % 2):2 * (u % 2) + 2, :], ACT.Identity,
                                     bias=w("qk_b")[:, u:u + 1]).then_inc(s["qk"], 1)
            act.wait_ge(s["v"], TILES)
            nc.scalar.activation(gate[:, :, :], V[:, :, P:VN], ACT.Exp).then_inc(s["aord"], 1)
            act.wait_ge(s["aord"], 1)
            nc.scalar.activation(gate[:, :, :], gate[:, :, :], ACT.Exp, scale=-1.0).then_inc(s["gate"], 1)
            act.wait_ge(s["cps"], 1)
            nc.scalar.activation(ctxT[:, :], psT[:, :], ACT.Copy).then_inc(s["cT"], 1)

        @block.vector
        def _(dve):
            v = nc.vector
            o = Order(dve, s["ord"])
            norm.statistics(o, c.H)
            norm.apply(dve, X, c.H).then_inc(s["x"], 1)
            dve.wait_ge(s["w"], 16)
            for i in range(TILES):
                dve.wait_ge(s["vps"], i + 1)
                v.tensor_tensor(V[:, i, :], psV[:, i % 2, 0:VN], w("vn_b"), ALU.add).then_inc(s["v"], 1)
            dve.wait_ge(s["gate"], 1)
            mask = w("mask").unsqueeze(1).unsqueeze(1).broadcast_to([P, PER_GROUP, LGROUPS, P])

            def context(i):
                dve.wait_ge(s["ops"], i + 1)
                v.tensor_tensor(ctx[:, i, :].rearrange("p (h d) -> p h d", d=LDIM),
                                psV[:, i % 2, 0:P].rearrange("p (h d) -> p h d", d=LDIM),
                                gate[:, i, :].unsqueeze(2).broadcast_to([P, LHEADS, LDIM]), ALU.mult
                                ).then_inc(s["ctx"], 1)

            for i in range(TILES):
                dve.wait_ge(s["sps"], i + 1)
                v.tensor_tensor(S[:, i % 2, :, :, :],
                                psS[:, :, 0:LGROUPS * P].rearrange("p j (a t) -> p j a t", t=P), mask, ALU.mult
                                ).then_inc(s["s"], 1)
                if i >= 1:
                    context(i - 1)
            context(TILES - 1)
            o.after(v.tensor_tensor(c.H[:, :, :], c.H[:, :, :],
                                    w("out_b").unsqueeze(1).broadcast_to([P, TILES, P]), ALU.add))
            dve.wait_ge(s["out"], 1)
            v.tensor_tensor(c.H[:, :, :], c.H[:, :, :],
                            psS[:, 0:2, :].rearrange("p a (i d) -> p (a i) d", d=P), ALU.add)

        @block.tensor
        def _(pe):
            mm = nc.tensor.matmul
            pe.wait_ge(s["x"], 1)
            transpose_tokens(c, psT, X).then_inc(s["xps"], 1)
            pe.wait_ge(s["w"], 16)
            pe.wait_ge(s["xT"], 1)
            for u in range(2 * LGROUPS):
                if u >= 2:
                    pe.wait_ge(s["qk"], u - 1)
                for q in range(2):
                    ins = mm(psS[:, 2 * (u % 2) + q, :], w("qk")[:, u * P:(u + 1) * P],
                             XT[:, q * HALF:(q + 1) * HALF], start=True, stop=True)
                ins.then_inc(s["qkps"], 1)
            for i in range(TILES):
                if i >= 2:
                    pe.wait_ge(s["v"], i - 1)
                mm(psV[:, i % 2, 0:VN], XT[:, i * P:(i + 1) * P], w("vn"), start=True, stop=True
                   ).then_inc(s["vps"], 1)
            pe.wait_ge(s["qk"], 2 * LGROUPS)

            def values(i):
                if i < 2:
                    pe.wait_ge(s["v"], TILES)
                else:
                    pe.wait_ge(s["ctx"], i - 1)
                pe.wait_ge(s["s"], i + 1)
                for h in range(LHEADS):
                    ins = mm(psV[:, i % 2, h * LDIM:(h + 1) * LDIM], S[:, i % 2, h % PER_GROUP, h // PER_GROUP, :],
                             V[:, i, h * LDIM:(h + 1) * LDIM], start=True, stop=True)
                ins.then_inc(s["ops"], 1)

            for i in range(TILES):
                if i >= 1:
                    pe.wait_ge(s["s"], i)
                for a in range(LGROUPS):
                    for j in range(PER_GROUP):
                        rows = slice(j * HEAD_SLOT, (j + 1) * HEAD_SLOT)
                        ins = mm(psS[:, j, a * P:(a + 1) * P], QK[rows, LGROUPS + a, i * P:(i + 1) * P],
                                 QK[rows, a, i * P:(i + 1) * P], start=True, stop=True)
                ins.then_inc(s["sps"], 1)
                if i >= 1:
                    values(i - 1)
            values(TILES - 1)
            pe.wait_ge(s["ctx"], TILES)
            transpose_tokens(c, psT, ctx).then_inc(s["cps"], 1)
            pe.wait_ge(s["cT"], 1)
            for i in range(TILES):
                ins = mm(psS[:, i // 4, (i % 4) * P:(i % 4 + 1) * P], ctxT[:, i * P:(i + 1) * P], w("out"),
                         start=True, stop=True)
            ins.then_inc(s["out"], 1)



CHEADS, CDIM = 8, 64
CPAIRS = CHEADS // 2
CAUSAL_COLS = [("q", CHEADS * CDIM), ("k", CHEADS * CDIM), ("v", CHEADS * CDIM), ("o", CPAIRS * P), ("mask", P)]
MASKED = -1e30


def lay_causal(np, x, A):
    def heads(a):
        return np.transpose(a, (1, 0, 2)).reshape(P, CHEADS * CDIM)
    A["causal"] = pack(np, CAUSAL_COLS, {
        "q": heads(x["L3_attn_W_q"]), "k": heads(x["L3_attn_W_k"]), "v": heads(x["L3_attn_W_v"]),
        "o": np.transpose(x["L3_attn_W_o"].reshape(CPAIRS, P, P), (1, 0, 2)).reshape(P, CPAIRS * P),
        "mask": np.where(row_mask(np).T > 0, 0, MASKED).astype(np.float32)})


def causal_attention(c, A):
    nc = c.nc
    at, n_cols = columns(CAUSAL_COLS)
    qk_units = 2 * CPAIRS * 2
    proj = qk_units + TILES
    with ExitStack() as st:
        W = c.sb("causal_w", [P, n_cols], st)

        def w(part):
            return W[:, at[part][0]:at[part][1]]

        norm = Norm(c, "causal_n", st)
        X = c.sb("causal_x", [P, TILES, P], st)
        XT = c.sb("causal_xT", [P, TOKENS], st)
        QK = c.sb("causal_qk", [P, 2, CPAIRS, TOKENS], st)
        V = c.sb("causal_v", [P, TILES, CHEADS * CDIM], st)
        L = c.sb("causal_l", [P, 2, CHEADS, P], st)
        pr = c.sb("causal_p", [P, 2, CHEADS, P], st)
        prT = c.sb("causal_pT", [P, 2, CHEADS, P], st)
        top = c.sb("causal_top", [P, 2, CHEADS], st)
        total = c.sb("causal_total", [P, 2, CHEADS], st)
        inv = c.sb("causal_inv", [P, 2, CHEADS], st)
        vals = c.sb("causal_vals", [P, 2, CPAIRS, P], st)
        psT = c.ps("causal_psT", [P, TOKENS], st)
        psS = c.ps("causal_psS", [P, 4, HALF], st)
        psO = c.ps("causal_psO", [P, CPAIRS, P], st)
        psF = c.ps("causal_psF", [P, HALF], st)
        names = ("w", "x", "xps", "xT", "pps", "pact", "pdve", "sps", "masked", "top", "exp", "inv", "norm", "tps",
                 "pT", "vps", "vals", "out", "added", "ord")
        s = {k: c.sem("causal_" + k) for k in names}
        block = st.enter_context(nc.Block())

        def projected(u):
            if u < qk_units:
                return QK[:, u // (2 * CPAIRS), u // 2 % CPAIRS, u % 2 * HALF:(u % 2 + 1) * HALF]
            return V[:, u - qk_units, :]

        @block.sync
        def _(sp):
            sp.dma_start(W[:, :], A["causal"]).then_inc(s["w"], 16)

        @block.gpsimd
        def _(pool):
            norm.power(pool)
            for i in range(TILES):
                pool.wait_ge(s["inv"], i + 1)
                nc.gpsimd.tensor_tensor(pr[:, i % 2, :, :], pr[:, i % 2, :, :],
                                        inv[:, i % 2, :].unsqueeze(2).broadcast_to([P, CHEADS, P]), ALU.mult
                                        ).then_inc(s["norm"], 1)

        @block.scalar
        def _(act):
            act.wait_ge(s["xps"], 1)
            nc.scalar.activation(XT[:, :], psT[:, :], ACT.Copy).then_inc(s["xT"], 1)
            for u in range(0, proj, 2):
                act.wait_ge(s["pps"], u + 1)
                nc.scalar.activation(projected(u), psS[:, u % 4, :], ACT.Copy).then_inc(s["pact"], 1)

            def transposed(i):
                act.wait_ge(s["tps"], i + 1)
                if i >= 2:
                    act.wait_ge(s["vps"], i - 1)
                nc.scalar.activation(prT[:, i % 2, :, :].rearrange("p h t -> p (h t)"), psT[:, :], ACT.Copy
                                     ).then_inc(s["pT"], 1)

            for i in range(TILES):
                act.wait_ge(s["top"], i + 1)
                if i >= 2:
                    act.wait_ge(s["tps"], i - 1)
                for h in range(CHEADS):
                    ins = nc.scalar.activation(pr[:, i % 2, h, :], L[:, i % 2, h, :], ACT.Exp,
                                               bias=top[:, i % 2, h:h + 1], accum_out=total[:, i % 2, h:h + 1])
                ins.then_inc(s["exp"], 1)
                if i >= 1:
                    transposed(i - 1)
            transposed(TILES - 1)

        @block.vector
        def _(dve):
            v = nc.vector
            o = Order(dve, s["ord"])
            norm.statistics(o, c.H)
            norm.apply(dve, X, c.H).then_inc(s["x"], 1)
            for u in range(1, proj, 2):
                dve.wait_ge(s["pps"], u + 1)
                v.tensor_copy(projected(u), psS[:, u % 4, :]).then_inc(s["pdve"], 1)
            dve.wait_ge(s["w"], 16)
            mask = w("mask").unsqueeze(1).broadcast_to([P, CHEADS, P])

            def close(i):
                dve.wait_ge(s["vps"], i + 1)
                v.tensor_copy(vals[:, i % 2, :, :], psO[:, :, :]).then_inc(s["vals"], 1)
                dve.wait_ge(s["out"], i + 1)
                v.tensor_tensor(c.H[:, i, :], c.H[:, i, :], psF[:, 0:P], ALU.add).then_inc(s["added"], 1)

            for i in range(TILES):
                dve.wait_ge(s["sps"], i + 1)
                if i >= 2:
                    dve.wait_ge(s["exp"], i - 1)
                v.scalar_tensor_tensor(L[:, i % 2, :, :],
                                       psS[:, 2 * (i % 2):2 * (i % 2) + 2, :].rearrange("p a (b t) -> p (a b) t", t=P),
                                       float(CDIM) ** -0.5, mask, ALU.mult, ALU.add).then_inc(s["masked"], 1)
                dve.wait_ge(s["masked"], i + 1)
                v.tensor_reduce(top[:, i % 2, :], L[:, i % 2, :, :], AX, ALU.max, negate=True).then_inc(s["top"], 1)
                dve.wait_ge(s["exp"], i + 1)
                v.reciprocal(inv[:, i % 2, :], total[:, i % 2, :]).then_inc(s["inv"], 1)
                if i >= 1:
                    close(i - 1)
            close(TILES - 1)

        @block.tensor
        def _(pe):
            mm = nc.tensor.matmul
            pe.wait_ge(s["x"], 1)
            transpose_tokens(c, psT, X).then_inc(s["xps"], 1)
            pe.wait_ge(s["w"], 16)
            pe.wait_ge(s["xT"], 1)

            def bank_free(u):
                prev = u - 4
                if prev >= 0:
                    pe.wait_ge(s["pact"] if prev % 2 == 0 else s["pdve"], prev // 2 + 1)

            for u in range(proj):
                bank_free(u)
                if u < qk_units:
                    part, pair, q = u // (2 * CPAIRS), u // 2 % CPAIRS, u % 2
                    ins = mm(psS[:, u % 4, :], w("qk"[part])[:, pair * P:(pair + 1) * P],
                             XT[:, q * HALF:(q + 1) * HALF], start=True, stop=True)
                else:
                    i = u - qk_units
                    ins = mm(psS[:, u % 4, :], XT[:, i * P:(i + 1) * P], w("v"), start=True, stop=True)
                ins.then_inc(s["pps"], 1)
            pe.wait_ge(s["pact"], proj // 2)
            pe.wait_ge(s["pdve"], proj // 2)

            def scores(i):
                if i >= 2:
                    pe.wait_ge(s["masked"], i - 1)
                for r in range(2):
                    rows = slice(r * CDIM, (r + 1) * CDIM)
                    for pair in range(CPAIRS):
                        ins = mm(psS[:, 2 * (i % 2) + r, pair * P:(pair + 1) * P],
                                 QK[rows, 0, pair, i * P:(i + 1) * P], QK[rows, 1, pair, i * P:(i + 1) * P],
                                 start=True, stop=True)
                ins.then_inc(s["sps"], 1)

            def values(i):
                pe.wait_ge(s["norm"], i + 1)
                if i >= 1:
                    pe.wait_ge(s["pT"], i)
                for h in range(CHEADS):
                    ins = nc.tensor.transpose(psT[:, h * P:(h + 1) * P], pr[:, i % 2, h, :], c.ident[:, :])
                ins.then_inc(s["tps"], 1)
                pe.wait_ge(s["pT"], i + 1)
                if i >= 1:
                    pe.wait_ge(s["vals"], i)
                for pair in range(CPAIRS):
                    for r in range(2):
                        ins = mm(psO[r * CDIM:(r + 1) * CDIM, pair, :],
                                 V[:, i, (2 * pair + r) * CDIM:(2 * pair + r + 1) * CDIM],
                                 prT[:, i % 2, r * CPAIRS + pair, :], start=True, stop=True)
                ins.then_inc(s["vps"], 1)
                pe.wait_ge(s["vals"], i + 1)
                if i >= 1:
                    pe.wait_ge(s["added"], i)
                for pair in range(CPAIRS):
                    ins = mm(psF[:, 0:P], vals[:, i % 2, pair, :], w("o")[:, pair * P:(pair + 1) * P],
                             start=pair == 0, stop=pair == CPAIRS - 1)
                ins.then_inc(s["out"], 1)

            scores(0)
            for i in range(TILES):
                if i + 1 < TILES:
                    scores(i + 1)
                values(i)



BF16 = mybir.dt.bfloat16
MOE, PICKS = 8, 2
STEPS = ROWS
STEP_TILE = P // PLACES
TRACKS = MOE * PICKS
SPLIT = 3
GROUPS = 2
MEMBERS = MOE // GROUPS
TRACK_ROWS = PICKS * PLACES
GATES = 4 * P
LSTM_COLS = [("wi", MOE * GATES), ("wh", MOE * GATES), ("wo", MOE * P), ("router", MOE), ("router_b", MOE),
             ("rank", MOE), ("place", PLACES), ("step", STEP_TILE), ("same", MEMBERS * PLACES), ("member", P),
             ("bo", P), ("b", GROUPS * GATES)]


def lay_lstm(np, x, A):
    g = {k[len("L1_ffn_"):]: v for k, v in x.items() if k.startswith("L1_ffn_")}

    def gates(a):
        parts = a.reshape(*a.shape[:-1], 4, P)
        return parts[..., [0, 1, 3, 2], :].reshape(a.shape)

    t = np.arange(P)
    row_member, row_place = t // TRACK_ROWS, t % PLACES
    col = np.arange(MEMBERS * PLACES)
    b = gates(g["b"]).reshape(GROUPS, MEMBERS, GATES)
    A["lstm"] = pack(np, LSTM_COLS, {
        "wi": np.transpose(gates(g["Wi"]), (1, 0, 2)).reshape(P, MOE * GATES),
        "wh": np.transpose(gates(g["Wh"]), (1, 0, 2)).reshape(P, MOE * GATES),
        "wo": np.transpose(g["Wo"], (1, 0, 2)).reshape(P, MOE * P), "router": g["router_w"],
        "router_b": np.tile(g["router_b"], (P, 1)),
        "rank": np.tile(np.arange(MOE, 0, -1, dtype=np.float32), (P, 1)),
        "place": (t[:, None] % PLACES == np.arange(PLACES)).astype(np.float32),
        "step": (t[:, None] // PLACES == np.arange(STEP_TILE)).astype(np.float32),
        "same": ((row_member[:, None] == col // PLACES) & (row_place[:, None] == col % PLACES)).astype(np.float32),
        "member": (np.arange(SPLIT * MEMBERS)[:, None] % MEMBERS == row_member).astype(np.float32),
        "bo": g["bo"], "b": np.transpose(b, (1, 0, 2)).reshape(MEMBERS, GROUPS * GATES)})


def lstm_experts(c, A):
    nc = c.nc
    at, n_cols = columns(LSTM_COLS)
    with ExitStack() as st:
        W = c.sb("lstm_w", [P, n_cols], st)

        def w(part, rows=P):
            return W[0:rows, at[part][0]:at[part][1]]

        def sb(name, shape, dt=F32):
            return c.sb("lstm_" + name, shape, st, dt)

        norm = Norm(c, "lstm_n", st)
        X, XT = sb("x", [P, TILES, P]), sb("xT", [P, TOKENS])
        L, hot, score = sb("l", [P, TILES, MOE]), sb("hot", [P, PICKS, TILES, MOE]), sb("score", [P, TILES, MOE])
        top, rank, ratio, wt = (sb(n, [P, PICKS, TILES]) for n in ("top", "rank_top", "ratio", "wt"))
        mask = sb("mask", [P, TILES, MOE, PICKS])
        coef = sb("coef", [P, TILES, MOE, PICKS])
        both = sb("both", [P, TILES, MOE])
        maskT = sb("maskT", [TRACKS, TOKENS], BF16)
        ident16 = sb("ident16", [TRACKS, TRACKS], BF16)
        maskB = sb("maskB", [P, TRACKS, TOKENS], BF16)
        bothT = sb("bothT", [MOE, TOKENS])
        spread = sb("spread", [P, TILES * TRACKS, PLACES])
        coefR = sb("coefR", [P, GROUPS, STEPS])
        parts = [sb(f"b_part{i}", [MEMBERS, GROUPS * GATES], BF16) for i in range(SPLIT)]
        left = sb("b_left", [MEMBERS, GROUPS * GATES])
        b3 = sb("b3", [SPLIT * MEMBERS, GROUPS * GATES], BF16)
        member = sb("member", [SPLIT * MEMBERS, P], BF16)
        xm = sb("xm", [P, 2, TRACKS, PLACES])
        pick = sb("pick", [P, 2, GROUPS, MEMBERS * PLACES])
        sig, cand = sb("sig", [P, GROUPS, 3 * P]), sb("cand", [P, GROUPS, P])
        ig, cell, cellt = sb("ig", [P, GROUPS, P]), sb("cell", [P, GROUPS, P]), sb("cellt", [P, GROUPS, P])
        hrow, hT = sb("hrow", [P, GROUPS, P]), sb("hT", [P, GROUPS, P])
        hsel = sb("hsel", [P, MOE, TOKENS])
        psG = c.ps("lstm_psG", [P, 4, HALF], st)
        psH = c.ps("lstm_psH", [P, GROUPS, HALF], st)
        psP = c.ps("lstm_psP", [P, 2, HALF], st)

        names = ("w", "x", "xps", "xT", "logit", "gap", "ratio", "mask", "coef", "mps", "mT", "bps", "bact", "bdve",
                 "bothps", "bothT", "spread", "rps", "coefR", "idb", "split", "moved", "memb", "zero", "xm", "pick",
                 "pickps", "hsel", "out", "ord")
        s = {k: c.sem("lstm_" + k) for k in names}
        gates_ps, gates_read, cell_in, cell_new, cell_tanh, h_row, h_T, h_ps = (
            [c.sem(f"lstm_{k}{g}") for g in range(GROUPS)]
            for k in ("gates", "gates_read", "cell_in", "cell_new", "cell_tanh", "h_row", "h_T", "h_ps"))
        block = st.enter_context(nc.Block())

        def steps(eng, body):
            body(0, 0, 0, False)
            body(1, 1, 1, False)
            with eng.Fori(1, STEPS // 2 - 1) as it:
                for j in range(2):
                    body(it * 2 + j, j, 2, False)
            body(STEPS - 2, 0, 2, False)
            body(STEPS - 1, 1, 2, True)

        @block.sync
        def _(sp):
            sp.dma_start(W[:, :], A["lstm"]).then_inc(s["w"], 16)
            sp.wait_ge(s["split"], SPLIT)
            for i in range(SPLIT):
                sp.dma_start(b3[i * MEMBERS:(i + 1) * MEMBERS, :], parts[i][:, :]).then_inc(s["moved"], 16)

        @block.gpsimd
        def _(pool):
            nc.gpsimd.memset(cell[:, :, :], 0.0).then_inc(s["zero"], 1)
            nc.gpsimd.memset(hT[:, :, :], 0.0).then_inc(s["zero"], 1)
            nc.gpsimd.tensor_copy(ident16[:, :], c.ident[0:TRACKS, 0:TRACKS]).then_inc(s["idb"], 1)
            norm.power(pool)
            pool.wait_ge(s["w"], 16)
            nc.gpsimd.tensor_copy(member[:, :], w("member", SPLIT * MEMBERS)).then_inc(s["memb"], 1)
            pool.wait_ge(s["xT"], 1)
            pool.wait_ge(s["bact"], TRACKS)
            pool.wait_ge(s["bdve"], TRACKS)
            pool.wait_ge(s["coefR"], 1)

            def masked_inputs(t, parity):
                nc.gpsimd.tensor_tensor(
                    xm[:, parity, :, :], maskB[:, :, bass.ds(t * PLACES, PLACES)],
                    XT[:, bass.ds(t * PLACES, PLACES)].unsqueeze(1).broadcast_to([P, TRACKS, PLACES]), ALU.mult
                    ).then_inc(s["xm"], 1)

            def body(t, parity, first, last):
                if first >= 1:
                    pool.wait_ge(gates_ps[1], t)
                if not last:
                    masked_inputs(t + 1, 1 - parity)
                nc.gpsimd.tensor_tensor(
                    pick[:, parity, :, :], w("same").unsqueeze(1).broadcast_to([P, GROUPS, MEMBERS * PLACES]),
                    coefR[:, :, bass.ds(t, 1)].broadcast_to([P, GROUPS, MEMBERS * PLACES]), ALU.mult
                    ).then_inc(s["pick"], 1)

            masked_inputs(0, 0)
            steps(pool, body)

        @block.scalar
        def _(act):
            a = nc.scalar.activation
            act.wait_ge(s["xps"], 1)
            a(XT[:, :], psG[:, 0:2, :].rearrange("p a n -> p (a n)"), ACT.Copy).then_inc(s["xT"], 1)
            act.wait_ge(s["gap"], 1)
            a(ratio[:, 0, :], ratio[:, 1, :], ACT.Exp).then_inc(s["ratio"], 1)
            for r in range(TRACKS):
                act.wait_ge(s["bps"], 2 * r + 1)
                a(maskB[:, r, 0:HALF], psG[:, 2 * r % 4, :], ACT.Copy).then_inc(s["bact"], 1)

            def picked(t, parity):
                act.wait_ge(s["pickps"], t + 1)
                a(hsel[:, :, bass.ds(t * PLACES, PLACES)],
                  psP[:, parity, 0:MOE * PLACES].rearrange("p (e b) -> p e b", b=PLACES), ACT.Copy
                  ).then_inc(s["hsel"], 1)

            def body(t, parity, first, last):
                for g in range(GROUPS):
                    act.wait_ge(gates_ps[g], t + 1)
                    a(sig[:, g, :], psG[:, 2 * parity + g, 0:3 * P], ACT.Sigmoid)
                    a(cand[:, g, :], psG[:, 2 * parity + g, 3 * P:GATES], ACT.Tanh).then_inc(gates_read[g], 1)
                for g in range(GROUPS):
                    act.wait_ge(cell_new[g], t + 1)
                    a(cellt[:, g, :], cell[:, g, :], ACT.Tanh).then_inc(cell_tanh[g], 1)
                if first >= 1:
                    picked(t - 1, 1 - parity)
                if last:
                    picked(t, parity)

            steps(act, body)

        @block.vector
        def _(dve):
            v = nc.vector
            o = Order(dve, s["ord"])
            norm.statistics(o, c.H)
            norm.apply(dve, X, c.H).then_inc(s["x"], 1)
            dve.wait_ge(s["w"], 16)
            o.after(v.tensor_copy(left[:, :], w("b", MEMBERS)))
            for i in range(SPLIT):
                v.tensor_copy(parts[i][:, :], left[:, :]).then_inc(s["split"], 1)
                dve.wait_ge(s["split"], i + 1)
                if i < SPLIT - 1:
                    o.after(v.tensor_tensor(left[:, :], left[:, :], parts[i][:, :], ALU.subtract))
            dve.wait_ge(s["logit"], 1)
            o.after(v.tensor_tensor(L[:, :, :], psH[:, 0, 0:TILES * MOE].rearrange("p (i e) -> p i e", e=MOE),
                                    w("router_b").unsqueeze(1).broadcast_to([P, TILES, MOE]), ALU.add))
            for k in range(PICKS):
                o.after(v.tensor_reduce(top[:, k, :], L[:, :, :], AX, ALU.max))
                o.after(v.tensor_tensor(score[:, :, :], L[:, :, :],
                                        top[:, k, :].unsqueeze(2).broadcast_to([P, TILES, MOE]), ALU.is_equal))
                o.after(v.tensor_tensor(score[:, :, :], score[:, :, :],
                                        w("rank").unsqueeze(1).broadcast_to([P, TILES, MOE]), ALU.mult))
                o.after(v.tensor_reduce(rank[:, k, :], score[:, :, :], AX, ALU.max))
                o.after(v.tensor_tensor(hot[:, k, :, :], score[:, :, :],
                                        rank[:, k, :].unsqueeze(2).broadcast_to([P, TILES, MOE]), ALU.is_equal))
                if k < PICKS - 1:
                    o.after(v.scalar_tensor_tensor(L[:, :, :], hot[:, k, :, :], MASKED, L[:, :, :],
                                                   ALU.mult, ALU.add))
            v.tensor_tensor(ratio[:, 1, :], top[:, 1, :], top[:, 0, :], ALU.subtract).then_inc(s["gap"], 1)
            for k in range(PICKS):
                ins = v.tensor_copy(mask[:, :, :, k], hot[:, k, :, :])
            ins.then_inc(s["mask"], 1)
            dve.wait_ge(s["ratio"], 1)
            o.after(v.tensor_scalar_add(wt[:, 1, :], ratio[:, 0, :], 1.0))
            o.after(v.reciprocal(wt[:, 0, :], wt[:, 1, :]))
            o.after(v.tensor_tensor(wt[:, 1, :], ratio[:, 0, :], wt[:, 0, :], ALU.mult))
            for k in range(PICKS):
                ins = v.tensor_tensor(coef[:, :, :, k], hot[:, k, :, :],
                                      wt[:, k, :].unsqueeze(2).broadcast_to([P, TILES, MOE]), ALU.mult)
            o.after(ins)
            v.tensor_tensor(both[:, :, :], coef[:, :, :, 0], coef[:, :, :, 1], ALU.add).then_inc(s["coef"], 1)
            v.tensor_tensor(spread[:, :, :],
                            coef[:, :, :, :].rearrange("p i e k -> p (i e k)").unsqueeze(2)
                            .broadcast_to([P, TILES * TRACKS, PLACES]),
                            w("place").unsqueeze(1).broadcast_to([P, TILES * TRACKS, PLACES]), ALU.mult
                            ).then_inc(s["spread"], 1)
            dve.wait_ge(s["mps"], 1)
            v.tensor_copy(maskT[:, :], psP[0:TRACKS, :, :].rearrange("p a n -> p (a n)")).then_inc(s["mT"], 1)
            dve.wait_ge(s["bothps"], 1)
            v.tensor_copy(bothT[:, :], psP[0:MOE, :, :].rearrange("p a n -> p (a n)")).then_inc(s["bothT"], 1)
            dve.wait_ge(s["rps"], 1)
            v.tensor_copy(coefR[:, :, :], psH[:, 0, 0:GROUPS * STEPS].rearrange("p (g t) -> p g t", t=STEPS)
                          ).then_inc(s["coefR"], 1)
            for r in range(TRACKS):
                dve.wait_ge(s["bps"], 2 * r + 2)
                v.tensor_copy(maskB[:, r, HALF:TOKENS], psG[:, (2 * r + 1) % 4, :]).then_inc(s["bdve"], 1)
            dve.wait_ge(s["zero"], 2)

            def body(t, parity, first, last):
                for g in range(GROUPS):
                    dve.wait_ge(gates_read[g], t + 1)
                    v.tensor_tensor(ig[:, g, :], sig[:, g, 0:P], cand[:, g, :], ALU.mult)
                    v.tensor_tensor(cell[:, g, :], sig[:, g, P:2 * P], cell[:, g, :], ALU.mult
                                    ).then_inc(cell_in[g], 1)
                    dve.wait_ge(cell_in[g], t + 1)
                    v.tensor_tensor(cell[:, g, :], cell[:, g, :], ig[:, g, :], ALU.add).then_inc(cell_new[g], 1)
                for g in range(GROUPS):
                    dve.wait_ge(cell_tanh[g], t + 1)
                    v.tensor_tensor(hrow[:, g, :], sig[:, g, 2 * P:3 * P], cellt[:, g, :], ALU.mult
                                    ).then_inc(h_row[g], 1)
                    dve.wait_ge(h_ps[g], t + 1)
                    v.tensor_copy(hT[:, g, :], psH[:, g, 0:P]).then_inc(h_T[g], 1)

            steps(dve, body)
            dve.wait_ge(s["out"], 1)
            v.tensor_tensor(c.H[:, :, :], c.H[:, :, :], psG[:, 0:2, :].rearrange("p a (i d) -> p (a i) d", d=P),
                            ALU.add)

        @block.tensor
        def _(pe):
            mm = nc.tensor.matmul
            tr = nc.tensor.transpose
            pe.wait_ge(s["x"], 1)
            for i in range(TILES):
                ins = tr(psG[:, i // 4, i % 4 * P:(i % 4 + 1) * P], X[:, i, :], c.ident[:, :])
            ins.then_inc(s["xps"], 1)
            pe.wait_ge(s["w"], 16)
            pe.wait_ge(s["xT"], 1)
            for i in range(TILES):
                ins = mm(psH[:, 0, i * MOE:(i + 1) * MOE], XT[:, i * P:(i + 1) * P], w("router"),
                         start=True, stop=True)
            ins.then_inc(s["logit"], 1)
            pe.wait_ge(s["mask"], 1)
            for i in range(TILES):
                ins = tr(psP[0:TRACKS, i // 4, i % 4 * P:(i % 4 + 1) * P],
                         mask[:, i, :, :].rearrange("p e k -> p (e k)"), c.ident[:, :])
            ins.then_inc(s["mps"], 1)
            pe.wait_ge(s["coef"], 1)
            pe.wait_ge(s["mT"], 1)
            for i in range(TILES):
                ins = tr(psP[0:MOE, i // 4, i % 4 * P:(i % 4 + 1) * P], both[:, i, :], c.ident[:, :])
            ins.then_inc(s["bothps"], 1)
            pe.wait_ge(s["spread"], 1)
            for i in range(TILES):
                for g in range(GROUPS):
                    first = (i * GROUPS + g) * TRACKS // GROUPS
                    ins = mm(psH[:, 0, g * STEPS + i * STEP_TILE:g * STEPS + (i + 1) * STEP_TILE],
                             spread[:, first:first + TRACKS // GROUPS, :].rearrange("p e b -> p (e b)"), w("step"),
                             start=True, stop=True)
            ins.then_inc(s["rps"], 1)
            pe.wait_ge(s["idb"], 1)
            for u in range(2 * TRACKS):
                r, q = u // 2, u % 2
                if u >= 4:
                    pe.wait_ge(s["bact"] if q == 0 else s["bdve"], r - 1)
                mm(psG[:, u % 4, :], ident16[:, r:r + 1].broadcast_to([TRACKS, P]),
                   maskT[:, q * HALF:(q + 1) * HALF], start=True, stop=True).then_inc(s["bps"], 1)
            pe.wait_ge(s["bact"], TRACKS)
            pe.wait_ge(s["bdve"], TRACKS)
            pe.wait_ge(s["moved"], 16 * SPLIT)
            pe.wait_ge(s["memb"], 1)
            pe.wait_ge(s["coefR"], 1)
            pe.wait_ge(s["bothT"], 1)
            pe.wait_ge(s["zero"], 2)

            def inputs(parity, g):
                bank = 2 * parity + g
                mm(psG[:, bank, :], member[:, :], b3[:, g * GATES:(g + 1) * GATES], start=True, stop=False)
                for j in range(MEMBERS):
                    e = g * MEMBERS + j
                    mm(psG[j * TRACK_ROWS:(j + 1) * TRACK_ROWS, bank, :],
                       xm[:, parity, e * PICKS:(e + 1) * PICKS, :].rearrange("p k b -> p (k b)"),
                       w("wi")[:, e * GATES:(e + 1) * GATES], start=False, stop=False)

            def body(t, parity, first, last):
                for g in range(GROUPS):
                    if first >= 1:
                        pe.wait_ge(h_T[g], t)
                    for j in range(MEMBERS):
                        e = g * MEMBERS + j
                        ins = mm(psG[j * TRACK_ROWS:(j + 1) * TRACK_ROWS, 2 * parity + g, :],
                                 hT[:, g, j * TRACK_ROWS:(j + 1) * TRACK_ROWS], w("wh")[:, e * GATES:(e + 1) * GATES],
                                 start=False, stop=True)
                    ins.then_inc(gates_ps[g], 1)
                for g in range(GROUPS):
                    if not last:
                        if g == 0:
                            pe.wait_ge(s["xm"], t + 2)
                        if first >= 1:
                            pe.wait_ge(gates_read[g], t)
                        inputs(1 - parity, g)
                    pe.wait_ge(h_row[g], t + 1)
                    tr(psH[:, g, 0:P], hrow[:, g, :], c.ident[:, :]).then_inc(h_ps[g], 1)
                pe.wait_ge(s["pick"], t + 1)
                if first >= 2:
                    pe.wait_ge(s["hsel"], t - 1)
                for g in range(GROUPS):
                    ins = mm(psP[:, parity, g * MEMBERS * PLACES:(g + 1) * MEMBERS * PLACES], hrow[:, g, :],
                             pick[:, parity, g, :], start=True, stop=True)
                ins.then_inc(s["pickps"], 1)

            pe.wait_ge(s["xm"], 1)
            for g in range(GROUPS):
                inputs(0, g)
            steps(pe, body)
            pe.wait_ge(s["hsel"], STEPS)
            pe.wait_ge(gates_read[0], STEPS)
            pe.wait_ge(gates_read[1], STEPS)
            for i in range(TILES):
                out = psG[:, i // 4, i % 4 * P:(i % 4 + 1) * P]
                for e in range(MOE):
                    mm(out, hsel[:, e, i * P:(i + 1) * P], w("wo")[:, e * P:(e + 1) * P], start=e == 0, stop=False)
                ins = mm(out, bothT[:, i * P:(i + 1) * P], w("bo", MOE), start=False, stop=True)
            ins.then_inc(s["out"], 1)



DHEADS, DDIM = 8, 64
ROLLS = 2
FEAT = 2 * DDIM
SEQ, BATCH = ROWS, PLACES
PAIRS = BATCH // 2
DSCALE, DEPS = DDIM ** -0.5, 1e-5
BLOCK16 = 16
YUNITS = 2 * 2 * (ROLLS + 1)
PRODUCTS = ["A0", "A1", "At1", "A2", "D2", "At2", "D3", "A3", "D4", "E0", "R1", "E1", "R2", "E2", "R3", "E3", "O"]
BY_SCALAR = ["A0", "A1", "At1", "A2", "At2", "A3", "E0", "E1", "E2"]
BY_VECTOR = [p for p in PRODUCTS if p not in BY_SCALAR]
DELTA_COLS = [("roll", 2 * DHEADS * (ROLLS + 1) * FEAT), ("sign", (ROLLS + 1) * FEAT), ("v", DHEADS * DDIM),
              ("beta", DHEADS), ("o", DHEADS * DDIM), ("g", P), ("b", P), ("eye", DDIM), ("near", DDIM),
              ("far", DDIM), ("upto", DDIM), ("one", 1)]


def lay_delta(np, x, A):
    w = x["L1_attn_W_qkvb"].reshape(DHEADS, 3 * DDIM + 1, P)
    kq = np.stack([w[:, DDIM:2 * DDIM], w[:, :DDIM]])
    both = np.concatenate([kq, kq], axis=2)
    rolled = np.stack([np.roll(both, i, axis=2) for i in range(ROLLS + 1)], axis=2)
    sign = np.repeat(np.array([1, -1], np.float32), DDIM)
    sign = np.concatenate([np.roll(sign, i) for i in range(ROLLS + 1)])
    s, t = np.arange(DDIM)[:, None], np.arange(DDIM)[None, :]
    near = (s < t) & (s // BLOCK16 == t // BLOCK16)
    far = (s < t) & (s // BLOCK16 != t // BLOCK16)

    def twice(a):
        return np.concatenate([a, a]).astype(np.float32)

    A["delta"] = pack(np, DELTA_COLS, {
        "roll": rolled.reshape(-1, P).T, "sign": np.tile(sign, (P, 1)),
        "v": w[:, 2 * DDIM:3 * DDIM].reshape(-1, P).T, "beta": w[:, 3 * DDIM].T,
        "o": np.transpose(x["L1_attn_W_o"].T.reshape(4, P, P), (1, 0, 2)).reshape(P, 4 * P),
        "g": np.tile(x["L1_attn_ln_g"], (P, 1)), "b": np.tile(x["L1_attn_ln_b"], (P, 1)),
        "eye": twice(s == t), "near": twice(near), "far": twice(far), "upto": twice(s <= t),
        "one": np.ones((P, 1), np.float32)})


def delta_attention(c, A):
    nc = c.nc
    at, n_cols = columns(DELTA_COLS)
    with ExitStack() as st:
        W = c.sb("delta_w", [P, n_cols], st)

        def w(part):
            return W[:, at[part][0]:at[part][1]]

        def sb(name, shape):
            return c.sb("delta_" + name, shape, st)

        n1, n2 = Norm(c, "delta_n1", st), Norm(c, "delta_n2", st)
        X = sb("x", [P, TILES, P])
        XT = sb("xT", [P, BATCH, SEQ])
        V = sb("v", [P, PAIRS, DHEADS, DDIM])
        beta = sb("beta", [P, PAIRS, DHEADS])
        Y0 = sb("y0", [P, 2, HALF])
        Z = sb("z", [P, 2, ROLLS, BATCH, 2, SEQ])
        sums, rk, nal, al = sb("sums", [P, 2, PAIRS]), sb("rk", [P, PAIRS]), sb("nal", [P, PAIRS]), sb("al", [P, PAIRS])
        ga = sb("ga", [P, PAIRS, SEQ])
        mats = {k: sb(k, [P, PAIRS, SEQ]) for k in
                ("At0", "far", "S", "A0", "A1", "At1", "A2", "At2", "A3", "D1", "D2", "D3", "D4", "rhs", "E", "R",
                 "dl")}
        den = sb("den", [P, PAIRS])
        O = sb("o", [P, PAIRS, DHEADS, DDIM])
        OT = sb("oT", [P, 4, TOKENS])
        AT = sb("aT", [P, TOKENS])
        psY = c.ps("delta_psY", [P, 2, HALF], st)
        psGS = c.ps("delta_psGS", [P, PAIRS, 2, SEQ], st)
        psM = [c.ps(f"delta_ps{k}", [P, 2, PAIRS, SEQ], st) for k in "AB"]

        names = ("w", "signed", "x", "xps", "xT", "vps", "v", "bps", "beta", "yps", "y0", "z", "sums", "gs", "gsread",
                 "lists", "product", "scalar", "vector", "ops", "oT", "aps", "aT", "back", "ord", "den")
        s = {k: c.sem("delta_" + k) for k in names}
        block = st.enter_context(nc.Block())
        lo_hi = [slice(0, DDIM), slice(DDIM, P)]

        def done(eng, h, name):
            if name in BY_SCALAR:
                eng.wait_ge(s["scalar"], h * len(BY_SCALAR) + BY_SCALAR.index(name) + 1)
            else:
                eng.wait_ge(s["vector"], h * len(BY_VECTOR) + BY_VECTOR.index(name) + 1)

        def ready(eng, h, name):
            eng.wait_ge(s["product"], h * len(PRODUCTS) + PRODUCTS.index(name) + 1)

        def bank(name):
            return psM[PRODUCTS.index(name) % 2]

        def unit(h, u):
            return h * YUNITS + u, u // (2 * (ROLLS + 1)), u // (ROLLS + 1) % 2, u % (ROLLS + 1)

        @block.sync
        def _(sp):
            sp.dma_start(W[:, :], A["delta"]).then_inc(s["w"], 16)

        @block.gpsimd
        def _(pool):
            n1.power(pool)
            pool.wait_ge(s["w"], 16)
            r = w("roll").rearrange("p (h f) -> p h f", f=(ROLLS + 1) * FEAT)
            nc.gpsimd.tensor_tensor(r, r, w("sign").unsqueeze(1).broadcast_to([P, 2 * DHEADS, (ROLLS + 1) * FEAT]),
                                    ALU.mult).then_inc(s["signed"], 1)
            n2.power(pool)

        @block.scalar
        def _(act):
            a = nc.scalar.activation
            act.wait_ge(s["xps"], 1)
            a(XT[:, :, :].rearrange("p b l -> p l b"),
              psGS[:, :, :, :].rearrange("p a k l -> p (a k l)").rearrange("p (l b) -> p l b", b=BATCH), ACT.Copy
              ).then_inc(s["xT"], 1)
            act.wait_ge(s["bps"], 1)
            a(beta[:, :, :], psGS[:, 0, :, :].rearrange("p a b -> p (a b)")[:, 0:PAIRS * DHEADS]
              .rearrange("p (j h) -> p j h", h=DHEADS), ACT.Sigmoid).then_inc(s["beta"], 1)

            def project(h, u):
                n, kq, half, roll = unit(h, u)
                if roll == 0:
                    act.wait_ge(s["yps"], n + 1)
                    m = n // (ROLLS + 1)
                    if m >= 2:
                        act.wait_ge(s["z"], (m - 1) * ROLLS)
                    a(Y0[:, m % 2, :], psY[:, n % 2, :], ACT.Relu).then_inc(s["y0"], 1)

            for u in range(YUNITS):
                project(0, u)
            for h in range(DHEADS):
                for k, name in enumerate(PRODUCTS):
                    if name in BY_SCALAR:
                        ready(act, h, name)
                        dst = mats["E" if name[0] == "E" else name]
                        for b, rows in enumerate(lo_hi):
                            ins = a(dst[rows, :, :], bank(name)[rows, b, :, :], ACT.Copy)
                        ins.then_inc(s["scalar"], 1)
                    if h + 1 < DHEADS and k < YUNITS:
                        project(h + 1, k)
            for j in range(PAIRS):
                act.wait_ge(s["ops"], j + 1)
                a(OT[:, :, j * P:(j + 1) * P], psM[0][:, j % 2, :, :].rearrange("p a b -> p (a b)")
                  .rearrange("p (k t) -> p k t", t=P), ACT.Copy).then_inc(s["oT"], 1)
            act.wait_ge(s["aps"], 1)
            a(AT[:, :].rearrange("p (l b) -> p b l", b=BATCH),
              psGS[:, :, :, :].rearrange("p a k l -> p (a k) l"), ACT.Copy).then_inc(s["aT"], 1)

        @block.vector
        def _(dve):
            v = nc.vector
            o = Order(dve, s["ord"])
            n1.statistics(o, c.H)
            n1.apply(dve, X, c.H).then_inc(s["x"], 1)
            for j in range(PAIRS):
                dve.wait_ge(s["vps"], j + 1)
                v.tensor_copy(V[:, j, :, :].rearrange("p h d -> p (h d)"), psY[:, j % 2, :]).then_inc(s["v"], 1)

            def project(h, u):
                n, kq, half, roll = unit(h, u)
                if roll > 0:
                    dve.wait_ge(s["yps"], n + 1)
                    m = n // (ROLLS + 1)
                    dve.wait_ge(s["y0"], m + 1)
                    v.scalar_tensor_tensor(Z[:, h % 2, roll - 1, half * BATCH // 2:(half + 1) * BATCH // 2, kq, :],
                                           psY[:, n % 2, :].rearrange("p (b l) -> p b l", l=SEQ), 0.0,
                                           Y0[:, m % 2, :].rearrange("p (b l) -> p b l", l=SEQ), ALU.max, ALU.mult
                                           ).then_inc(s["z"], 1)

            def wide(a):
                return a.unsqueeze(2).broadcast_to([P, PAIRS, SEQ])

            def each(part):
                return w(part).unsqueeze(1).broadcast_to([P, PAIRS, SEQ])

            for u in range(YUNITS):
                project(0, u)
            dve.wait_ge(s["beta"], 1)
            for h in range(DHEADS):
                dve.wait_ge(s["sums"], h + 1)
                o.after(v.tensor_copy(sums[:, :, :], psM[1][:, 0, 0:1, 0:2 * PAIRS].rearrange(
                    "p a (k j) -> p (a k) j", j=PAIRS)))
                o.after(v.reciprocal(rk[:, :], sums[:, 0, :]))
                o.after(v.tensor_tensor(al[:, :], rk[:, :], rk[:, :], ALU.mult))
                o.after(v.tensor_tensor(al[:, :], al[:, :], beta[:, :, h], ALU.mult))
                o.after(v.tensor_scalar_mul(nal[:, :], al[:, :], -1.0))
                dve.wait_ge(s["gs"], h + 1)
                o.after(v.tensor_tensor(ga[:, :, :], psGS[:, :, 0, :], wide(nal[:, :]), ALU.mult))
                v.tensor_tensor(mats["At0"][:, :, :], ga[:, :, :], each("near"), ALU.mult).then_inc(s["lists"], 1)
                dve.wait_ge(s["lists"], h + 1)
                v.tensor_tensor(mats["D1"][:, :, :], mats["At0"][:, :, :], each("eye"), ALU.add)
                v.tensor_tensor(mats["far"][:, :, :], ga[:, :, :], each("far"), ALU.mult)
                v.tensor_tensor(mats["rhs"][:, :, :], V[:, :, h, :], wide(sums[:, 0, :]), ALU.mult)
                v.tensor_tensor(mats["S"][:, :, :], psGS[:, :, 1, :], each("upto"), ALU.mult
                                ).then_inc(s["gsread"], 1)
                dve.wait_ge(s["gsread"], h + 1)
                for k, name in enumerate(PRODUCTS):
                    if name in BY_VECTOR:
                        ready(dve, h, name)
                        for b, rows in enumerate(lo_hi):
                            src = bank(name)[rows, b, :, :]
                            if name == "O":
                                continue
                            if name[0] == "D":
                                ins = v.tensor_tensor(mats[name][rows, :, :], src,
                                                      mats["D" + str(int(name[1]) - 1)][rows, :, :], ALU.add)
                            elif name[0] == "R":
                                ins = v.tensor_tensor(mats["R"][rows, :, :], src, mats["rhs"][rows, :, :], ALU.add)
                            else:
                                ins = v.tensor_tensor(mats["dl"][rows, :, :], src,
                                                      al[rows, :].unsqueeze(2).broadcast_to([DDIM, PAIRS, SEQ]),
                                                      ALU.mult)
                        if name == "O":
                            for b, rows in enumerate(lo_hi):
                                ins = v.scalar_tensor_tensor(den[rows, :], sums[rows, 1, :], DEPS,
                                                             psM[1][rows, b, 0, 0:PAIRS], ALU.mult, ALU.add)
                            o.after(ins)
                            o.after(v.reciprocal(den[:, :], den[:, :]))
                            o.after(v.tensor_scalar_mul(den[:, :], den[:, :], DSCALE))
                            for b, rows in enumerate(lo_hi):
                                ins = v.tensor_tensor(O[rows, :, h, :], bank(name)[rows, b, :, :],
                                                      den[rows, :].unsqueeze(2).broadcast_to([DDIM, PAIRS, SEQ]),
                                                      ALU.mult)
                        ins.then_inc(s["vector"], 1)
                    if h + 1 < DHEADS and k < YUNITS:
                        project(h + 1, k)
            dve.wait_ge(s["back"], 1)
            o.after(v.tensor_tensor(X[:, :, :], X[:, :, :], psY[:, :, :].rearrange("p a (i d) -> p (a i) d", d=P),
                                    ALU.add))
            n2.statistics(o, X)
            o.after(n2.apply(dve, X, X))
            o.after(v.tensor_tensor(X[:, :, :], X[:, :, :], w("g").unsqueeze(1).broadcast_to([P, TILES, P]),
                                    ALU.mult))
            o.after(v.tensor_tensor(X[:, :, :], X[:, :, :], w("b").unsqueeze(1).broadcast_to([P, TILES, P]),
                                    ALU.add))
            v.tensor_tensor(c.H[:, :, :], c.H[:, :, :], X[:, :, :], ALU.add)

        @block.tensor
        def _(pe):
            mm = nc.tensor.matmul
            tr = nc.tensor.transpose
            xt = XT[:, :, :].rearrange("p b l -> p (b l)")
            gs = psGS[:, :, :, :].rearrange("p a k l -> p (a k l)")
            pe.wait_ge(s["x"], 1)
            for i in range(TILES):
                ins = tr(gs[:, i * P:(i + 1) * P], X[:, i, :], c.ident[:, :])
            ins.then_inc(s["xps"], 1)
            pe.wait_ge(s["w"], 16)
            pe.wait_ge(s["xT"], 1)
            for j in range(PAIRS):
                ins = mm(gs[:, j * DHEADS:(j + 1) * DHEADS], xt[:, j * P:(j + 1) * P], w("beta"),
                         start=True, stop=True)
            ins.then_inc(s["bps"], 1)
            for j in range(PAIRS):
                if j >= 2:
                    pe.wait_ge(s["v"], j - 1)
                mm(psY[:, j % 2, :], xt[:, j * P:(j + 1) * P], w("v"), start=True, stop=True).then_inc(s["vps"], 1)
            pe.wait_ge(s["v"], PAIRS)
            pe.wait_ge(s["signed"], 1)

            def project(h, u):
                n, kq, half, roll = unit(h, u)
                if n >= 2:
                    m, r = (n - 2) // (ROLLS + 1), (n - 2) % (ROLLS + 1)
                    if r == 0:
                        pe.wait_ge(s["y0"], m + 1)
                    else:
                        pe.wait_ge(s["z"], m * ROLLS + r)
                col = at["roll"][0] + ((kq * DHEADS + h) * (ROLLS + 1) + roll) * FEAT
                mm(psY[:, n % 2, :], W[:, col:col + FEAT], xt[:, half * HALF:(half + 1) * HALF],
                   start=True, stop=True).then_inc(s["yps"], 1)

            def squares(h, name, left, right):
                for j in range(PAIRS):
                    for b, rows in enumerate(lo_hi):
                        rhs = w("eye")[rows, :] if right == "eye" else mats[right][rows, j, :]
                        ins = mm(bank(name)[rows, b, j, :], mats[left][rows, j, :], rhs, start=True, stop=True)
                return ins

            OPERANDS = {"A0": ("At0", "eye"), "A1": ("At0", "A0"), "At1": ("A0", "At0"), "A2": ("At1", "A1"),
                        "D2": ("A1", "D1"), "At2": ("A1", "At1"), "D3": ("A2", "D2"), "A3": ("At2", "A2"),
                        "D4": ("A3", "D3"), "E0": ("D4", "rhs"), "R1": ("far", "E"), "E1": ("D4", "R"),
                        "R2": ("far", "E"), "E2": ("D4", "R"), "R3": ("far", "E"), "E3": ("D4", "R"),
                        "O": ("S", "dl")}
            NEEDS = {"A1": ["A0"], "At1": ["A0"], "A2": ["A1", "At1"], "D2": ["A1"], "At2": ["A1", "At1"],
                     "D3": ["A2", "D2"], "A3": ["At2"], "D4": ["A3", "D3"], "E0": ["D4"], "R1": ["E0"], "E1": ["R1"],
                     "R2": ["E1"], "E2": ["R2"], "R3": ["E2"], "E3": ["R3"], "O": ["E3"]}

            for u in range(YUNITS):
                project(0, u)
            for h in range(DHEADS):
                pe.wait_ge(s["z"], (h + 1) * 4 * ROLLS)
                if h >= 1:
                    done(pe, h - 1, "O")
                for kq in range(2):
                    for j in range(PAIRS):
                        for b, rows in enumerate(lo_hi):
                            for r in range(ROLLS):
                                ins = mm(psM[1][rows, 0, 0, kq * PAIRS + j:kq * PAIRS + j + 1],
                                         Z[:, h % 2, r, 2 * j + b, kq, :], w("one"), start=r == 0,
                                         stop=r == ROLLS - 1)
                ins.then_inc(s["sums"], 1)
                if h == 0:
                    pe.wait_ge(s["beta"], 1)
                else:
                    pe.wait_ge(s["gsread"], h)
                for j in range(PAIRS):
                    for b, rows in enumerate(lo_hi):
                        for r in range(ROLLS):
                            ins = mm(psGS[rows, j, :, :], Z[:, h % 2, r, 2 * j + b, 0, :],
                                     Z[:, h % 2, r, 2 * j + b, :, :], start=r == 0, stop=r == ROLLS - 1)
                ins.then_inc(s["gs"], 1)
                pe.wait_ge(s["lists"], h + 1)
                for k, name in enumerate(PRODUCTS):
                    for other in NEEDS.get(name, []):
                        done(pe, h, other)
                    if k >= 2:
                        done(pe, h, PRODUCTS[k - 2])
                    if name == "D2":
                        pe.wait_ge(s["gsread"], h + 1)
                    ins = squares(h, name, *OPERANDS[name])
                    if name == "O":
                        for j in range(PAIRS):
                            for b, rows in enumerate(lo_hi):
                                ins = mm(psM[1][rows, b, 0, j:j + 1], mats["S"][rows, j, :], rk[rows, j:j + 1],
                                         start=True, stop=True)
                    ins.then_inc(s["product"], 1)
                    if h + 1 < DHEADS and k < YUNITS:
                        project(h + 1, k)
            done(pe, DHEADS - 1, "O")
            for j in range(PAIRS):
                if j >= 2:
                    pe.wait_ge(s["oT"], j - 1)
                flat = psM[0][:, j % 2, :, :].rearrange("p a b -> p (a b)")
                for k in range(4):
                    ins = tr(flat[:, k * P:(k + 1) * P],
                             O[:, j, 2 * k:2 * k + 2, :].rearrange("p h d -> p (h d)"), c.ident[:, :])
                ins.then_inc(s["ops"], 1)
            pe.wait_ge(s["oT"], PAIRS)
            for q in range(2):
                for k in range(4):
                    ins = mm(gs[:, q * HALF:(q + 1) * HALF], w("o")[:, k * P:(k + 1) * P],
                             OT[:, k, q * HALF:(q + 1) * HALF], start=k == 0, stop=k == 3)
            ins.then_inc(s["aps"], 1)
            pe.wait_ge(s["aT"], 1)
            for i in range(TILES):
                ins = tr(psY[:, i // 4, i % 4 * P:(i % 4 + 1) * P], AT[:, i * P:(i + 1) * P], c.ident[:, :])
            ins.then_inc(s["back"], 1)



GROUPS8, GHEADS, GDIM, LATENT = 8, 16, 128, 100
ZDIM = GROUPS8 * GHEADS * GDIM
FF2 = 2 * P
SPANS = P // 32
ROUNDS = GHEADS // 4
HALVES8 = GHEADS * PLACES // P
NORM_FLOOR = 1e-12
PRE_COLS = [("gamma", P), ("wk", GROUPS8 * GDIM), ("bk", GROUPS8), ("aw1", GROUPS8 * LATENT), ("aw1_b", 1),
            ("aw2", LATENT), ("aw2_b", 1), ("aw2_row", LATENT), ("row", 2 * SPANS), ("same_row", P), ("span", SPANS),
            ("one", 1), ("w1_b", FF2), ("g2", FF2), ("w2", 2 * P), ("w2_b", P)]
GROUP_COLS = [("q", GHEADS * GDIM), ("k", GDIM), ("v", GDIM), ("bq", GHEADS), ("bk", 1), ("bv", 1),
              ("g1", GHEADS)]


def lay_grouped(np, x, A):
    g = {k[len("L3_ffn_"):]: v for k, v in x.items() if k.startswith("L3_ffn_")}
    wk, wv = g["Wkv_w"][:, :GROUPS8 * GDIM], g["Wkv_w"][:, GROUPS8 * GDIM:]
    bk, bv = g["Wkv_b"][:GROUPS8 * GDIM].reshape(GROUPS8, GDIM), g["Wkv_b"][GROUPS8 * GDIM:].reshape(GROUPS8, GDIM)
    t = np.arange(P)
    row = t // PLACES

    def tiled(a):
        return np.tile(a, (P, 1))

    A["g_pre"] = pack(np, PRE_COLS, {
        "gamma": tiled(g["gamma_norm"]), "wk": wk, "bk": bk.T,
        "aw1": np.transpose(g["aw1_w"].reshape(GROUPS8, GDIM, LATENT), (1, 0, 2)).reshape(P, -1),
        "aw1_b": g["aw1_b"], "aw2": g["aw2_w"], "aw2_b": g["aw2_b"], "aw2_row": tiled(g["aw2_b"]),
        "row": (row[:, None] == np.arange(2 * SPANS)).astype(np.float32),
        "same_row": (row[:, None] == row[None, :]).astype(np.float32),
        "span": (t[:, None] // 32 == np.arange(SPANS)).astype(np.float32), "one": np.ones((P, 1), np.float32),
        "w1_b": tiled(g["wz_b1"]), "g2": tiled(g["wz_g2"]),
        "w2": np.transpose(g["wz_w2"].reshape(2, P, P), (1, 0, 2)).reshape(P, 2 * P), "w2_b": tiled(g["wz_b2"])})
    per = []
    for i in range(GROUPS8):
        cols = slice(i * GHEADS * GDIM, (i + 1) * GHEADS * GDIM)
        per.append(pack(np, GROUP_COLS, {
            "q": g["Wq_w"][:, cols], "k": wk[:, i * GDIM:(i + 1) * GDIM], "v": wv[:, i * GDIM:(i + 1) * GDIM],
            "bq": g["Wq_b"][cols].reshape(GHEADS, GDIM).T, "bk": bk[i], "bv": bv[i],
            "g1": g["wz_g1"][cols].reshape(GHEADS, GDIM).T}))
    A["g_qkv"] = np.stack(per)
    A["g_w1"] = np.transpose(g["wz_w1"].reshape(GROUPS8, GHEADS, GDIM, FF2), (0, 2, 1, 3)).reshape(
        GROUPS8, P, GHEADS * FF2)


def grouped_attention(c, A):
    nc = c.nc
    at, n_pre = columns(PRE_COLS)
    gat, n_group = columns(GROUP_COLS)
    outer = ExitStack()
    with outer:
        W = c.sb("g_pre", [P, n_pre], outer)

        def w(part, rows=P):
            return W[0:rows, at[part][0]:at[part][1]]

        XT = c.sb("g_xT", [P, TOKENS], outer)
        wS = c.sb("g_wS", [P, TILES, 2, SPANS, LATENT], outer)
        wT = c.sb("g_wT", [LATENT, 2, ROWS, PLACES], outer)
        hacc = c.sb("g_hacc", [P, TILES, FF2], outer)
        dacc = c.sb("g_dacc", [P, TILES, 2 * PLACES], outer)
        compress(c, A, W, w, XT, wS, wT)
        heads(c, A, w, gat, n_group, XT, wS, wT, hacc, dacc)
        project_out(c, w, hacc, dacc)


def compress(c, A, W, w, XT, wS, wT):
    nc = c.nc
    with ExitStack() as st:
        def sb(name, shape):
            return c.sb("gc_" + name, shape, st)

        norm = Norm(c, "gc_n", st)
        X, sq = sb("x", [P, TILES, P]), sb("sq", [P, TILES, P])
        ss, rn = sb("ss", [P, TILES]), sb("rn", [P, TILES])
        KT = sb("kT", [P, 2, HALF])
        A1 = sb("a1", [LATENT, TOKENS])
        wl, tk = sb("wl", [LATENT, ROWS, PLACES]), sb("tk", [P, TILES, LATENT])
        top, tot = sb("top", [P, TILES]), sb("tot", [P, TILES])
        topf, totf = sb("topf", [LATENT, ROWS]), sb("totf", [LATENT, ROWS])
        psT = c.ps("gc_psT", [P, TOKENS], st)
        psK = c.ps("gc_psK", [P, 2, HALF], st)
        psW = c.ps("gc_psW", [P, TOKENS], st)
        psX = c.ps("gc_psX", [P, 2, 4, P], st)
        names = ("w", "x", "ss", "rn", "xps", "xT", "kps", "k", "kused", "a1", "wps", "tok", "sub", "exp",
                 "p1", "p1ps", "wl", "wlps", "lat", "sublat", "explat", "ord", "zero")
        s = {k: c.sem("gc_" + k) for k in names}
        block = st.enter_context(nc.Block())
        units = 2 * GROUPS8

        @block.sync
        def _(sp):
            sp.dma_start(W[:, :], A["g_pre"]).then_inc(s["w"], 16)

        @block.gpsimd
        def _(pool):
            nc.gpsimd.memset(wT[:, :, :, :], 0.0).then_inc(s["zero"], 1)
            norm.power(pool)
            pool.wait_ge(s["ss"], 1)
            nc.gpsimd.tensor_tensor(rn[:, :], ss[:, :], c.half_neg[:, 0:TILES], ALU.pow).then_inc(s["rn"], 1)

        @block.scalar
        def _(act):
            a = nc.scalar.activation
            act.wait_ge(s["xps"], 1)
            a(XT[:, :], psT[:, :], ACT.Copy).then_inc(s["xT"], 1)
            act.wait_ge(s["w"], 16)
            for u in range(units):
                act.wait_ge(s["kps"], u + 1)
                if u >= 2:
                    act.wait_ge(s["kused"], u - 1)
                a(KT[:, u % 2, :], psK[:, u % 2, :], ACT.Identity, bias=w("bk")[:, u // 2:u // 2 + 1]
                  ).then_inc(s["k"], 1)
            act.wait_ge(s["kused"], units)
            a(A1[:, :], psW[0:LATENT, :], ACT.Silu, bias=w("aw1_b", LATENT)).then_inc(s["a1"], 1)
            act.wait_ge(s["wps"], 1)
            a(wl[:, :, :].rearrange("p b t -> p (b t)"), psT[0:LATENT, :], ACT.Identity, bias=w("aw2_b", LATENT)
              ).then_inc(s["lat"], 1)
            act.wait_ge(s["sub"], 1)
            a(tk[:, :, :], tk[:, :, :], ACT.Exp).then_inc(s["exp"], 1)
            act.wait_ge(s["sublat"], 1)
            a(wl[:, :, :], wl[:, :, :], ACT.Exp).then_inc(s["explat"], 1)

        @block.vector
        def _(dve):
            v = nc.vector
            o = Order(dve, s["ord"])
            norm.statistics(o, c.H)
            o.after(norm.apply(dve, X, c.H))
            o.after(v.tensor_tensor(sq[:, :, :], X[:, :, :], X[:, :, :], ALU.mult))
            o.after(v.tensor_reduce(ss[:, :], sq[:, :, :], AX, ALU.add))
            v.tensor_scalar_max(ss[:, :], ss[:, :], NORM_FLOOR ** 2).then_inc(s["ss"], 1)
            dve.wait_ge(s["w"], 16)
            dve.wait_ge(s["rn"], 1)
            for i in range(TILES):
                ins = v.tensor_scalar(X[:, i, :], X[:, i, :], rn[:, i:i + 1], float(P) ** 0.5, ALU.mult, ALU.mult)
            o.after(ins)
            v.tensor_tensor(X[:, :, :], X[:, :, :], w("gamma").unsqueeze(1).broadcast_to([P, TILES, P]), ALU.mult
                            ).then_inc(s["x"], 1)
            dve.wait_ge(s["wps"], 1)
            o.after(v.tensor_tensor(tk[:, :, :], psX[:, :, :, 0:LATENT].rearrange("p a i l -> p (a i) l"),
                                    w("aw2_row").unsqueeze(1).broadcast_to([P, TILES, LATENT]), ALU.add))
            o.after(v.tensor_reduce(top[:, :], tk[:, :, :], AX, ALU.max))
            v.tensor_tensor(tk[:, :, :], tk[:, :, :], top[:, :].unsqueeze(2).broadcast_to([P, TILES, LATENT]),
                            ALU.subtract).then_inc(s["sub"], 1)
            dve.wait_ge(s["lat"], 1)
            o.after(v.tensor_reduce(topf[:, :], wl[:, :, :], AX, ALU.max))
            v.tensor_tensor(wl[:, :, :], wl[:, :, :], topf[:, :].unsqueeze(2).broadcast_to([LATENT, ROWS, PLACES]),
                            ALU.subtract).then_inc(s["sublat"], 1)
            dve.wait_ge(s["exp"], 1)
            o.after(v.tensor_reduce(tot[:, :], tk[:, :, :], AX, ALU.add))
            o.after(v.reciprocal(tot[:, :], tot[:, :]))
            o.after(v.tensor_scalar_mul(tot[:, :], tot[:, :], 0.5 / PLACES))
            v.tensor_tensor(tk[:, :, :], tk[:, :, :], tot[:, :].unsqueeze(2).broadcast_to([P, TILES, LATENT]),
                            ALU.mult).then_inc(s["p1"], 1)
            dve.wait_ge(s["explat"], 1)
            o.after(v.tensor_reduce(totf[:, :], wl[:, :, :], AX, ALU.add))
            o.after(v.reciprocal(totf[:, :], totf[:, :]))
            o.after(v.tensor_scalar_mul(totf[:, :], totf[:, :], 0.5 / LATENT))
            o.after(v.tensor_tensor(wl[:, :, :], wl[:, :, :],
                                    totf[:, :].unsqueeze(2).broadcast_to([LATENT, ROWS, PLACES]), ALU.mult))
            dve.wait_ge(s["p1ps"], 1)
            v.tensor_tensor(wl[:, :, :].rearrange("p b t -> p (b t)"), wl[:, :, :].rearrange("p b t -> p (b t)"),
                            psW[0:LATENT, :], ALU.add).then_inc(s["wl"], 1)
            dve.wait_ge(s["wl"], 1)
            dve.wait_ge(s["zero"], 1)
            for par in range(2):
                rows = wl[:, :, :].rearrange("p (n r) t -> p n r t", r=2)[:, :, par, :]
                v.tensor_copy(wT[:, par, :, :].rearrange("p (n r) t -> p n r t", r=2)[:, :, par, :], rows)
            dve.wait_ge(s["wlps"], 1)
            for par in range(2):
                for q in range(SPANS):
                    v.tensor_scalar(wS[:, :, par, q, :], psX[:, :, :, 0:LATENT].rearrange("p a i l -> p (a i) l"),
                                    w("row")[:, 2 * q + par:2 * q + par + 1], float(GDIM) ** -0.5,
                                    ALU.mult, ALU.mult)

        @block.tensor
        def _(pe):
            mm, tr = nc.tensor.matmul, nc.tensor.transpose
            pe.wait_ge(s["x"], 1)
            transpose_tokens(c, psT, X).then_inc(s["xps"], 1)
            pe.wait_ge(s["w"], 16)
            pe.wait_ge(s["xT"], 1)

            def reduce_keys(u):
                g, q = u // 2, u % 2
                pe.wait_ge(s["k"], u + 1)
                ins = mm(psW[0:LATENT, q * HALF:(q + 1) * HALF], w("aw1")[:, g * LATENT:(g + 1) * LATENT],
                         KT[:, u % 2, :], start=g == 0, stop=g == GROUPS8 - 1)
                ins.then_inc(s["kused"], 1)
                return ins

            for u in range(units):
                g, q = u // 2, u % 2
                if u >= 2:
                    pe.wait_ge(s["k"], u - 1)
                mm(psK[:, u % 2, :], w("wk")[:, g * GDIM:(g + 1) * GDIM], XT[:, q * HALF:(q + 1) * HALF],
                   start=True, stop=True).then_inc(s["kps"], 1)
                if u >= 1:
                    reduce_keys(u - 1)
            reduce_keys(units - 1)
            pe.wait_ge(s["a1"], 1)
            for q in range(2):
                mm(psT[0:LATENT, q * HALF:(q + 1) * HALF], w("aw2", LATENT), A1[:, q * HALF:(q + 1) * HALF],
                   start=True, stop=True)
            for i in range(TILES):
                ins = mm(psX[:, i // 4, i % 4, 0:LATENT], A1[:, i * P:(i + 1) * P], w("aw2", LATENT),
                         start=True, stop=True)
            ins.then_inc(s["wps"], 1)
            pe.wait_ge(s["p1"], 1)
            for i in range(TILES):
                ins = tr(psW[0:LATENT, i * P:(i + 1) * P], tk[:, i, :], c.ident[:, :])
            ins.then_inc(s["p1ps"], 1)
            pe.wait_ge(s["wl"], 1)
            flat = wl[:, :, :].rearrange("p b t -> p (b t)")
            for i in range(TILES):
                ins = tr(psX[:, i // 4, i % 4, 0:LATENT], flat[:, i * P:(i + 1) * P], c.ident[0:LATENT, 0:LATENT])
            ins.then_inc(s["wlps"], 1)


def heads(c, A, w, gat, n_group, XT, wS, wT, hacc, dacc):
    nc = c.nc
    UNITS, TURN = GROUPS8 * TILES, 2 * TILES
    ROWCOLS = GHEADS * PLACES
    PREP = 8
    W1_PARTS = 4
    with ExitStack() as st:
        def sb(name, shape):
            return c.sb("gh_" + name, shape, st)

        G = sb("qkv", [P, 2, n_group])
        W1 = sb("w1", [P, 2, GHEADS, FF2])
        KT, VT = sb("kT", [P, TOKENS]), sb("vT", [P, 2, TOKENS])
        V, VV = sb("v", [P, 2, TILES, GDIM]), sb("vv", [P, P])
        bqk = sb("bqk", [P, TILES, GHEADS])
        QT = sb("qT", [P, GHEADS, P])
        AT = sb("aT", [P, 2, ROWCOLS])
        PR = sb("p", [P, 2, 4, SPANS, LATENT])
        top, tot = sb("top", [P, 4, SPANS]), sb("tot", [P, 2, 4, SPANS])
        PT = sb("pT", [LATENT, SPANS, 2, ROWCOLS])
        BT = sb("bT", [P, 2, ROWCOLS])
        DD = sb("dd", [P, 2, ROWCOLS])
        dred = sb("dred", [P, 2, PLACES])
        zT = sb("zT", [P, GHEADS, 8, PLACES])
        psS = c.ps("gh_psS", [P, 4, HALF], st)
        psA = c.ps("gh_psA", [P, 2, ROWCOLS], st)
        psR = c.ps("gh_psR", [P, 2, HALF], st)
        psH = c.ps("gh_psH", [P, HALF], st)
        names = ("gzero", "round", "read", "aps", "aT", "sps", "max", "sub", "exp", "total", "inv", "norm", "vvps",
                 "vv", "bps", "bT", "zps", "zact", "zdve", "cps", "cread", "dred", "hps", "h", "w1s")
        s = {k: c.sem("gh_" + k) for k in names}
        s_g = [c.sem(f"gh_qkv{i}") for i in range(2)]
        s_w = [c.sem(f"gh_w1_{i}") for i in range(2)]
        block = st.enter_context(nc.Block())

        class Slot:

            def __init__(self, it, col):
                self.it, self.col = it, col
                known = isinstance(it, int)
                v = it * TURN + col if known else None
                self.opens = not known or v < UNITS
                self.mids = not known or 1 <= v <= UNITS
                self.closes = not known or 2 <= v
                self.later = not known or v >= 3
                self.preps = self.col % TILES == TILES - 1 and (not known or v < UNITS - 1)
                self.first = known and v == 0
                self.tile, self.group = col % TILES, col // TILES % 2
                self.mid_tile, self.mid_group = (col - 1) % TILES, (col - 1) // TILES % 2
                self.out_tile, self.out_group = (col - 2) % TILES, (col - 2) // TILES % 2
                self.base = PREP if self.first else 8 * col + 4 + PREP * (col // TILES)
                if known and v == UNITS:
                    self.base -= PREP

            def units(self, k):
                return self.it * TURN + (self.col + k)

            def rounds(self, k):
                return self.it * (8 * TURN + 2 * PREP) + (self.base + k)

            def loads(self, k):
                n = self.col // TILES + k
                return n % 2, self.it * 16 + (n // 2 + 1) * 16

        def slots(eng, body):
            for col in range(2):
                body(Slot(0, col))
            with eng.Fori(0, UNITS // TURN - 1) as it:
                for col in range(2, TURN + 2):
                    body(Slot(it, col))
            for col in range(2, TURN + 2):
                body(Slot(UNITS // TURN - 1, col))

        def g(gg, part):
            return G[:, gg, gat[part][0]:gat[part][1]]

        @block.sync
        def _(sp):
            for gg in range(2):
                sp.dma_start(G[:, gg, :], A["g_qkv"][gg, :, :]).then_inc(s_g[gg], 16)
                sp.dma_start(W1[:, gg, :, :].rearrange("p h f -> p (h f)"), A["g_w1"][gg, :, :]).then_inc(s_w[gg], 16)
            with sp.Fori(1, GROUPS8 // 2) as it:
                for gg in range(2):
                    sp.wait_ge(s["aps"], it * TURN + (gg * TILES + TILES - TURN))
                    sp.wait_ge(s["w1s"], it * 2 * W1_PARTS + (gg + 1 - 2) * W1_PARTS)
                    sp.dma_start(G[:, gg, :], A["g_qkv"][bass.ds(it * 2 + gg, 1), :, :].rearrange("a p n -> (a p) n")
                                 ).then_inc(s_g[gg], 16)
                    sp.wait_ge(s["hps"], it * TURN + (gg * TILES + TILES - TURN))
                    sp.dma_start(W1[:, gg, :, :].rearrange("p h f -> p (h f)"),
                                 A["g_w1"][bass.ds(it * 2 + gg, 1), :, :].rearrange("a p n -> (a p) n")
                                 ).then_inc(s_w[gg], 16)

        @block.gpsimd
        def _(pool):
            def scale_w1(gg, part):
                hh = slice(part * GHEADS // W1_PARTS, (part + 1) * GHEADS // W1_PARTS)
                nc.gpsimd.tensor_tensor(W1[:, gg, hh, :], W1[:, gg, hh, :],
                                        g(gg, "g1")[:, hh].unsqueeze(2).broadcast_to([P, GHEADS // W1_PARTS, FF2]),
                                        ALU.mult).then_inc(s["w1s"], 1)

            nc.gpsimd.memset(hacc[:, :, :], 0.0).then_inc(s["gzero"], 1)
            nc.gpsimd.memset(dacc[:, :, :], 0.0).then_inc(s["gzero"], 1)

            def body(t):
                if t.first:
                    pool.wait_ge(s_g[0], 16)
                    pool.wait_ge(s_w[0], 16)
                    for part in range(W1_PARTS):
                        scale_w1(0, part)
                if t.opens:
                    pool.wait_ge(s["inv"], t.units(1))
                    b = t.col % 2
                    nc.gpsimd.tensor_tensor(PR[:, b, :, :, :], PR[:, b, :, :, :],
                                            tot[:, b, :, :].unsqueeze(3).broadcast_to([P, 4, SPANS, LATENT]),
                                            ALU.mult).then_inc(s["norm"], 1)
                part = t.tile - 3
                if 0 <= part < W1_PARTS and (not isinstance(t.it, int) or t.it * TURN + t.col < UNITS - TILES):
                    gg, loads = t.loads(1)
                    pool.wait_ge(s_g[gg], loads)
                    pool.wait_ge(s_w[gg], loads)
                    scale_w1(gg, part)

            slots(pool, body)

        @block.scalar
        def _(act):
            a = nc.scalar.activation

            def rounds(t, k, n, put):
                for r in range(n):
                    act.wait_ge(s["round"], t.rounds(k + r + 1))
                    put(r, psR[:, r % 2, :]).then_inc(s["read"], 1)

            def prep(t, k, gg):
                def put(r, bank):
                    q = r % 2
                    half = slice(q * HALF, (q + 1) * HALF)
                    if r < 2:
                        return a(KT[:, half], bank, ACT.Identity, bias=g(gg, "bk"))
                    if r < 4:
                        return a(VT[:, gg, half], bank, ACT.Identity, bias=g(gg, "bv"))
                    tiles = slice(q * TILES // 2, (q + 1) * TILES // 2)
                    if r < 6:
                        return a(bqk[:, tiles, :].rearrange("p i h -> p (i h)"), bank[:, 0:TILES // 2 * GHEADS],
                                 ACT.Copy)
                    return a(V[:, gg, tiles, :].rearrange("p i d -> p (i d)"), bank, ACT.Copy)
                rounds(t, k, PREP, put)

            def body(t):
                if t.first:
                    prep(t, -PREP, 0)
                k = 0
                if t.opens:
                    rounds(t, 0, ROUNDS, lambda r, bank: a(
                        QT[:, 4 * r:4 * r + 4, :].rearrange("p h t -> p (h t)"), bank, ACT.Copy))
                    k += ROUNDS
                if t.preps:
                    prep(t, k, 1 - t.group)
                    k += PREP
                if t.mids:
                    rounds(t, k, SPANS, lambda r, bank: a(
                        PT[:, r, :, :].rearrange("p a b -> p (a b)"), bank[0:LATENT, :], ACT.Copy))
                    act.wait_ge(s["bps"], t.units(0))
                    a(BT[:, :, :], psA[:, :, :], ACT.Copy).then_inc(s["bT"], 1)
                if t.opens:
                    act.wait_ge(s["sub"], t.units(1))
                    b = t.col % 2
                    a(PR[:, b, :, :, :], PR[:, b, :, :, :], ACT.Exp).then_inc(s["exp"], 1)
                if t.mids:
                    act.wait_ge(s["zps"], t.units(0))
                    for q in (0, 1):
                        ins = a(zT[:, :, 2 * q:2 * q + 2, :].rearrange("p h r t -> p r h t"),
                                psS[:, q, :].rearrange("p (r h t) -> p r h t", r=2, h=GHEADS), ACT.Copy)
                    ins.then_inc(s["zact"], 1)

            slots(act, body)

        @block.vector
        def _(dve):
            v = nc.vector

            def body(t):
                b = t.col % 2
                if t.opens:
                    dve.wait_ge(s["aps"], t.units(1))
                    v.tensor_tensor(AT[:, :, :].rearrange("p r (h t) -> p r h t", t=PLACES),
                                    psA[:, :, :].rearrange("p r (h t) -> p r h t", t=PLACES),
                                    bqk[:, t.tile, :].unsqueeze(1).unsqueeze(3)
                                    .broadcast_to([P, 2, GHEADS, PLACES]), ALU.add).then_inc(s["aT"], 1)
                    sc = psS[:, :, 0:SPANS * LATENT].rearrange("p j (q l) -> p j q l", l=LATENT)
                    dve.wait_ge(s["sps"], t.units(1))
                    v.tensor_reduce(top[:, :, :], sc, AX, ALU.max).then_inc(s["max"], 1)
                if t.mids:
                    dve.wait_ge(s["vvps"], t.units(0))
                    v.tensor_tensor(VV[:, :], psA[:, 0, 0:P], w("same_row"), ALU.mult).then_inc(s["vv"], 1)
                if t.opens:
                    dve.wait_ge(s["max"], t.units(1))
                    v.tensor_tensor(PR[:, b, :, :, :], sc,
                                    top[:, :, :].unsqueeze(3).broadcast_to([P, 4, SPANS, LATENT]), ALU.subtract
                                    ).then_inc(s["sub"], 1)
                    dve.wait_ge(s["exp"], t.units(1))
                    v.tensor_reduce(tot[:, b, :, :], PR[:, b, :, :, :], AX, ALU.add).then_inc(s["total"], 1)
                    dve.wait_ge(s["total"], t.units(1))
                    v.reciprocal(tot[:, b, :, :], tot[:, b, :, :]).then_inc(s["inv"], 1)
                if t.closes:
                    dve.wait_ge(s["hps"], t.units(-1))
                    v.tensor_tensor(hacc[:, t.out_tile, :], hacc[:, t.out_tile, :], psH[:, 0:FF2], ALU.add
                                    ).then_inc(s["h"], 1)
                if t.mids:
                    dve.wait_ge(s["zps"], t.units(0))
                    for q in (2, 3):
                        ins = v.tensor_copy(zT[:, :, 2 * q:2 * q + 2, :].rearrange("p h r t -> p r h t"),
                                            psS[:, q, :].rearrange("p (r h t) -> p r h t", r=2, h=GHEADS))
                    ins.then_inc(s["zdve"], 1)
                    dve.wait_ge(s["cps"], t.units(0))
                    v.tensor_tensor(DD[:, :, :], BT[:, :, :], psA[:, :, :], ALU.mult).then_inc(s["cread"], 1)
                    dve.wait_ge(s["cread"], t.units(0))
                    v.tensor_reduce(dred[:, :, :], DD[:, :, :].rearrange("p r (h t) -> p r t h", t=PLACES), AX,
                                    ALU.add).then_inc(s["dred"], 1)
                    dve.wait_ge(s["dred"], t.units(0))
                    v.tensor_tensor(dacc[:, t.mid_tile, :], dacc[:, t.mid_tile, :],
                                    dred[:, :, :].rearrange("p r t -> p (r t)"), ALU.add)

            dve.wait_ge(s["gzero"], 2)
            slots(dve, body)

        @block.tensor
        def _(pe):
            mm, tr = nc.tensor.matmul, nc.tensor.transpose

            def round_(t, k, r, put, first=False):
                if not (first and r < 2):
                    pe.wait_ge(s["read"], t.rounds(k + r - 1))
                put(r, psR[:, r % 2, :]).then_inc(s["round"], 1)

            def prep(t, k, gg, loads):
                pe.wait_ge(s_g[gg], loads)

                def put(r, bank):
                    q = r % 2
                    half = slice(q * HALF, (q + 1) * HALF)
                    if r < 4:
                        return mm(bank, g(gg, "kv"[r // 2]), XT[:, half], start=True, stop=True)
                    if r == 6:
                        pe.wait_ge(s["read"], t.rounds(k + 4))
                    if r == 4:
                        pe.wait_ge(s["read"], t.rounds(k + 3))
                    for j in range(TILES // 2):
                        i = q * TILES // 2 + j
                        if r < 6:
                            ins = mm(bank[:, j * GHEADS:(j + 1) * GHEADS], KT[:, i * P:(i + 1) * P], g(gg, "bq"),
                                     start=True, stop=True)
                        else:
                            ins = tr(bank[:, j * P:(j + 1) * P], VT[:, gg, i * P:(i + 1) * P], c.ident[:, :])
                    return ins

                for r in range(PREP):
                    round_(t, k, r, put, first=t.first)

            def body(t):
                pieces = [3, 3, 2, 3, 2, 3]
                done = [0]

                def out_heads():
                    if not t.closes:
                        return
                    if done[0] == 0:
                        pe.wait_ge(s["zact"], t.units(-1))
                        pe.wait_ge(s["zdve"], t.units(-1))
                        if t.later:
                            pe.wait_ge(s["h"], t.units(-2))
                        if t.out_tile == 0:
                            n = (t.col - 2) // TILES + 1
                            pe.wait_ge(s["w1s"], t.it * 2 * W1_PARTS + n * W1_PARTS)
                    for h in range(done[0], done[0] + pieces[0]):
                        ins = mm(psH[:, 0:FF2], zT[:, h, :, :].rearrange("p r t -> p (r t)"),
                                 W1[:, t.out_group, h, :], start=h == 0, stop=h == GHEADS - 1)
                    done[0] += pieces.pop(0)
                    if not pieces:
                        ins.then_inc(s["hps"], 1)

                if t.first:
                    prep(t, -PREP, 0, 16)
                k = 0
                if t.opens:
                    if t.tile == 0:
                        gg, loads = t.loads(0)
                        pe.wait_ge(s_g[gg], loads)

                    def queries(r, bank):
                        for h in range(4):
                            lo = gat["q"][0] + (4 * r + h) * GDIM
                            ins = mm(bank[:, h * P:(h + 1) * P], G[:, t.group, lo:lo + GDIM],
                                     XT[:, t.tile * P:(t.tile + 1) * P], start=True, stop=True)
                        return ins
                    for r in range(ROUNDS):
                        round_(t, 0, r, queries)
                    k += ROUNDS
                out_heads()
                if t.opens:
                    pe.wait_ge(s["read"], t.rounds(ROUNDS))
                    if t.closes:
                        pe.wait_ge(s["cread"], t.units(-1))
                    for q in range(SPANS):
                        lo = t.tile * P + q * 32
                        for par in range(2):
                            row = 2 * q + par
                            ins = mm(psA[q * 32:(q + 1) * 32, par, :], KT[:, lo:lo + 32],
                                     QT[:, :, row * PLACES:(row + 1) * PLACES], start=True, stop=True)
                    ins.then_inc(s["aps"], 1)
                out_heads()
                if t.opens:
                    pe.wait_ge(s["aT"], t.units(1))
                    for j in range(4):
                        par, hh = j // 2, j % 2
                        ins = mm(psS[:, j, 0:SPANS * LATENT], AT[:, par, hh * P:(hh + 1) * P],
                                 wS[:, t.tile, par, :, :].rearrange("p q l -> p (q l)"), start=True, stop=True)
                    ins.then_inc(s["sps"], 1)
                if t.preps:
                    gg, loads = t.loads(1)
                    prep(t, k, gg, loads)
                    k += PREP
                if t.mids:
                    if t.closes:
                        pe.wait_ge(s["cread"], t.units(-1))
                    mm(psA[:, 0, 0:P], VT[:, t.mid_group, t.mid_tile * P:(t.mid_tile + 1) * P],
                       VT[:, t.mid_group, t.mid_tile * P:(t.mid_tile + 1) * P], start=True, stop=True
                       ).then_inc(s["vvps"], 1)
                    pe.wait_ge(s["norm"], t.units(0))

                    def turned(q, bank):
                        for j in range(4):
                            ins = tr(bank[0:LATENT, j * P:(j + 1) * P], PR[:, (t.col - 1) % 2, j, q, :],
                                     c.ident[:, :])
                        return ins
                    for q in range(SPANS):
                        round_(t, k, q, turned)
                        if q in (1, 2):
                            out_heads()
                else:
                    out_heads()
                    out_heads()
                out_heads()
                if t.mids:
                    pe.wait_ge(s["read"], t.rounds(k + SPANS))
                    pe.wait_ge(s["vv"], t.units(0))
                    cols = wT[:, :, :, :].rearrange("p r b t -> p r (b t)")
                    for par in range(2):
                        for q in range(SPANS):
                            lo = t.mid_tile * P + q * 32
                            ins = mm(psA[q * 32:(q + 1) * 32, par, :], cols[:, par, lo:lo + 32], PT[:, q, par, :],
                                     start=True, stop=True)
                    ins.then_inc(s["bps"], 1)
                out_heads()
                if t.mids:
                    pe.wait_ge(s["bT"], t.units(0))
                    if t.opens:
                        pe.wait_ge(s["sub"], t.units(1))
                    for par in range(2):
                        for q in range(SPANS):
                            span = slice(q * 32, (q + 1) * 32)
                            ins = mm(psS[:, q, par * ROWCOLS:(par + 1) * ROWCOLS],
                                     V[span, t.mid_group, t.mid_tile, :], BT[span, par, :], start=True, stop=True)
                    ins.then_inc(s["zps"], 1)
                    mm(psA[:, :, :], VV[:, :], BT[:, :, :], start=True, stop=True).then_inc(s["cps"], 1)

            slots(pe, body)


def project_out(c, w, hacc, dacc):
    nc = c.nc
    with ExitStack() as st:
        def sb(name, shape):
            return c.sb("go_" + name, shape, st)

        E = sb("e", [P, TILES, SPANS, 2 * PLACES])
        n2, rz, ss, rh = (sb(n, [P, TILES]) for n in ("n2", "rz", "ss", "rh"))
        h1, sq = sb("h1", [P, TILES, FF2]), sb("sq", [P, TILES, FF2])
        hT = sb("hT", [P, 2, TOKENS])
        out = sb("out", [P, TILES, P])
        psN = c.ps("go_psN", [P, TILES], st)
        psT = c.ps("go_psT", [P, 2, TOKENS], st)
        psO = c.ps("go_psO", [P, TOKENS], st)
        names = ("e", "n2ps", "n2", "rz", "pre", "h1", "ss", "rh", "h1n", "tps", "hT", "ops", "sum", "silu", "ord")
        s = {k: c.sem("go_" + k) for k in names}
        block = st.enter_context(nc.Block())

        @block.gpsimd
        def _(pool):
            pool.wait_ge(s["n2"], 1)
            nc.gpsimd.tensor_tensor(rz[:, :], n2[:, :], c.half_neg[:, 0:TILES], ALU.pow).then_inc(s["rz"], 1)
            pool.wait_ge(s["ss"], 1)
            nc.gpsimd.tensor_tensor(rh[:, :], ss[:, :], c.half_neg[:, 0:TILES], ALU.pow).then_inc(s["rh"], 1)

        @block.scalar
        def _(act):
            a = nc.scalar.activation
            act.wait_ge(s["pre"], 1)
            a(h1[:, :, :], hacc[:, :, :], ACT.Silu).then_inc(s["h1"], 1)
            act.wait_ge(s["tps"], 1)
            a(hT[:, :, :], psT[:, :, :], ACT.Copy).then_inc(s["hT"], 1)
            act.wait_ge(s["sum"], 1)
            a(out[:, :, :], out[:, :, :], ACT.Silu).then_inc(s["silu"], 1)

        @block.vector
        def _(dve):
            v = nc.vector
            o = Order(dve, s["ord"])
            for i in range(TILES):
                ins = v.tensor_tensor(E[:, i, :, :], dacc[:, i, :].unsqueeze(1).broadcast_to([P, SPANS, 2 * PLACES]),
                                      w("span").unsqueeze(2).broadcast_to([P, SPANS, 2 * PLACES]), ALU.mult)
            ins.then_inc(s["e"], 1)
            dve.wait_ge(s["n2ps"], 1)
            v.tensor_scalar_max(n2[:, :], psN[:, :], NORM_FLOOR ** 2).then_inc(s["n2"], 1)
            dve.wait_ge(s["rz"], 1)
            for i in range(TILES):
                ins = v.tensor_scalar(hacc[:, i, :], hacc[:, i, :], rz[:, i:i + 1], float(ZDIM) ** 0.5,
                                      ALU.mult, ALU.mult)
            o.after(ins)
            v.tensor_tensor(hacc[:, :, :], hacc[:, :, :], w("w1_b").unsqueeze(1).broadcast_to([P, TILES, FF2]),
                            ALU.add).then_inc(s["pre"], 1)
            dve.wait_ge(s["h1"], 1)
            o.after(v.tensor_tensor(sq[:, :, :], h1[:, :, :], h1[:, :, :], ALU.mult))
            o.after(v.tensor_reduce(ss[:, :], sq[:, :, :], AX, ALU.add))
            v.tensor_scalar_max(ss[:, :], ss[:, :], NORM_FLOOR ** 2).then_inc(s["ss"], 1)
            dve.wait_ge(s["rh"], 1)
            for i in range(TILES):
                ins = v.tensor_scalar(h1[:, i, :], h1[:, i, :], rh[:, i:i + 1], float(FF2) ** 0.5,
                                      ALU.mult, ALU.mult)
            o.after(ins)
            v.tensor_tensor(h1[:, :, :], h1[:, :, :], w("g2").unsqueeze(1).broadcast_to([P, TILES, FF2]), ALU.mult
                            ).then_inc(s["h1n"], 1)
            dve.wait_ge(s["ops"], 1)
            v.tensor_tensor(out[:, :, :], psO[:, :].rearrange("p (i d) -> p i d", d=P),
                            w("w2_b").unsqueeze(1).broadcast_to([P, TILES, P]), ALU.add).then_inc(s["sum"], 1)
            dve.wait_ge(s["silu"], 1)
            v.tensor_tensor(c.H[:, :, :], c.H[:, :, :], out[:, :, :], ALU.add)

        @block.tensor
        def _(pe):
            mm, tr = nc.tensor.matmul, nc.tensor.transpose
            pe.wait_ge(s["e"], 1)
            for i in range(TILES):
                ins = mm(psN[:, i:i + 1], E[:, i, :, :].rearrange("p q t -> p (q t)"), w("one"),
                         start=True, stop=True)
            ins.then_inc(s["n2ps"], 1)
            pe.wait_ge(s["h1n"], 1)
            for k in range(2):
                for i in range(TILES):
                    ins = tr(psT[:, k, i * P:(i + 1) * P], h1[:, i, k * P:(k + 1) * P], c.ident[:, :])
            ins.then_inc(s["tps"], 1)
            pe.wait_ge(s["hT"], 1)
            for i in range(TILES):
                for k in range(2):
                    ins = mm(psO[:, i * P:(i + 1) * P], hT[:, k, i * P:(i + 1) * P], w("w2")[:, k * P:(k + 1) * P],
                             start=k == 0, stop=k == 1)
            ins.then_inc(s["ops"], 1)



def build(nc, A, hin, out):
    layers = [token_embedding, mamba, switch_experts, delta_attention, lstm_experts, linear_attention,
              binned_experts, causal_attention, grouped_attention]
    with ExitStack() as stack:
        c = Chip(nc, stack)
        c.H = c.sb("stream", [P, TILES, P])
        c.ident = c.sb("ident", [P, P])
        c.half_neg = c.sb("half_neg", [P, 2 * TILES])
        start(c, hin)
        for n in LAYERS:
            if n == 5:
                c.renew()
            layers[n](c, A)
        finish(c, out)
        c.sems.close()


def lay_out(x):
    import numpy as np
    A = {}
    if 0 in LAYERS:
        w = np.transpose(x["L0_tok_weight"], (1, 0, 2)).reshape(GENES, EMB)
        A["genes"] = np.concatenate([w, x["L0_tok_mask"], np.transpose(x["x"])], axis=1).reshape(
            GENE_TILES, GENE_P, EMB_ROW)
        A["tok_bias"] = x["L0_tok_bias"].reshape(1, EMB)
    for fn, n in ((lay_mamba, 1), (lay_switch, 2), (lay_delta, 3), (lay_lstm, 4), (lay_linear, 5), (lay_binned, 6),
                  (lay_causal, 7), (lay_grouped, 8)):
        if n in LAYERS:
            fn(np, x, A)
    return {k: np.ascontiguousarray(v) for k, v in A.items()}


def kernel(**inputs):
    import numpy as np
    import concourse.bacc as bacc
    from concourse.bass_utils import run_bass_kernel_spmd

    x = {k: np.asarray(v) for k, v in inputs.items()}
    arrays = lay_out(x)
    nc = bacc.Bacc("TRN2", target_bir_lowering=False, num_devices=1)
    A = {k: nc.dram_tensor("in_" + k, list(a.shape), F32, kind="ExternalInput").ap() for k, a in arrays.items()}
    feed = {"in_" + k: a for k, a in arrays.items()}
    hin = None
    if "hin" in x:
        hin = nc.dram_tensor("in_hin", list(x["hin"].shape), F32, kind="ExternalInput").ap()
        feed["in_hin"] = np.ascontiguousarray(x["hin"])
    out = nc.dram_tensor("out_0", [ROWS, PLACES, P], F32, kind="ExternalOutput").ap()
    build(nc, A, hin, out)
    r = run_bass_kernel_spmd(nc, [feed], core_ids=[0])
    return r.results[0]["out_0"]
```

```python
from contextlib import ExitStack

import concourse.bass as bass
from concourse import mybir

F32 = mybir.dt.float32
ALU = mybir.AluOpType
ACT = mybir.ActivationFunctionType
AX = mybir.AxisListType.X

P = 128
ROWS, PLACES = 64, 16
TOKENS = ROWS * PLACES
TILES = TOKENS // P
HALF = 512
LN_EPS = 1e-5


class Chip:

    def __init__(self, nc, stack):
        self.nc, self.stack = nc, stack
        self.sems, self.used = ExitStack(), []

    def sem(self, name):
        h = self.sems.enter_context(self.nc.semaphore(name))
        self.used.append(h)
        return h

    def renew(self):
        nc, used = self.nc, self.used
        if used:
            with nc.Block() as block:
                @block.gpsimd
                def _(pool):
                    for h in used:
                        nc.gpsimd.sem_clear(h)
            self.sems.close()
        self.sems, self.used = ExitStack(), []

    def sb(self, name, shape, stack=None, dt=F32):
        return (stack or self.stack).enter_context(self.nc.sbuf_tensor(name, shape, dt))

    def ps(self, name, shape, stack):
        return stack.enter_context(self.nc.psum_tensor(name, shape, F32))


class Order:

    def __init__(self, eng, sem):
        self.eng, self.sem, self.n = eng, sem, 0

    def after(self, ins):
        self.n += 1
        ins.then_inc(self.sem, 1)
        self.eng.wait_ge(self.sem, self.n)


def constants(c, pool, s_zero, s_ident):
    nc = c.nc
    nc.gpsimd.memset(c.ident[:, :], 0.0).then_inc(s_zero, 1)
    nc.gpsimd.memset(c.half_neg[:, :], -0.5).then_inc(s_zero, 1)
    pool.wait_ge(s_zero, 2)
    nc.gpsimd.affine_select(out=c.ident[:, :], in_=c.ident[:, :], compare_op=ALU.not_equal, fill=1.0,
                            base=0, pattern=[[-1, P]], channel_multiplier=1).then_inc(s_ident, 1)
    pool.wait_ge(s_ident, 1)


def finish(c, out):
    nc = c.nc
    s_out = c.sem("stored")
    with nc.Block() as block:
        @block.sync
        def _(sp):
            sp.dma_start(out.rearrange("b e d -> (b e) d").rearrange("(i p) d -> p i d", p=P), c.H[:, :, :]
                         ).then_inc(s_out, 16)
            sp.wait_ge(s_out, 16)



class Norm:

    def __init__(self, c, name, stack):
        self.c = c
        self.stats = c.sb(name + "_stats", [P, TILES, 6], stack)
        self.mean_var = c.sb(name + "_mean_var", [P, TILES, 2], stack)
        self.var_eps = c.sb(name + "_var_eps", [P, TILES], stack)
        self.rstd = c.sb(name + "_rstd", [P, TILES], stack)
        self.s_var, self.s_rstd = c.sem(name + "_var"), c.sem(name + "_rstd")

    def statistics(self, o, src):
        v = self.c.nc.vector
        for i in range(TILES):
            last = v.bn_stats(self.stats[:, i, :], src[:, i, :])
        o.after(last)
        for i in range(TILES):
            last = v.bn_aggr(self.mean_var[:, i, :], self.stats[:, i, :])
        o.after(last)
        v.tensor_scalar_add(self.var_eps[:, :], self.mean_var[:, :, 1], LN_EPS).then_inc(self.s_var, 1)

    def power(self, pool):
        pool.wait_ge(self.s_var, 1)
        self.c.nc.gpsimd.tensor_tensor(self.rstd[:, :], self.var_eps[:, :], self.c.half_neg[:, 0:TILES],
                                       ALU.pow).then_inc(self.s_rstd, 1)

    def apply(self, dve, dst, src):
        dve.wait_ge(self.s_rstd, 1)
        for i in range(TILES):
            last = self.c.nc.vector.tensor_scalar(dst[:, i, :], src[:, i, :], self.mean_var[:, i, 0:1],
                                                  self.rstd[:, i:i + 1], ALU.subtract, ALU.mult)
        return last


def transpose_tokens(c, dst, src):
    for i in range(TILES):
        last = c.nc.tensor.transpose(dst[:, i * P:(i + 1) * P], src[:, i, :], c.ident[:, :])
    return last



GENES, GENE_P, SLOTS = 5000, 125, 5
GENE_TILES = GENES // GENE_P
EMB = PLACES * P
EMB_ROW = EMB + P + ROWS


def token_embedding(c, A):
    nc = c.nc
    s_load = [c.sem(f"genes_loaded{s}") for s in range(SLOTS)]
    s_masked, s_used, s_bias, s_sum = c.sem("masked"), c.sem("genes_used"), c.sem("emb_bias"), c.sem("emb_sum")
    s_zero, s_ident = c.sem("zeroed"), c.sem("identity")
    s_swap, s_swapped, s_back = c.sem("emb_swap"), c.sem("emb_swapped"), c.sem("emb_back")
    with ExitStack() as st:
        ring = c.sb("gene_ring", [GENE_P, SLOTS, EMB_ROW], st)
        bias = c.sb("emb_bias_rows", [P, EMB // 2], st)
        summed = c.sb("emb_rows", [P, PLACES // 2, P], st)
        feat = c.sb("emb_feat", [P, ROWS, PLACES], st)
        acc = c.ps("emb_acc", [P, EMB // 2], st)
        swap = c.ps("emb_swap_ps", [P, PLACES, ROWS], st)
        back = c.ps("emb_back_ps", [P, TILES, P], st)
        genes = A["genes"]

        block = st.enter_context(nc.Block())

        @block.gpsimd
        def _(pool):
            constants(c, pool, s_zero, s_ident)

        @block.sync
        def _(sp):
            for s in range(SLOTS):
                sp.dma_start(ring[:, s, :], genes[s, :, :]).then_inc(s_load[s], 16)
            for half in range(2):
                sp.dma_start(bias[half * ROWS:(half + 1) * ROWS, :],
                             A["tok_bias"][:, half * EMB // 2:(half + 1) * EMB // 2].broadcast_to([ROWS, EMB // 2])
                             ).then_inc(s_bias, 16)
            with sp.Fori(1, GENE_TILES // SLOTS) as it:
                for s in range(SLOTS):
                    sp.wait_ge(s_used, it * SLOTS + (s + 1 - SLOTS))
                    sp.dma_start(ring[:, s, :], genes[bass.ds(it * SLOTS + s, 1), :, :].rearrange("a p n -> (a p) n")
                                 ).then_inc(s_load[s], 16)

        @block.vector
        def _(dve):
            with dve.Fori(0, GENE_TILES // SLOTS) as it:
                for s in range(SLOTS):
                    dve.wait_ge(s_load[s], it * 16 + 16)
                    w = ring[:, s, 0:EMB].rearrange("p (e f) -> p e f", f=P)
                    m = ring[:, s, EMB:EMB + P].unsqueeze(1).broadcast_to([GENE_P, PLACES, P])
                    nc.vector.tensor_tensor(w, w, m, ALU.mult).then_inc(s_masked, 1)
            dve.wait_ge(s_bias, 32)
            dve.wait_ge(s_used, GENE_TILES)
            nc.vector.tensor_tensor(summed[:, :, :].rearrange("p e f -> p (e f)"), acc[:, :], bias[:, :],
                                    ALU.add).then_inc(s_sum, 1)
            dve.wait_ge(s_swap, 1)
            nc.vector.tensor_copy(feat[:, :, :].rearrange("p b e -> p e b"), swap[:, :, :]).then_inc(s_swapped, 1)
            dve.wait_ge(s_back, 1)
            nc.vector.tensor_copy(c.H[:, :, :], back[:, :, :])

        @block.tensor
        def _(pe):
            def tile(s, first, last):
                for q in range(EMB // HALF // 2):
                    for half in range(2):
                        lo = half * EMB // 2 + q * HALF
                        ins = nc.tensor.matmul(acc[half * ROWS:(half + 1) * ROWS, q * HALF:(q + 1) * HALF],
                                               ring[:, s, EMB + P:EMB_ROW], ring[:, s, lo:lo + HALF],
                                               start=first, stop=last)
                ins.then_inc(s_used, 1)

            for s in range(SLOTS):
                pe.wait_ge(s_masked, s + 1)
                tile(s, s == 0, False)
            with pe.Fori(1, GENE_TILES // SLOTS - 1) as it:
                for s in range(SLOTS):
                    pe.wait_ge(s_masked, it * SLOTS + (s + 1))
                    tile(s, False, False)
            for s in range(SLOTS):
                pe.wait_ge(s_masked, GENE_TILES - SLOTS + s + 1)
                tile(s, False, s == SLOTS - 1)
            pe.wait_ge(s_sum, 1)
            pe.wait_ge(s_ident, 1)
            for e in range(PLACES):
                half, rows = e // (PLACES // 2), slice(e // (PLACES // 2) * ROWS, (e // (PLACES // 2) + 1) * ROWS)
                ins = nc.tensor.transpose(swap[:, e, :], summed[rows, e - half * PLACES // 2, :],
                                          c.ident[rows, rows])
            ins.then_inc(s_swap, 1)
            pe.wait_ge(s_swapped, 1)
            for i in range(TILES):
                ins = nc.tensor.transpose(back[:, i, :],
                                          feat[:, :, :].rearrange("p b e -> p (b e)")[:, i * P:(i + 1) * P],
                                          c.ident[:, :])
            ins.then_inc(s_back, 1)



def columns(widths):
    at, n = {}, 0
    for name, w in widths:
        at[name] = (n, n + w)
        n += w
    return at, n


def pack(np, widths, parts):
    at, n = columns(widths)
    out = np.zeros((P, n), np.float32)
    for name, w in widths:
        a = parts[name].reshape(-1, w)
        out[:a.shape[0], at[name][0]:at[name][1]] = a
    return out



HID, STATES, RANK = 256, 16, 64
HH = HID // P
PAD = PLACES + 2
SEG = PLACES + 1
RING = 4
MAMBA = [("w_in", HID), ("w1", HH * RANK), ("w2", HID), ("w_out", HH * P), ("conv", HH * 3), ("a", HH * STATES),
         ("d", HH), ("b2", HH), ("gamma", 1), ("beta", 1), ("b1", 1)]


def halves(np, a):
    return np.transpose(a.reshape(HH, P, -1), (1, 0, 2)).reshape(P, -1)


def lay_mamba(np, x, A):
    g = {k[len("L0_attn_"):]: v for k, v in x.items() if k.startswith("L0_attn_")}
    A["mamba"] = pack(np, MAMBA, {
        "w_in": g["W_in"].T, "w1": halves(np, g["dt_W1"].T), "w2": g["dt_W2"].T, "w_out": halves(np, g["W_out"].T),
        "conv": halves(np, g["conv_w"].reshape(HID, 3)), "a": halves(np, g["A"]), "d": halves(np, g["D"]),
        "b2": halves(np, g["dt_b2"]), "gamma": g["ln_gamma"], "beta": g["ln_beta"], "b1": g["dt_b1"]})


def mamba(c, A):
    nc = c.nc
    at, n_cols = columns(MAMBA)
    with ExitStack() as st:
        W = c.sb("mamba_w", [P, n_cols], st)

        def w(name, rows=P):
            return W[0:rows, at[name][0]:at[name][1]]

        n1, n2 = Norm(c, "mamba_n1", st), Norm(c, "mamba_n2", st)
        X1 = c.sb("mamba_x1", [P, TILES, P], st)
        X2 = c.sb("mamba_x2", [P, TILES, P], st)
        xnT = c.sb("mamba_xnT", [P, TOKENS], st)
        hpad = c.sb("mamba_hpad", [P, HH, ROWS, PAD], st)
        conv = c.sb("mamba_conv", [P, HH, ROWS, PLACES], st)
        hs = c.sb("mamba_hs", [P, HH, TOKENS], st)
        d1 = c.sb("mamba_d1", [RANK, TOKENS], st)
        z = c.sb("mamba_z", [P, HH, TOKENS], st)
        mag = c.sb("mamba_mag", [P, HH, TOKENS], st)
        dt = c.sb("mamba_dt", [P, HH, TOKENS], st)
        U = c.sb("mamba_u", [P, HH, ROWS, PAD], st)
        dU = c.sb("mamba_du", [P, HH, ROWS, SEG], st)
        Y = c.sb("mamba_y", [P, HH, ROWS, PLACES], st)
        dA = c.sb("mamba_dA", [P, RING, ROWS, SEG], st)
        S = c.sb("mamba_state", [P, RING, ROWS, SEG], st)
        WA = c.sb("mamba_wa", [P, HH, STATES, P], st)
        ea = c.sb("mamba_ea", [P, HH * STATES], st)
        aneg = c.sb("mamba_aneg", [P, HH * STATES], st)
        tiny = c.sb("mamba_tiny", [P, HH * STATES], st)
        safe = c.sb("mamba_safe", [P, HH * STATES], st)
        inv = c.sb("mamba_inv", [P, HH * STATES], st)
        coef = c.sb("mamba_coef", [P, HH, STATES], st)
        csum = c.sb("mamba_csum", [P, HH], st)
        outT = c.sb("mamba_outT", [P, TOKENS], st)
        psA = c.ps("mamba_psA", [P, TOKENS], st)
        psH = c.ps("mamba_psH", [P, HH, TOKENS], st)
        psO = c.ps("mamba_psO", [P, TOKENS], st)

        names = ("w", "x2", "xt", "xn", "h", "hcopy", "conv", "hs", "d1ps", "d1", "d2ps", "mag", "log", "dt", "expa",
                 "coef", "wa", "pads", "dA", "state", "used", "y", "outps", "outT", "back", "x1", "cord", "aord")
        s = {k: c.sem("mamba_" + k) for k in names}
        block = st.enter_context(nc.Block())

        @block.sync
        def _(sp):
            sp.dma_start(W[:, :], A["mamba"]).then_inc(s["w"], 16)

        @block.gpsimd
        def _(pool):
            nc.gpsimd.memset(hpad[:, :, :, :], 0.0).then_inc(s["pads"], 1)
            nc.gpsimd.memset(U[:, :, :, :], 0.0).then_inc(s["pads"], 1)
            nc.gpsimd.memset(dA[:, :, :, :], 0.0).then_inc(s["pads"], 1)
            n1.power(pool)
            n2.power(pool)
            pool.wait_ge(s["coef"], 1)
            for h in range(HH):
                wo = w("w_out")[:, h * P:(h + 1) * P].unsqueeze(1).broadcast_to([P, STATES, P])
                k = coef[:, h, :].unsqueeze(2).broadcast_to([P, STATES, P])
                nc.gpsimd.tensor_tensor(WA[:, h, :, :], wo, k, ALU.mult).then_inc(s["wa"], 1)

        @block.scalar
        def _(act):
            act.wait_ge(s["w"], 16)
            nc.scalar.activation(ea[:, :], w("a"), ACT.Exp).then_inc(s["expa"], 1)
            act.wait_ge(s["xt"], 1)
            nc.scalar.activation(xnT[:, :], psA[:, :], ACT.Identity, bias=w("beta"), scale=w("gamma")
                                 ).then_inc(s["xn"], 1)
            act.wait_ge(s["h"], 1)
            act.wait_ge(s["pads"], 1)
            for h in range(HH):
                nc.scalar.activation(hpad[:, h, :, 1:1 + PLACES],
                                     psH[:, h, :].rearrange("p (b l) -> p b l", l=PLACES), ACT.Copy
                                     ).then_inc(s["hcopy"], 1)
            for h in range(HH):
                act.wait_ge(s["conv"], h + 1)
                nc.scalar.activation(hs[:, h, :], conv[:, h, :, :].rearrange("p b l -> p (b l)"), ACT.Silu
                                     ).then_inc(s["hs"], 1)
            act.wait_ge(s["d1ps"], 1)
            nc.scalar.activation(d1[:, :], psA[0:RANK, :], ACT.Relu, bias=w("b1", RANK)).then_inc(s["d1"], 1)
            act.wait_ge(s["mag"], 1)
            nc.scalar.activation(mag[:, :, :], mag[:, :, :], ACT.Exp, scale=-1.0).then_inc(s["aord"], 1)
            act.wait_ge(s["aord"], 1)
            nc.scalar.activation(mag[:, :, :], mag[:, :, :], ACT.Ln, bias=1.0).then_inc(s["log"], 1)
            act.wait_ge(s["dt"], 1)
            act.wait_ge(s["pads"], 3)
            for k in range(HH * STATES):
                h, n = k % HH, k // HH
                if k >= RING:
                    act.wait_ge(s["state"], k - RING + 1)
                nc.scalar.activation(dA[:, k % RING, :, 1:SEG], dt[:, h, :].rearrange("p (b l) -> p b l", l=PLACES),
                                     ACT.Exp, scale=aneg[:, h * STATES + n:h * STATES + n + 1]).then_inc(s["dA"], 1)
            act.wait_ge(s["outps"], 1)
            nc.scalar.activation(outT[:, :], psO[:, :], ACT.Copy).then_inc(s["outT"], 1)

        @block.vector
        def _(dve):
            v = nc.vector
            o = Order(dve, s["cord"])
            n1.statistics(o, c.H)
            o.after(n1.apply(dve, X1, c.H))
            n2.statistics(o, X1)
            n2.apply(dve, X2, X1).then_inc(s["x2"], 1)
            o.after(v.tensor_tensor(c.H[:, :, :], c.H[:, :, :], X1[:, :, :], ALU.add))
            dve.wait_ge(s["expa"], 1)
            v.tensor_scalar_mul(aneg[:, :], ea[:, :], -1.0)
            o.after(v.tensor_scalar(tiny[:, :], ea[:, :], 1e-5, None, ALU.is_lt))
            o.after(v.tensor_scalar(safe[:, :], tiny[:, :], -1.0, 1.0, ALU.mult, ALU.add))
            o.after(v.tensor_tensor(safe[:, :], safe[:, :], aneg[:, :], ALU.mult))
            o.after(v.tensor_tensor(safe[:, :], safe[:, :], tiny[:, :], ALU.add))
            o.after(v.reciprocal(inv[:, :], safe[:, :]))
            o.after(v.tensor_tensor(coef[:, :, :].rearrange("p h n -> p (h n)"), inv[:, :], w("a"), ALU.mult))
            v.tensor_reduce(csum[:, :], coef[:, :, :], AX, ALU.add).then_inc(s["coef"], 1)
            for h in range(HH):
                k = w("conv")[:, 3 * h:3 * h + 3]
                dve.wait_ge(s["hcopy"], h + 1)
                o.after(v.tensor_scalar(conv[:, h, :, :], hpad[:, h, :, 1:1 + PLACES], k[:, 1:2], None, ALU.mult))
                o.after(v.scalar_tensor_tensor(conv[:, h, :, :], hpad[:, h, :, 0:PLACES], k[:, 0:1],
                                               conv[:, h, :, :], ALU.mult, ALU.add))
                v.scalar_tensor_tensor(conv[:, h, :, :], hpad[:, h, :, 2:PAD], k[:, 2:3], conv[:, h, :, :],
                                       ALU.mult, ALU.add).then_inc(s["conv"], 1)
            dve.wait_ge(s["d2ps"], 1)
            for h in range(HH):
                last = v.tensor_scalar(z[:, h, :], psH[:, h, :], w("b2")[:, h:h + 1], None, ALU.add)
            o.after(last)
            v.scalar_tensor_tensor(mag[:, :, :], z[:, :, :], -1.0, z[:, :, :], ALU.mult, ALU.max).then_inc(s["mag"], 1)
            dve.wait_ge(s["log"], 1)
            o.after(v.scalar_tensor_tensor(dt[:, :, :], z[:, :, :], 0.0, mag[:, :, :], ALU.max, ALU.add))
            dve.wait_ge(s["pads"], 2)
            for h in range(HH):
                last = v.tensor_tensor(U[:, h, :, 1:1 + PLACES], dt[:, h, :].rearrange("p (b l) -> p b l", l=PLACES),
                                       hs[:, h, :].rearrange("p (b l) -> p b l", l=PLACES), ALU.mult)
            last.then_inc(s["dt"], 1)
            dve.wait_ge(s["dt"], 1)
            for h in range(HH):
                last = v.tensor_tensor(dU[:, h, :, :], U[:, h, :, 1:PAD], U[:, h, :, 0:SEG], ALU.subtract)
            o.after(last)
            for k in range(HH * STATES):
                h = k % HH
                dve.wait_ge(s["dA"], k + 1)
                if k >= RING:
                    dve.wait_ge(s["used"], k - RING + 1)
                v.tensor_tensor_scan(S[:, k % RING, :, :].rearrange("p b l -> p (b l)"),
                                     dA[:, k % RING, :, :].rearrange("p b l -> p (b l)"),
                                     dU[:, h, :, :].rearrange("p b l -> p (b l)"), 0.0, ALU.mult, ALU.add
                                     ).then_inc(s["state"], 1)
            for h in range(HH):
                last = v.tensor_scalar(Y[:, h, :, :], U[:, h, :, 2:PAD], csum[:, h:h + 1], -1.0, ALU.mult, ALU.mult)
            o.after(last)
            for h in range(HH):
                last = v.scalar_tensor_tensor(Y[:, h, :, :].rearrange("p b l -> p (b l)"), hs[:, h, :],
                                              w("d")[:, h:h + 1], Y[:, h, :, :].rearrange("p b l -> p (b l)"),
                                              ALU.mult, ALU.add)
            last.then_inc(s["y"], 1)
            dve.wait_ge(s["back"], 1)
            v.tensor_tensor(c.H[:, :, :], c.H[:, :, :], psA[:, :].rearrange("p (i d) -> p i d", d=P), ALU.add)

        @block.tensor
        def _(pe):
            mm = nc.tensor.matmul
            pe.wait_ge(s["x2"], 1)
            transpose_tokens(c, psA, X2).then_inc(s["xt"], 1)
            pe.wait_ge(s["xn"], 1)
            for h in range(HH):
                for q in range(2):
                    ins = mm(psH[:, h, q * HALF:(q + 1) * HALF], w("w_in")[:, h * P:(h + 1) * P],
                             xnT[:, q * HALF:(q + 1) * HALF], start=True, stop=True)
            ins.then_inc(s["h"], 1)
            pe.wait_ge(s["hs"], HH)
            for q in range(2):
                for h in range(HH):
                    ins = mm(psA[0:RANK, q * HALF:(q + 1) * HALF], w("w1")[:, h * RANK:(h + 1) * RANK],
                             hs[:, h, q * HALF:(q + 1) * HALF], start=h == 0, stop=h == HH - 1)
            ins.then_inc(s["d1ps"], 1)
            pe.wait_ge(s["d1"], 1)
            for h in range(HH):
                for q in range(2):
                    ins = mm(psH[:, h, q * HALF:(q + 1) * HALF], w("w2", RANK)[:, h * P:(h + 1) * P],
                             d1[:, q * HALF:(q + 1) * HALF], start=True, stop=True)
            ins.then_inc(s["d2ps"], 1)
            pe.wait_ge(s["wa"], HH)
            for k in range(HH * STATES):
                h, n = k % HH, k // HH
                pe.wait_ge(s["state"], k + 1)
                for q in range(2):
                    ins = mm(psO[:, q * HALF:(q + 1) * HALF], WA[:, h, n, :],
                             S[:, k % RING, q * ROWS // 2:(q + 1) * ROWS // 2, 1:SEG], start=k == 0, stop=False)
                ins.then_inc(s["used"], 1)
            pe.wait_ge(s["y"], 1)
            for h in range(HH):
                for q in range(2):
                    ins = mm(psO[:, q * HALF:(q + 1) * HALF], w("w_out")[:, h * P:(h + 1) * P],
                             Y[:, h, q * ROWS // 2:(q + 1) * ROWS // 2, :], start=False, stop=h == HH - 1)
            ins.then_inc(s["outps"], 1)
            pe.wait_ge(s["outT"], 1)
            for i in range(TILES):
                ins = nc.tensor.transpose(psA[:, i * P:(i + 1) * P], outT[:, i * P:(i + 1) * P], c.ident[:, :])
            ins.then_inc(s["back"], 1)



SWITCH, BINS = 16, (-1.5, -1.0, -0.5, 0.0, 0.5, 1.0, 1.5)
CAPACITY = int(1.2 * TOKENS / SWITCH)
PER_BANK = HALF // P
BANKS = 4
SWITCH_COLS = [("w", SWITCH * P), ("gate", SWITCH), ("gate_b", SWITCH), ("rank", SWITCH), ("tri", P), ("ones", P),
               ("bias", P)]
BINNED_COLS = [("w", (len(BINS) + 1) * P)]


def lay_switch(np, x, A):
    A["switch"] = pack(np, SWITCH_COLS, {
        "w": np.transpose(x["L0_ffn_expert_w"], (2, 0, 1)).reshape(P, SWITCH * P), "gate": x["L0_ffn_switch_w"].T,
        "gate_b": np.tile(x["L0_ffn_switch_b"], (P, 1)),
        "rank": np.tile(np.arange(SWITCH, 0, -1, dtype=np.float32), (P, 1)),
        "tri": np.triu(np.ones((P, P), np.float32)), "ones": np.ones((P, P), np.float32),
        "bias": x["L0_ffn_expert_b"]})


def lay_binned(np, x, A):
    A["binned"] = np.transpose(x["L2_ffn_W"], (1, 0, 2)).reshape(P, (len(BINS) + 1) * P)


def picked_experts(c, name, W_dram, cols, n_exp, routed):
    nc = c.nc
    at, n_cols = columns(cols)
    groups = n_exp // PER_BANK
    with ExitStack() as st:
        W = c.sb(name + "_w", [P, n_cols], st)

        def w(part, rows=P):
            return W[0:rows, at[part][0]:at[part][1]]

        norm = Norm(c, name + "_n", st)
        X = c.sb(name + "_x", [P, TILES, P], st)
        XT = c.sb(name + "_xT", [P, TOKENS], st)
        K = c.sb(name + "_k", [P, TILES, n_exp], st)
        acc = c.sb(name + "_acc", [P, TILES, HALF], st)
        prod = c.sb(name + "_prod", [P, BANKS, HALF], st)
        psT = c.ps(name + "_psT", [P, TOKENS], st)
        psE = c.ps(name + "_psE", [P, BANKS, HALF], st)
        psL = c.ps(name + "_psL", [P, TILES, n_exp], st)
        psC = c.ps(name + "_psC", [P, TILES, n_exp], st)
        s = {k: c.sem(f"{name}_{k}") for k in ("w", "x", "xps", "xT", "out", "taken", "ord", "ones", "even", "odd",
                                               "folded")}
        if routed:
            s.update({k: c.sem(f"{name}_{k}") for k in ("logit", "shift", "exp", "hot", "count", "k", "kps", "kT",
                                                        "bias")})
            L, E, hot, score, before = (c.sb(f"{name}_{k}", [P, TILES, n_exp], st)
                                        for k in ("l", "e", "hot", "score", "before"))
            top, total, prob, rest = (c.sb(f"{name}_{k}", [P, TILES], st) for k in ("top", "total", "prob", "rest"))
            KT = c.sb(name + "_kT", [n_exp, TOKENS], st)
        else:
            above = c.sb(name + "_above", [P, TILES, n_exp + 1], st)
        block = st.enter_context(nc.Block())

        def add(engine, ops, parity, g, i):
            m, n = g * TILES + i, (g - 1) * TILES // 2 + i // 2
            mine = s["odd" if parity else "even"]
            engine.wait_ge(s["taken"], m + 1)
            if g >= 2:
                engine.wait_ge(mine, n + 1 - TILES // 2)
            ops.tensor_tensor(acc[:, i, :], acc[:, i, :], prod[:, m % BANKS, :], ALU.add).then_inc(mine, 1)

        def fold(engine, ops, parity):
            mine, n = s["odd" if parity else "even"], (groups - 1) * TILES // 2
            a = acc[:, :, :].rearrange("p (t q) n -> p t q n", q=2)[:, :, parity, :]
            hh = c.H[:, :, :].rearrange("p (t q) d -> p t q d", q=2)[:, :, parity, :]
            engine.wait_ge(mine, n)
            ops.tensor_tensor(a[:, :, 0:2 * P], a[:, :, 0:2 * P], a[:, :, 2 * P:], ALU.add).then_inc(mine, 1)
            engine.wait_ge(mine, n + 1)
            ops.tensor_tensor(a[:, :, 0:P], a[:, :, 0:P], a[:, :, P:2 * P], ALU.add).then_inc(mine, 1)
            engine.wait_ge(mine, n + 2)
            ops.tensor_tensor(hh, hh, a[:, :, 0:P], ALU.add).then_inc(s["folded"], 1)

        @block.sync
        def _(sp):
            sp.dma_start(W[:, :], W_dram).then_inc(s["w"], 16)

        @block.gpsimd
        def _(pool):
            if not routed:
                nc.gpsimd.memset(above[:, :, 0:1], 1.0).then_inc(s["ones"], 1)
                nc.gpsimd.memset(above[:, :, n_exp:n_exp + 1], 0.0).then_inc(s["ones"], 1)
            norm.power(pool)
            for g in range(1, groups):
                for i in range(0, TILES, 2):
                    add(pool, nc.gpsimd, 0, g, i)
            fold(pool, nc.gpsimd, 0)

        @block.scalar
        def _(act):
            act.wait_ge(s["xps"], 1)
            nc.scalar.activation(XT[:, :], psT[:, :], ACT.Copy).then_inc(s["xT"], 1)
            if routed:
                act.wait_ge(s["shift"], 1)
                nc.scalar.activation(E[:, :, :], L[:, :, :], ACT.Exp).then_inc(s["exp"], 1)
                act.wait_ge(s["kps"], 1)
                nc.scalar.activation(KT[:, :], psT[0:n_exp, :], ACT.Copy).then_inc(s["kT"], 1)

        @block.vector
        def _(dve):
            v = nc.vector
            o = Order(dve, s["ord"])
            norm.statistics(o, c.H)
            norm.apply(dve, X, c.H).then_inc(s["x"], 1)
            if routed:
                dve.wait_ge(s["w"], 16)
                dve.wait_ge(s["logit"], 1)
                o.after(v.tensor_tensor(L[:, :, :], psL[:, :, :],
                                        w("gate_b").unsqueeze(1).broadcast_to([P, TILES, n_exp]), ALU.add))
                o.after(v.tensor_reduce(top[:, :], L[:, :, :], AX, ALU.max))
                tops = top[:, :].unsqueeze(2).broadcast_to([P, TILES, n_exp])
                v.tensor_tensor(score[:, :, :], L[:, :, :], tops, ALU.is_equal)
                o.after(v.tensor_tensor(L[:, :, :], L[:, :, :], tops, ALU.subtract))
                v.tensor_tensor(score[:, :, :], score[:, :, :],
                                w("rank").unsqueeze(1).broadcast_to([P, TILES, n_exp]), ALU.mult
                                ).then_inc(s["shift"], 1)
                dve.wait_ge(s["shift"], 1)
                o.after(v.tensor_reduce(top[:, :], score[:, :, :], AX, ALU.max))
                o.after(v.tensor_tensor(hot[:, :, :], score[:, :, :],
                                        top[:, :].unsqueeze(2).broadcast_to([P, TILES, n_exp]), ALU.is_equal))
                o.after(v.memset(before[:, 0, :], 0.0))
                for i in range(1, TILES):
                    ins = v.tensor_tensor(before[:, i, :], before[:, i - 1, :], hot[:, i - 1, :], ALU.add)
                    if i < TILES - 1:
                        o.after(ins)
                ins.then_inc(s["hot"], 1)
                dve.wait_ge(s["exp"], 1)
                o.after(v.tensor_reduce(total[:, :], E[:, :, :], AX, ALU.add))
                o.after(v.reciprocal(prob[:, :], total[:, :]))
                dve.wait_ge(s["count"], 1)
                o.after(v.scalar_tensor_tensor(K[:, :, :].rearrange("p i e -> p (i e)"),
                                               psC[:, :, :].rearrange("p i e -> p (i e)"), float(CAPACITY),
                                               hot[:, :, :].rearrange("p i e -> p (i e)"), ALU.is_le, ALU.mult))
                o.after(v.tensor_tensor(K[:, :, :], K[:, :, :],
                                        prob[:, :].unsqueeze(2).broadcast_to([P, TILES, n_exp]), ALU.mult))
                v.tensor_reduce(total[:, :], K[:, :, :], AX, ALU.add).then_inc(s["k"], 1)
                dve.wait_ge(s["k"], 1)
                o.after(v.tensor_tensor(rest[:, :], prob[:, :], total[:, :], ALU.subtract))
                for i in range(TILES):
                    ins = v.scalar_tensor_tensor(c.H[:, i, :], X[:, i, :], rest[:, i:i + 1], c.H[:, i, :],
                                                 ALU.mult, ALU.add)
                o.after(ins)
            else:
                dve.wait_ge(s["x"], 1)
                dve.wait_ge(s["ones"], 2)
                for n, edge in enumerate(BINS):
                    ins = v.tensor_scalar(above[:, :, n + 1:n + 2], X[:, :, 0:1], edge, None, ALU.is_gt)
                o.after(ins)
                o.after(v.tensor_tensor(K[:, :, :], above[:, :, 0:n_exp], above[:, :, 1:n_exp + 1], ALU.subtract))
            for m in range(groups * TILES):
                g, i = m // TILES, m % TILES
                dve.wait_ge(s["out"], m + 1)
                if g > 0 and i % 2 == 0 and (g > 1 or i >= BANKS):
                    dve.wait_ge(s["even"], (g - 1) * TILES // 2 + (i - BANKS) // 2 + 1)
                v.tensor_tensor((acc[:, i, :] if g == 0 else prod[:, m % BANKS, :]).rearrange("p (e d) -> p e d", d=P),
                                psE[:, m % BANKS, :].rearrange("p (e d) -> p e d", d=P),
                                K[:, i, g * PER_BANK:(g + 1) * PER_BANK].unsqueeze(2)
                                .broadcast_to([P, PER_BANK, P]), ALU.mult).then_inc(s["taken"], 1)
                if g > 0 and i % 2 == 1:
                    add(dve, v, 1, g, i)
            fold(dve, v, 1)
            if routed:
                dve.wait_ge(s["bias"], 1)
                dve.wait_ge(s["folded"], 2)
                v.tensor_tensor(c.H[:, :, :], c.H[:, :, :], psT[:, :].rearrange("p (i d) -> p i d", d=P), ALU.add)

        @block.tensor
        def _(pe):
            mm = nc.tensor.matmul

            def expert_bank(m):
                g, i = m // TILES, m % TILES
                if m >= BANKS:
                    pe.wait_ge(s["taken"], m - BANKS + 1)
                mm(psE[:, m % BANKS, :], XT[:, i * P:(i + 1) * P],
                   W[:, at["w"][0] + g * HALF:at["w"][0] + (g + 1) * HALF], start=True, stop=True
                   ).then_inc(s["out"], 1)

            pe.wait_ge(s["x"], 1)
            transpose_tokens(c, psT, X).then_inc(s["xps"], 1)
            pe.wait_ge(s["w"], 16)
            pe.wait_ge(s["xT"], 1)
            if routed:
                for i in range(TILES):
                    ins = mm(psL[:, i, :], XT[:, i * P:(i + 1) * P], w("gate"), start=True, stop=True)
                ins.then_inc(s["logit"], 1)
            for m in range(BANKS):
                expert_bank(m)
            if routed:
                pe.wait_ge(s["hot"], 1)
                mm(psC[:, :, :], w("tri"), hot[:, :, :], start=True, stop=False)
                mm(psC[:, :, :], w("ones"), before[:, :, :], start=False, stop=True).then_inc(s["count"], 1)
                pe.wait_ge(s["k"], 1)
                for i in range(TILES):
                    ins = nc.tensor.transpose(psT[0:n_exp, i * P:(i + 1) * P], K[:, i, :], c.ident[:, :])
                ins.then_inc(s["kps"], 1)
                pe.wait_ge(s["kT"], 1)
                for i in range(TILES):
                    ins = mm(psT[:, i * P:(i + 1) * P], KT[:, i * P:(i + 1) * P], w("bias", n_exp),
                             start=True, stop=True)
                ins.then_inc(s["bias"], 1)
            for m in range(BANKS, groups * TILES):
                expert_bank(m)


def switch_experts(c, A):
    picked_experts(c, "switch", A["switch"], SWITCH_COLS, SWITCH, True)


def binned_experts(c, A):
    picked_experts(c, "binned", A["binned"], BINNED_COLS, len(BINS) + 1, False)



LHEADS, LDIM = 8, 16
HEAD_SLOT = 32
LGROUPS = LHEADS * HEAD_SLOT // P
PER_GROUP = LHEADS // LGROUPS
LINEAR_UNITS = 3 * LGROUPS
LINEAR_COLS = [("qkn", LINEAR_UNITS * P), ("qkn_b", LINEAR_UNITS), ("v", LGROUPS * P), ("v_b", LGROUPS * P),
               ("mask", P), ("out", LGROUPS * P), ("out_b", P)]


def row_mask(np):
    t = np.arange(P)
    return ((t[:, None] // PLACES == t[None, :] // PLACES) & (t[:, None] <= t[None, :])).astype(np.float32)


def lay_linear(np, x, A):
    w, b = x["L2_attn_Wvqkn_w"], x["L2_attn_Wvqkn_b"]

    def slots(a):
        out = np.zeros((LHEADS, HEAD_SLOT, a.shape[1]), np.float32)
        out[:, :LDIM] = a.reshape(LHEADS, LDIM, -1)
        return out.reshape(LHEADS * HEAD_SLOT, -1)

    def slotted(a, part):
        return slots(a[part * P:(part + 1) * P].reshape(P, -1))

    qkn_w = np.concatenate([slotted(w, 1), slotted(w, 2), np.repeat(w[3 * P:], HEAD_SLOT, axis=0)])
    qkn_b = np.concatenate([slotted(b, 1)[:, 0], slotted(b, 2)[:, 0], np.repeat(b[3 * P:], HEAD_SLOT)])
    A["linear"] = pack(np, LINEAR_COLS, {
        "qkn": qkn_w.T, "qkn_b": qkn_b.reshape(LINEAR_UNITS, P).T, "v": slotted(w, 0).T,
        "v_b": np.tile(slotted(b, 0)[:, 0], (P, 1)), "mask": row_mask(np),
        "out": np.transpose(slots(x["L2_attn_out_w"].T).reshape(LGROUPS, P, P), (1, 0, 2)).reshape(P, LGROUPS * P),
        "out_b": np.tile(x["L2_attn_out_b"], (P, 1))})


def linear_attention(c, A):
    nc = c.nc
    at, n_cols = columns(LINEAR_COLS)
    with ExitStack() as st:
        W = c.sb("linear_w", [P, n_cols], st)

        def w(part):
            return W[:, at[part][0]:at[part][1]]

        norm = Norm(c, "linear_n", st)
        X = c.sb("linear_x", [P, TILES, P], st)
        XT = c.sb("linear_xT", [P, TOKENS], st)
        QK = c.sb("linear_qk", [P, 2 * LGROUPS, TOKENS], st)
        V = c.sb("linear_v", [P, TILES, LGROUPS * P], st)
        gate = c.sb("linear_gate", [P, LGROUPS, TOKENS], st)
        S = c.sb("linear_s", [P, 2, PER_GROUP, LGROUPS, P], st)
        ctx = c.sb("linear_ctx", [P, LGROUPS, TOKENS], st)
        psT = c.ps("linear_psT", [P, TOKENS], st)
        psS = c.ps("linear_psS", [P, PER_GROUP, HALF], st)
        psV = c.ps("linear_psV", [P, 2, HALF], st)
        names = ("w", "x", "xps", "xT", "qkps", "qk", "vps", "v", "gate", "sps", "s", "ops", "ctx", "out",
                 "ord")
        s = {k: c.sem("linear_" + k) for k in names}
        block = st.enter_context(nc.Block())

        @block.sync
        def _(sp):
            sp.dma_start(W[:, :], A["linear"]).then_inc(s["w"], 16)

        @block.gpsimd
        def _(pool):
            norm.power(pool)

        @block.scalar
        def _(act):
            act.wait_ge(s["xps"], 1)
            nc.scalar.activation(XT[:, :], psT[:, :], ACT.Copy).then_inc(s["xT"], 1)
            for u in range(LINEAR_UNITS):
                act.wait_ge(s["qkps"], u + 1)
                gated = u >= 2 * LGROUPS
                nc.scalar.activation(gate[:, u - 2 * LGROUPS, :] if gated else QK[:, u, :],
                                     psS[:, 2 * (u % 2):2 * (u % 2) + 2, :], ACT.Exp if gated else ACT.Identity,
                                     bias=w("qkn_b")[:, u:u + 1]).then_inc(s["qk"], 1)
            act.wait_ge(s["qk"], LINEAR_UNITS)
            nc.scalar.activation(gate[:, :, :], gate[:, :, :], ACT.Exp, scale=-1.0).then_inc(s["gate"], 1)

        @block.vector
        def _(dve):
            v = nc.vector
            o = Order(dve, s["ord"])
            norm.statistics(o, c.H)
            norm.apply(dve, X, c.H).then_inc(s["x"], 1)
            dve.wait_ge(s["w"], 16)
            for i in range(TILES):
                dve.wait_ge(s["vps"], i + 1)
                v.tensor_tensor(V[:, i, :], psV[:, i % 2, 0:LGROUPS * P], w("v_b"), ALU.add).then_inc(s["v"], 1)
            mask = w("mask").unsqueeze(1).unsqueeze(1).broadcast_to([P, PER_GROUP, LGROUPS, P])

            def context(i):
                dve.wait_ge(s["ops"], i + 1)
                if i == 0:
                    dve.wait_ge(s["gate"], 1)
                v.tensor_tensor(ctx[:, :, i * P:(i + 1) * P],
                                psV[:, i % 2, 0:LGROUPS * P].rearrange("p (a t) -> p a t", t=P),
                                gate[:, :, i * P:(i + 1) * P], ALU.mult).then_inc(s["ctx"], 1)

            for i in range(TILES):
                dve.wait_ge(s["sps"], i + 1)
                v.tensor_tensor(S[:, i % 2, :, :, :],
                                psS[:, :, 0:LGROUPS * P].rearrange("p j (a t) -> p j a t", t=P), mask, ALU.mult
                                ).then_inc(s["s"], 1)
                if i >= 1:
                    context(i - 1)
            context(TILES - 1)
            o.after(v.tensor_tensor(c.H[:, :, :], c.H[:, :, :],
                                    w("out_b").unsqueeze(1).broadcast_to([P, TILES, P]), ALU.add))
            dve.wait_ge(s["out"], 1)
            v.tensor_tensor(c.H[:, :, :], c.H[:, :, :],
                            psS[:, 0:2, :].rearrange("p a (i d) -> p (a i) d", d=P), ALU.add)

        @block.tensor
        def _(pe):
            mm = nc.tensor.matmul
            pe.wait_ge(s["x"], 1)
            transpose_tokens(c, psT, X).then_inc(s["xps"], 1)
            pe.wait_ge(s["w"], 16)
            pe.wait_ge(s["xT"], 1)
            for u in range(LINEAR_UNITS):
                if u >= 2:
                    pe.wait_ge(s["qk"], u - 1)
                for q in range(2):
                    ins = mm(psS[:, 2 * (u % 2) + q, :], w("qkn")[:, u * P:(u + 1) * P],
                             XT[:, q * HALF:(q + 1) * HALF], start=True, stop=True)
                ins.then_inc(s["qkps"], 1)
            for i in range(TILES):
                if i >= 2:
                    pe.wait_ge(s["v"], i - 1)
                mm(psV[:, i % 2, 0:LGROUPS * P], XT[:, i * P:(i + 1) * P], w("v"), start=True, stop=True
                   ).then_inc(s["vps"], 1)
            pe.wait_ge(s["qk"], LINEAR_UNITS)

            def values(i):
                if i < 2:
                    pe.wait_ge(s["v"], TILES)
                else:
                    pe.wait_ge(s["ctx"], i - 1)
                pe.wait_ge(s["s"], i + 1)
                for a in range(LGROUPS):
                    for j in range(PER_GROUP):
                        h = a * PER_GROUP + j
                        ins = mm(psV[j * HEAD_SLOT:(j + 1) * HEAD_SLOT, i % 2, a * P:(a + 1) * P],
                                 V[:, i, h * HEAD_SLOT:(h + 1) * HEAD_SLOT], S[:, i % 2, j, a, :],
                                 start=True, stop=True)
                ins.then_inc(s["ops"], 1)

            for i in range(TILES):
                if i >= 1:
                    pe.wait_ge(s["s"], i)
                for a in range(LGROUPS):
                    for j in range(PER_GROUP):
                        rows = slice(j * HEAD_SLOT, (j + 1) * HEAD_SLOT)
                        ins = mm(psS[:, j, a * P:(a + 1) * P], QK[rows, LGROUPS + a, i * P:(i + 1) * P],
                                 QK[rows, a, i * P:(i + 1) * P], start=True, stop=True)
                ins.then_inc(s["sps"], 1)
                if i >= 1:
                    values(i - 1)
            values(TILES - 1)
            pe.wait_ge(s["ctx"], TILES)
            for i in range(TILES):
                for a in range(LGROUPS):
                    ins = mm(psS[:, i // 4, (i % 4) * P:(i % 4 + 1) * P], ctx[:, a, i * P:(i + 1) * P],
                             w("out")[:, a * P:(a + 1) * P], start=a == 0, stop=a == LGROUPS - 1)
            ins.then_inc(s["out"], 1)



CHEADS, CDIM = 8, 64
CPAIRS = CHEADS // 2
CAUSAL_COLS = [("q", CHEADS * CDIM), ("k", CHEADS * CDIM), ("v", CHEADS * CDIM), ("o", CPAIRS * P), ("mask", P)]
MASKED = -1e30


def lay_causal(np, x, A):
    def heads(a):
        return np.transpose(a, (1, 0, 2)).reshape(P, CHEADS * CDIM)
    A["causal"] = pack(np, CAUSAL_COLS, {
        "q": heads(x["L3_attn_W_q"]), "k": heads(x["L3_attn_W_k"]), "v": heads(x["L3_attn_W_v"]),
        "o": np.transpose(x["L3_attn_W_o"].reshape(CPAIRS, P, P), (1, 0, 2)).reshape(P, CPAIRS * P),
        "mask": np.where(row_mask(np).T > 0, 0, MASKED).astype(np.float32)})


def causal_attention(c, A):
    nc = c.nc
    at, n_cols = columns(CAUSAL_COLS)
    qk_units = 2 * CPAIRS * 2
    proj = qk_units + TILES
    with ExitStack() as st:
        W = c.sb("causal_w", [P, n_cols], st)

        def w(part):
            return W[:, at[part][0]:at[part][1]]

        norm = Norm(c, "causal_n", st)
        X = c.sb("causal_x", [P, TILES, P], st)
        XT = c.sb("causal_xT", [P, TOKENS], st)
        QK = c.sb("causal_qk", [P, 2, CPAIRS, TOKENS], st)
        V = c.sb("causal_v", [P, TILES, CHEADS * CDIM], st)
        L = c.sb("causal_l", [P, 2, CHEADS, P], st)
        pr = c.sb("causal_p", [P, 2, CHEADS, P], st)
        prT = c.sb("causal_pT", [P, 2, CHEADS, P], st)
        top = c.sb("causal_top", [P, 2, CHEADS], st)
        total = c.sb("causal_total", [P, 2, CHEADS], st)
        inv = c.sb("causal_inv", [P, 2, CHEADS], st)
        vals = c.sb("causal_vals", [P, 2, CPAIRS, P], st)
        psT = c.ps("causal_psT", [P, TOKENS], st)
        psS = c.ps("causal_psS", [P, 4, HALF], st)
        psO = c.ps("causal_psO", [P, CPAIRS, P], st)
        psF = c.ps("causal_psF", [P, HALF], st)
        names = ("w", "x", "xps", "xT", "pps", "pact", "pdve", "sps", "masked", "top", "exp", "inv", "norm", "tps",
                 "pT", "vps", "vals", "out", "added", "ord")
        s = {k: c.sem("causal_" + k) for k in names}
        block = st.enter_context(nc.Block())

        def projected(u):
            if u < qk_units:
                return QK[:, u // (2 * CPAIRS), u // 2 % CPAIRS, u % 2 * HALF:(u % 2 + 1) * HALF]
            return V[:, u - qk_units, :]

        def slots(**parts):
            for t in range(TILES + 3):
                for part, delay in parts.values():
                    if 0 <= t - delay < TILES:
                        part(t - delay)

        @block.sync
        def _(sp):
            sp.dma_start(W[:, :], A["causal"]).then_inc(s["w"], 16)

        @block.gpsimd
        def _(pool):
            norm.power(pool)
            for i in range(TILES):
                pool.wait_ge(s["inv"], i + 1)
                nc.gpsimd.tensor_tensor(pr[:, i % 2, :, :], pr[:, i % 2, :, :],
                                        inv[:, i % 2, :].unsqueeze(2).broadcast_to([P, CHEADS, P]), ALU.mult
                                        ).then_inc(s["norm"], 1)

        @block.scalar
        def _(act):
            act.wait_ge(s["xps"], 1)
            nc.scalar.activation(XT[:, :], psT[:, :], ACT.Copy).then_inc(s["xT"], 1)
            for u in range(0, proj, 2):
                act.wait_ge(s["pps"], u + 1)
                nc.scalar.activation(projected(u), psS[:, u % 4, :], ACT.Copy).then_inc(s["pact"], 1)

            def transposed(i):
                act.wait_ge(s["tps"], i + 1)
                if i >= 2:
                    act.wait_ge(s["vps"], i - 1)
                nc.scalar.activation(prT[:, i % 2, :, :].rearrange("p h t -> p (h t)"), psT[:, :], ACT.Copy
                                     ).then_inc(s["pT"], 1)

            def exponentials(i):
                act.wait_ge(s["top"], i + 1)
                if i >= 2:
                    act.wait_ge(s["tps"], i - 1)
                    act.wait_ge(s["inv"], i - 1)
                for h in range(CHEADS):
                    ins = nc.scalar.activation(pr[:, i % 2, h, :], L[:, i % 2, h, :], ACT.Exp,
                                               bias=top[:, i % 2, h:h + 1], accum_out=total[:, i % 2, h:h + 1])
                ins.then_inc(s["exp"], 1)

            slots(exponentials=(exponentials, 1), transposed=(transposed, 2))

        @block.vector
        def _(dve):
            v = nc.vector
            o = Order(dve, s["ord"])
            norm.statistics(o, c.H)
            norm.apply(dve, X, c.H).then_inc(s["x"], 1)
            for u in range(1, proj, 2):
                dve.wait_ge(s["pps"], u + 1)
                v.tensor_copy(projected(u), psS[:, u % 4, :]).then_inc(s["pdve"], 1)
            dve.wait_ge(s["w"], 16)
            mask = w("mask").unsqueeze(1).broadcast_to([P, CHEADS, P])

            def values(i):
                dve.wait_ge(s["vps"], i + 1)
                if i >= 2:
                    dve.wait_ge(s["out"], i - 1)
                v.tensor_copy(vals[:, i % 2, :, :], psO[:, :, :]).then_inc(s["vals"], 1)

            def add(i):
                dve.wait_ge(s["out"], i + 1)
                v.tensor_tensor(c.H[:, i, :], c.H[:, i, :], psF[:, 0:P], ALU.add).then_inc(s["added"], 1)

            def mask_scores(i):
                dve.wait_ge(s["sps"], i + 1)
                if i >= 2:
                    dve.wait_ge(s["exp"], i - 1)
                v.scalar_tensor_tensor(L[:, i % 2, :, :],
                                       psS[:, 2 * (i % 2):2 * (i % 2) + 2, :].rearrange("p a (b t) -> p (a b) t", t=P),
                                       float(CDIM) ** -0.5, mask, ALU.mult, ALU.add).then_inc(s["masked"], 1)
                dve.wait_ge(s["masked"], i + 1)
                v.tensor_reduce(top[:, i % 2, :], L[:, i % 2, :, :], AX, ALU.max, negate=True).then_inc(s["top"], 1)

            def invert(i):
                dve.wait_ge(s["exp"], i + 1)
                if i >= 2:
                    dve.wait_ge(s["norm"], i - 1)
                v.reciprocal(inv[:, i % 2, :], total[:, i % 2, :]).then_inc(s["inv"], 1)

            slots(values=(values, 3), mask_scores=(mask_scores, 0), add=(add, 3), invert=(invert, 1))

        @block.tensor
        def _(pe):
            mm = nc.tensor.matmul
            pe.wait_ge(s["x"], 1)
            transpose_tokens(c, psT, X).then_inc(s["xps"], 1)
            pe.wait_ge(s["w"], 16)
            pe.wait_ge(s["xT"], 1)

            def bank_free(u):
                prev = u - 4
                if prev >= 0:
                    pe.wait_ge(s["pact"] if prev % 2 == 0 else s["pdve"], prev // 2 + 1)

            for u in range(proj):
                bank_free(u)
                if u < qk_units:
                    part, pair, q = u // (2 * CPAIRS), u // 2 % CPAIRS, u % 2
                    ins = mm(psS[:, u % 4, :], w("qk"[part])[:, pair * P:(pair + 1) * P],
                             XT[:, q * HALF:(q + 1) * HALF], start=True, stop=True)
                else:
                    i = u - qk_units
                    ins = mm(psS[:, u % 4, :], XT[:, i * P:(i + 1) * P], w("v"), start=True, stop=True)
                ins.then_inc(s["pps"], 1)
            pe.wait_ge(s["pact"], proj // 2)
            pe.wait_ge(s["pdve"], proj // 2)

            def scores(i):
                if i >= 2:
                    pe.wait_ge(s["masked"], i - 1)
                for pair in range(CPAIRS):
                    for r in range(2):
                        rows = slice(r * CDIM, (r + 1) * CDIM)
                        ins = mm(psS[:, 2 * (i % 2) + r, pair * P:(pair + 1) * P],
                                 QK[rows, 0, pair, i * P:(i + 1) * P], QK[rows, 1, pair, i * P:(i + 1) * P],
                                 start=True, stop=True)
                ins.then_inc(s["sps"], 1)

            def turn(i):
                pe.wait_ge(s["norm"], i + 1)
                if i >= 1:
                    pe.wait_ge(s["pT"], i)
                for h in range(CHEADS):
                    ins = nc.tensor.transpose(psT[:, h * P:(h + 1) * P], pr[:, i % 2, h, :], c.ident[:, :])
                ins.then_inc(s["tps"], 1)

            def values(i):
                pe.wait_ge(s["pT"], i + 1)
                if i >= 1:
                    pe.wait_ge(s["vals"], i)
                for pair in range(CPAIRS):
                    for r in range(2):
                        ins = mm(psO[r * CDIM:(r + 1) * CDIM, pair, :],
                                 V[:, i, (2 * pair + r) * CDIM:(2 * pair + r + 1) * CDIM],
                                 prT[:, i % 2, r * CPAIRS + pair, :], start=True, stop=True)
                ins.then_inc(s["vps"], 1)

            def output(i):
                pe.wait_ge(s["vals"], i + 1)
                if i >= 1:
                    pe.wait_ge(s["added"], i)
                for pair in range(CPAIRS):
                    ins = mm(psF[:, 0:P], vals[:, i % 2, pair, :], w("o")[:, pair * P:(pair + 1) * P],
                             start=pair == 0, stop=pair == CPAIRS - 1)
                ins.then_inc(s["out"], 1)

            slots(scores=(scores, 0), turn=(turn, 2), output=(output, 3), values=(values, 2))



BF16 = mybir.dt.bfloat16
MOE, PICKS = 8, 2
STEPS = ROWS
STEP_TILE = P // PLACES
TRACKS = MOE * PICKS
SPLIT = 3
GROUPS = 2
MEMBERS = MOE // GROUPS
TRACK_ROWS = PICKS * PLACES
GATES = 4 * P
LSTM_COLS = [("router", MOE), ("router_b", MOE), ("rank", MOE), ("place", PLACES), ("step", STEP_TILE),
             ("same", MEMBERS * PLACES), ("member", P), ("bo", P), ("b", GROUPS * GATES), ("wi", MOE * GATES),
             ("wh", MOE * GATES), ("wo", MOE * P)]


def lay_lstm(np, x, A):
    g = {k[len("L1_ffn_"):]: v for k, v in x.items() if k.startswith("L1_ffn_")}

    def gates(a):
        parts = a.reshape(*a.shape[:-1], 4, P)
        return parts[..., [0, 1, 3, 2], :].reshape(a.shape)

    t = np.arange(P)
    row_member, row_place = t // TRACK_ROWS, t % PLACES
    col = np.arange(MEMBERS * PLACES)
    b = gates(g["b"]).reshape(GROUPS, MEMBERS, GATES)
    A["lstm"] = pack(np, LSTM_COLS, {
        "wi": np.transpose(gates(g["Wi"]), (1, 0, 2)).reshape(P, MOE * GATES),
        "wh": np.transpose(gates(g["Wh"]), (1, 0, 2)).reshape(P, MOE * GATES),
        "wo": np.transpose(g["Wo"], (1, 0, 2)).reshape(P, MOE * P), "router": g["router_w"],
        "router_b": np.tile(g["router_b"], (P, 1)),
        "rank": np.tile(np.arange(MOE, 0, -1, dtype=np.float32), (P, 1)),
        "place": (t[:, None] % PLACES == np.arange(PLACES)).astype(np.float32),
        "step": (t[:, None] // PLACES == np.arange(STEP_TILE)).astype(np.float32),
        "same": ((row_member[:, None] == col // PLACES) & (row_place[:, None] == col % PLACES)).astype(np.float32),
        "member": (np.arange(SPLIT * MEMBERS)[:, None] % MEMBERS == row_member).astype(np.float32),
        "bo": g["bo"], "b": np.transpose(b, (1, 0, 2)).reshape(MEMBERS, GROUPS * GATES)})


def lstm_experts(c, A):
    nc = c.nc
    at, n_cols = columns(LSTM_COLS)
    with ExitStack() as st:
        W = c.sb("lstm_w", [P, n_cols], st)

        def w(part, rows=P):
            return W[0:rows, at[part][0]:at[part][1]]

        def sb(name, shape, dt=F32):
            return c.sb("lstm_" + name, shape, st, dt)

        norm = Norm(c, "lstm_n", st)
        X, XT = sb("x", [P, TILES, P]), sb("xT", [P, TOKENS])
        L, hot, score = sb("l", [P, TILES, MOE]), sb("hot", [P, PICKS, TILES, MOE]), sb("score", [P, TILES, MOE])
        top, rank, ratio, wt = (sb(n, [P, PICKS, TILES]) for n in ("top", "rank_top", "ratio", "wt"))
        mask = sb("mask", [P, TILES, MOE, PICKS])
        coef = sb("coef", [P, TILES, MOE, PICKS])
        both = sb("both", [P, TILES, MOE])
        maskT = sb("maskT", [TRACKS, TOKENS], BF16)
        ident16 = sb("ident16", [TRACKS, TRACKS], BF16)
        maskB = sb("maskB", [P, TRACKS, TOKENS], BF16)
        bothT = sb("bothT", [MOE, TOKENS])
        spread = sb("spread", [P, TILES * TRACKS, PLACES])
        coefR = sb("coefR", [P, GROUPS, STEPS])
        parts = [sb(f"b_part{i}", [MEMBERS, GROUPS * GATES], BF16) for i in range(SPLIT)]
        left = sb("b_left", [MEMBERS, GROUPS * GATES])
        b3 = sb("b3", [SPLIT * MEMBERS, GROUPS * GATES], BF16)
        member = sb("member", [SPLIT * MEMBERS, P], BF16)
        xm = sb("xm", [P, 2, TRACKS, PLACES])
        pick = sb("pick", [P, 2, GROUPS, MEMBERS * PLACES])
        sig, cand = sb("sig", [P, GROUPS, 3 * P]), sb("cand", [P, GROUPS, P])
        ig, cell, cellt = sb("ig", [P, GROUPS, P]), sb("cell", [P, GROUPS, P]), sb("cellt", [P, GROUPS, P])
        hrow, hT = sb("hrow", [P, GROUPS, P]), sb("hT", [P, GROUPS, P])
        hsel = sb("hsel", [P, MOE, TOKENS])
        psG = c.ps("lstm_psG", [P, 4, HALF], st)
        psH = c.ps("lstm_psH", [P, GROUPS, HALF], st)
        psP = c.ps("lstm_psP", [P, 2, HALF], st)

        names = ("w", "large", "x", "xps", "xT", "logit", "gap", "ratio", "mask", "coef", "mps", "mT", "bps", "bact",
                 "bdve",
                 "bothps", "bothT", "spread", "rps", "coefR", "idb", "split", "moved", "memb", "zero", "xm", "pick",
                 "pickps", "hsel", "out", "ord")
        s = {k: c.sem("lstm_" + k) for k in names}
        gates_ps, gates_read, cell_in, cell_new, cell_tanh, h_row, h_T, h_ps = (
            [c.sem(f"lstm_{k}{g}") for g in range(GROUPS)]
            for k in ("gates", "gates_read", "cell_in", "cell_new", "cell_tanh", "h_row", "h_T", "h_ps"))
        block = st.enter_context(nc.Block())

        def steps(eng, body):
            body(0, 0, 0, False)
            body(1, 1, 1, False)
            with eng.Fori(1, STEPS // 2 - 1) as it:
                for j in range(2):
                    body(it * 2 + j, j, 2, False)
            body(STEPS - 2, 0, 2, False)
            body(STEPS - 1, 1, 2, True)

        def more(t):
            return not isinstance(t, int) or t + 2 < STEPS

        @block.sync
        def _(sp):
            first = at["wi"][0]
            sp.dma_start(W[:, 0:first], A["lstm"][:, 0:first]).then_inc(s["w"], 16)
            sp.dma_start(W[:, first:], A["lstm"][:, first:]).then_inc(s["large"], 16)
            sp.wait_ge(s["split"], SPLIT)
            for i in range(SPLIT):
                sp.dma_start(b3[i * MEMBERS:(i + 1) * MEMBERS, :], parts[i][:, :]).then_inc(s["moved"], 16)

        @block.gpsimd
        def _(pool):
            nc.gpsimd.memset(cell[:, :, :], 0.0).then_inc(s["zero"], 1)
            nc.gpsimd.memset(hT[:, :, :], 0.0).then_inc(s["zero"], 1)
            nc.gpsimd.tensor_copy(ident16[:, :], c.ident[0:TRACKS, 0:TRACKS]).then_inc(s["idb"], 1)
            norm.power(pool)
            pool.wait_ge(s["w"], 16)
            nc.gpsimd.tensor_copy(member[:, :], w("member", SPLIT * MEMBERS)).then_inc(s["memb"], 1)
            pool.wait_ge(s["xT"], 1)
            pool.wait_ge(s["bact"], TRACKS)
            pool.wait_ge(s["bdve"], TRACKS)
            pool.wait_ge(s["coefR"], 1)

            def masked_inputs(t, parity):
                nc.gpsimd.tensor_tensor(
                    xm[:, parity, :, :], maskB[:, :, bass.ds(t * PLACES, PLACES)],
                    XT[:, bass.ds(t * PLACES, PLACES)].unsqueeze(1).broadcast_to([P, TRACKS, PLACES]), ALU.mult
                    ).then_inc(s["xm"], 1)

            def body(t, parity, first, last):
                if first >= 1:
                    pool.wait_ge(gates_ps[1], t)
                nc.gpsimd.tensor_tensor(
                    pick[:, parity, :, :], w("same").unsqueeze(1).broadcast_to([P, GROUPS, MEMBERS * PLACES]),
                    coefR[:, :, bass.ds(t, 1)].broadcast_to([P, GROUPS, MEMBERS * PLACES]), ALU.mult
                    ).then_inc(s["pick"], 1)
                if more(t):
                    if first < 2:
                        pool.wait_ge(gates_ps[1], t + 1)
                    masked_inputs(t + 2, parity)

            masked_inputs(0, 0)
            masked_inputs(1, 1)
            steps(pool, body)

        @block.scalar
        def _(act):
            a = nc.scalar.activation
            act.wait_ge(s["xps"], 1)
            a(XT[:, :], psG[:, 0:2, :].rearrange("p a n -> p (a n)"), ACT.Copy).then_inc(s["xT"], 1)
            act.wait_ge(s["gap"], 1)
            a(ratio[:, 0, :], ratio[:, 1, :], ACT.Exp).then_inc(s["ratio"], 1)
            for r in range(TRACKS):
                act.wait_ge(s["bps"], 2 * r + 1)
                a(maskB[:, r, 0:HALF], psG[:, 2 * r % 4, :], ACT.Copy).then_inc(s["bact"], 1)

            def picked(t, parity):
                act.wait_ge(s["pickps"], t + 1)
                a(hsel[:, :, bass.ds(t * PLACES, PLACES)],
                  psP[:, parity, 0:MOE * PLACES].rearrange("p (e b) -> p e b", b=PLACES), ACT.Copy
                  ).then_inc(s["hsel"], 1)

            def body(t, parity, first, last):
                for g in range(GROUPS):
                    act.wait_ge(gates_ps[g], t + 1)
                    a(sig[:, g, :], psG[:, 2 * parity + g, 0:3 * P], ACT.Sigmoid)
                    a(cand[:, g, :], psG[:, 2 * parity + g, 3 * P:GATES], ACT.Tanh).then_inc(gates_read[g], 1)
                    act.wait_ge(cell_new[g], t + 1)
                    a(cellt[:, g, :], cell[:, g, :], ACT.Tanh).then_inc(cell_tanh[g], 1)
                    if g == 0 and first >= 1:
                        picked(t - 1, 1 - parity)
                if last:
                    picked(t, parity)

            steps(act, body)

        @block.vector
        def _(dve):
            v = nc.vector
            o = Order(dve, s["ord"])
            norm.statistics(o, c.H)
            norm.apply(dve, X, c.H).then_inc(s["x"], 1)
            dve.wait_ge(s["w"], 16)
            o.after(v.tensor_copy(left[:, :], w("b", MEMBERS)))
            for i in range(SPLIT):
                v.tensor_copy(parts[i][:, :], left[:, :]).then_inc(s["split"], 1)
                dve.wait_ge(s["split"], i + 1)
                if i < SPLIT - 1:
                    o.after(v.tensor_tensor(left[:, :], left[:, :], parts[i][:, :], ALU.subtract))
            dve.wait_ge(s["logit"], 1)
            o.after(v.tensor_tensor(L[:, :, :], psH[:, 0, 0:TILES * MOE].rearrange("p (i e) -> p i e", e=MOE),
                                    w("router_b").unsqueeze(1).broadcast_to([P, TILES, MOE]), ALU.add))
            for k in range(PICKS):
                o.after(v.tensor_reduce(top[:, k, :], L[:, :, :], AX, ALU.max))
                o.after(v.tensor_tensor(score[:, :, :], L[:, :, :],
                                        top[:, k, :].unsqueeze(2).broadcast_to([P, TILES, MOE]), ALU.is_equal))
                o.after(v.tensor_tensor(score[:, :, :], score[:, :, :],
                                        w("rank").unsqueeze(1).broadcast_to([P, TILES, MOE]), ALU.mult))
                o.after(v.tensor_reduce(rank[:, k, :], score[:, :, :], AX, ALU.max))
                o.after(v.tensor_tensor(hot[:, k, :, :], score[:, :, :],
                                        rank[:, k, :].unsqueeze(2).broadcast_to([P, TILES, MOE]), ALU.is_equal))
                if k < PICKS - 1:
                    o.after(v.scalar_tensor_tensor(L[:, :, :], hot[:, k, :, :], MASKED, L[:, :, :],
                                                   ALU.mult, ALU.add))
            v.tensor_tensor(ratio[:, 1, :], top[:, 1, :], top[:, 0, :], ALU.subtract).then_inc(s["gap"], 1)
            for k in range(PICKS):
                ins = v.tensor_copy(mask[:, :, :, k], hot[:, k, :, :])
            ins.then_inc(s["mask"], 1)
            dve.wait_ge(s["ratio"], 1)
            o.after(v.tensor_scalar_add(wt[:, 1, :], ratio[:, 0, :], 1.0))
            o.after(v.reciprocal(wt[:, 0, :], wt[:, 1, :]))
            o.after(v.tensor_tensor(wt[:, 1, :], ratio[:, 0, :], wt[:, 0, :], ALU.mult))
            for k in range(PICKS):
                ins = v.tensor_tensor(coef[:, :, :, k], hot[:, k, :, :],
                                      wt[:, k, :].unsqueeze(2).broadcast_to([P, TILES, MOE]), ALU.mult)
            o.after(ins)
            v.tensor_tensor(both[:, :, :], coef[:, :, :, 0], coef[:, :, :, 1], ALU.add).then_inc(s["coef"], 1)
            v.tensor_tensor(spread[:, :, :],
                            coef[:, :, :, :].rearrange("p i e k -> p (i e k)").unsqueeze(2)
                            .broadcast_to([P, TILES * TRACKS, PLACES]),
                            w("place").unsqueeze(1).broadcast_to([P, TILES * TRACKS, PLACES]), ALU.mult
                            ).then_inc(s["spread"], 1)
            dve.wait_ge(s["mps"], 1)
            v.tensor_copy(maskT[:, :], psP[0:TRACKS, :, :].rearrange("p a n -> p (a n)")).then_inc(s["mT"], 1)
            dve.wait_ge(s["bothps"], 1)
            v.tensor_copy(bothT[:, :], psP[0:MOE, :, :].rearrange("p a n -> p (a n)")).then_inc(s["bothT"], 1)
            dve.wait_ge(s["rps"], 1)
            v.tensor_copy(coefR[:, :, :], psH[:, 0, 0:GROUPS * STEPS].rearrange("p (g t) -> p g t", t=STEPS)
                          ).then_inc(s["coefR"], 1)
            for r in range(TRACKS):
                dve.wait_ge(s["bps"], 2 * r + 2)
                v.tensor_copy(maskB[:, r, HALF:TOKENS], psG[:, (2 * r + 1) % 4, :]).then_inc(s["bdve"], 1)
            dve.wait_ge(s["zero"], 2)

            def body(t, parity, first, last):
                for g in range(GROUPS):
                    dve.wait_ge(gates_read[g], t + 1)
                    v.tensor_tensor(ig[:, g, :], sig[:, g, 0:P], cand[:, g, :], ALU.mult)
                    v.tensor_tensor(cell[:, g, :], sig[:, g, P:2 * P], cell[:, g, :], ALU.mult
                                    ).then_inc(cell_in[g], 1)
                    dve.wait_ge(cell_in[g], t + 1)
                    v.tensor_tensor(cell[:, g, :], cell[:, g, :], ig[:, g, :], ALU.add).then_inc(cell_new[g], 1)
                    dve.wait_ge(cell_tanh[g], t + 1)
                    v.tensor_tensor(hrow[:, g, :], sig[:, g, 2 * P:3 * P], cellt[:, g, :], ALU.mult
                                    ).then_inc(h_row[g], 1)
                    dve.wait_ge(h_ps[g], t + 1)
                    v.tensor_copy(hT[:, g, :], psH[:, g, 0:P]).then_inc(h_T[g], 1)

            steps(dve, body)
            dve.wait_ge(s["out"], 1)
            v.tensor_tensor(c.H[:, :, :], c.H[:, :, :], psG[:, 0:2, :].rearrange("p a (i d) -> p (a i) d", d=P),
                            ALU.add)

        @block.tensor
        def _(pe):
            mm = nc.tensor.matmul
            tr = nc.tensor.transpose
            pe.wait_ge(s["x"], 1)
            for i in range(TILES):
                ins = tr(psG[:, i // 4, i % 4 * P:(i % 4 + 1) * P], X[:, i, :], c.ident[:, :])
            ins.then_inc(s["xps"], 1)
            pe.wait_ge(s["w"], 16)
            pe.wait_ge(s["xT"], 1)
            for i in range(TILES):
                ins = mm(psH[:, 0, i * MOE:(i + 1) * MOE], XT[:, i * P:(i + 1) * P], w("router"),
                         start=True, stop=True)
            ins.then_inc(s["logit"], 1)
            pe.wait_ge(s["mask"], 1)
            for i in range(TILES):
                ins = tr(psP[0:TRACKS, i // 4, i % 4 * P:(i % 4 + 1) * P],
                         mask[:, i, :, :].rearrange("p e k -> p (e k)"), c.ident[:, :])
            ins.then_inc(s["mps"], 1)
            pe.wait_ge(s["coef"], 1)
            pe.wait_ge(s["mT"], 1)
            for i in range(TILES):
                ins = tr(psP[0:MOE, i // 4, i % 4 * P:(i % 4 + 1) * P], both[:, i, :], c.ident[:, :])
            ins.then_inc(s["bothps"], 1)
            pe.wait_ge(s["spread"], 1)
            for i in range(TILES):
                for g in range(GROUPS):
                    first = (i * GROUPS + g) * TRACKS // GROUPS
                    ins = mm(psH[:, 0, g * STEPS + i * STEP_TILE:g * STEPS + (i + 1) * STEP_TILE],
                             spread[:, first:first + TRACKS // GROUPS, :].rearrange("p e b -> p (e b)"), w("step"),
                             start=True, stop=True)
            ins.then_inc(s["rps"], 1)
            pe.wait_ge(s["idb"], 1)
            for u in range(2 * TRACKS):
                r, q = u // 2, u % 2
                if u >= 4:
                    pe.wait_ge(s["bact"] if q == 0 else s["bdve"], r - 1)
                mm(psG[:, u % 4, :], ident16[:, r:r + 1].broadcast_to([TRACKS, P]),
                   maskT[:, q * HALF:(q + 1) * HALF], start=True, stop=True).then_inc(s["bps"], 1)
            pe.wait_ge(s["bact"], TRACKS)
            pe.wait_ge(s["bdve"], TRACKS)
            pe.wait_ge(s["moved"], 16 * SPLIT)
            pe.wait_ge(s["memb"], 1)
            pe.wait_ge(s["coefR"], 1)
            pe.wait_ge(s["bothT"], 1)
            pe.wait_ge(s["zero"], 2)

            def inputs(parity, g):
                bank = 2 * parity + g
                mm(psG[:, bank, :], member[:, :], b3[:, g * GATES:(g + 1) * GATES], start=True, stop=False)
                for j in range(MEMBERS):
                    e = g * MEMBERS + j
                    mm(psG[j * TRACK_ROWS:(j + 1) * TRACK_ROWS, bank, :],
                       xm[:, parity, e * PICKS:(e + 1) * PICKS, :].rearrange("p k b -> p (k b)"),
                       w("wi")[:, e * GATES:(e + 1) * GATES], start=False, stop=False)

            def recur(parity, g):
                for j in range(MEMBERS):
                    e = g * MEMBERS + j
                    ins = mm(psG[j * TRACK_ROWS:(j + 1) * TRACK_ROWS, 2 * parity + g, :],
                             hT[:, g, j * TRACK_ROWS:(j + 1) * TRACK_ROWS], w("wh")[:, e * GATES:(e + 1) * GATES],
                             start=False, stop=True)
                ins.then_inc(gates_ps[g], 1)

            def body(t, parity, first, last):
                for g in range(GROUPS):
                    pe.wait_ge(h_row[g], t + 1)
                    tr(psH[:, g, 0:P], hrow[:, g, :], c.ident[:, :]).then_inc(h_ps[g], 1)
                    if g == 0:
                        pe.wait_ge(s["pick"], t + 1)
                        if first >= 2:
                            pe.wait_ge(s["hsel"], t - 1)
                    ins = mm(psP[:, parity, g * MEMBERS * PLACES:(g + 1) * MEMBERS * PLACES], hrow[:, g, :],
                             pick[:, parity, g, :], start=True, stop=True)
                    if g == GROUPS - 1:
                        ins.then_inc(s["pickps"], 1)
                    if more(t):
                        if g == 0:
                            pe.wait_ge(s["xm"], t + 3)
                        pe.wait_ge(gates_read[g], t + 1)
                        inputs(parity, g)
                    if not last:
                        pe.wait_ge(h_T[g], t + 1)
                        recur(1 - parity, g)

            pe.wait_ge(s["large"], 16)
            for t in range(2):
                pe.wait_ge(s["xm"], t + 1)
                for g in range(GROUPS):
                    inputs(t, g)
                    if t == 0:
                        recur(t, g)
            steps(pe, body)
            pe.wait_ge(s["hsel"], STEPS)
            pe.wait_ge(gates_read[0], STEPS)
            pe.wait_ge(gates_read[1], STEPS)
            for i in range(TILES):
                out = psG[:, i // 4, i % 4 * P:(i % 4 + 1) * P]
                for e in range(MOE):
                    mm(out, hsel[:, e, i * P:(i + 1) * P], w("wo")[:, e * P:(e + 1) * P], start=e == 0, stop=False)
                ins = mm(out, bothT[:, i * P:(i + 1) * P], w("bo", MOE), start=False, stop=True)
            ins.then_inc(s["out"], 1)



DHEADS, DDIM = 8, 64
ROLLS = 2
ZBUFS = 3
FEAT = 2 * DDIM
SEQ, BATCH = ROWS, PLACES
PAIRS = BATCH // 2
DSCALE, DEPS = DDIM ** -0.5, 1e-5
BLOCK16 = 16
YUNITS = 2 * 2 * (ROLLS + 1)
CHAINS = 2
DMEMBERS = PAIRS // CHAINS
DSTEPS = [(("A0", "F"), "scalar"), (("A1", "At1"), "scalar"), (("A2", "At2"), "scalar"), (("D2",), "vector"),
         (("A3",), "scalar"), (("D3",), "vector"), (("D4",), "vector"), (("T", "Tt"), "scalar"),
         (("E0",), "scalar"), (("T2t",), "scalar"), (("E1",), "vector"), (("dl",), "vector"), (("O",), "vector")]
STEP_OF = {name: k for k, (names, _) in enumerate(DSTEPS) for name in names}
OPERANDS = {"A0": ("At0", "eye"), "F": ("far", "eye"), "A1": ("At0", "A0"), "At1": ("A0", "At0"),
            "A2": ("At1", "A1"), "At2": ("A1", "At1"), "D2": ("A1", "D1"), "A3": ("At2", "A2"), "D3": ("A2", "D2"),
            "D4": ("A3", "D3"), "T": ("D4", "F"), "Tt": ("F", "D4"), "E0": ("D4", "rhs"), "T2t": ("T", "Tt"),
            "E1": ("Tt", "E0"), "dl": ("T2t", "E1"), "O": ("S", "dl")}
QSUMS = ("D2", "D3", "D4", "E1")
LISTS = ("At0", "far", "D1", "rhs", "S", "dl")
DELTA_COLS = [("v", DHEADS * DDIM), ("beta", DHEADS), ("eye", DDIM), ("near", DDIM), ("far", DDIM), ("upto", DDIM),
              ("eps", 1), ("sign", (ROLLS + 1) * FEAT), ("roll", 2 * DHEADS * (ROLLS + 1) * FEAT),
              ("o", DHEADS * DDIM), ("g", P), ("b", P)]


def lay_delta(np, x, A):
    w = x["L1_attn_W_qkvb"].reshape(DHEADS, 3 * DDIM + 1, P)
    kq = np.stack([w[:, DDIM:2 * DDIM], w[:, :DDIM]])
    both = np.concatenate([kq, kq], axis=2)
    rolled = np.stack([np.roll(both, i, axis=2) for i in range(ROLLS + 1)], axis=2)
    sign = np.repeat(np.array([1, -1], np.float32), DDIM)
    sign = np.concatenate([np.roll(sign, i) for i in range(ROLLS + 1)])
    s, t = np.arange(DDIM)[:, None], np.arange(DDIM)[None, :]
    near = (s < t) & (s // BLOCK16 == t // BLOCK16)
    far = (s < t) & (s // BLOCK16 != t // BLOCK16)

    def twice(a):
        return np.concatenate([a, a]).astype(np.float32)

    A["delta"] = pack(np, DELTA_COLS, {
        "roll": rolled.reshape(-1, P).T, "sign": np.tile(sign, (P, 1)),
        "v": w[:, 2 * DDIM:3 * DDIM].reshape(-1, P).T, "beta": w[:, 3 * DDIM].T,
        "o": np.transpose(x["L1_attn_W_o"].T.reshape(4, P, P), (1, 0, 2)).reshape(P, 4 * P),
        "g": np.tile(x["L1_attn_ln_g"], (P, 1)), "b": np.tile(x["L1_attn_ln_b"], (P, 1)),
        "eye": twice(s == t), "near": twice(near), "far": twice(far), "upto": twice(s <= t),
        "eps": np.full((P, 1), DEPS, np.float32)})


def delta_attention(c, A):
    nc = c.nc
    at, n_cols = columns(DELTA_COLS)
    with ExitStack() as st:
        W = c.sb("delta_w", [P, n_cols], st)

        def w(part):
            return W[:, at[part][0]:at[part][1]]

        def sb(name, shape):
            return c.sb("delta_" + name, shape, st)

        n1, n2 = Norm(c, "delta_n1", st), Norm(c, "delta_n2", st)
        X = sb("x", [P, TILES, P])
        XT = sb("xT", [P, BATCH, SEQ])
        V = sb("v", [P, PAIRS, DHEADS, DDIM])
        beta = sb("beta", [P, PAIRS, DHEADS])
        Y0 = sb("y0", [P, 2, HALF])
        Z = sb("z", [P, ZBUFS, ROLLS, BATCH, 2 * SEQ + 1])
        sumk = sb("sumk", [P, 2, PAIRS])
        sumq = sb("sumq", [P, CHAINS, DMEMBERS])
        rk, al, nal = sb("rk", [P, PAIRS]), sb("al", [P, 2, PAIRS]), sb("nal", [P, PAIRS])
        ga = sb("ga", [P, PAIRS, SEQ - 1])
        lists = {k: sb(k, [P, 2, PAIRS, DDIM + 1 if k == "dl" else DDIM]) for k in LISTS}
        mats = {names: sb(names[0], [P, CHAINS, len(names), DMEMBERS, SEQ]) for names, _ in DSTEPS[:-2]}
        den = sb("den", [P, CHAINS, DMEMBERS])
        O = sb("o", [P, PAIRS, DHEADS, DDIM])
        OT = sb("oT", [P, 4, TOKENS])
        AT = sb("aT", [P, TOKENS])
        psY = c.ps("delta_psY", [P, 2, HALF], st)
        psGS = c.ps("delta_psGS", [P, PAIRS, 2 * SEQ], st)
        psM = c.ps("delta_psM", [P, 2 * CHAINS, HALF], st)

        names = ("w", "roll", "signed", "x", "xps", "xT", "vps", "v", "bps", "beta", "yps", "y0", "z", "gs",
                 "gsread", "ones", "ga", "lists", "product", "scalar", "vector", "ops", "oT", "aps", "aT", "back",
                 "ord")
        s = {k: c.sem("delta_" + k) for k in names}
        block = st.enter_context(nc.Block())
        lo_hi = [slice(0, DDIM), slice(DDIM, P)]
        readers = {e: [k for k, (_, by) in enumerate(DSTEPS) if by == e] for e in ("scalar", "vector")}

        def ready(eng, h, k, chain):
            eng.wait_ge(s["product"], (h * len(DSTEPS) + k) * CHAINS + chain + 1)

        def done(eng, h, k, chain):
            by = DSTEPS[k][1]
            eng.wait_ge(s[by], (h * len(readers[by]) + readers[by].index(k)) * CHAINS + chain + 1)

        def bank(h, k, chain):
            return psM[:, 2 * chain + (h * len(DSTEPS) + k) % 2, :]

        def members(chain):
            return slice(chain * DMEMBERS, (chain + 1) * DMEMBERS)

        def matrix(name, h, j, rows):
            if name == "eye":
                return w("eye")[rows, :]
            if name in LISTS:
                return lists[name][rows, h % 2, j, :]
            group = DSTEPS[STEP_OF[name]][0]
            return mats[group][rows, j // DMEMBERS, group.index(name), j % DMEMBERS, :]

        def unit(h, u):
            m = h * YUNITS // (ROLLS + 1) + u // (ROLLS + 1)
            return h * YUNITS + u, m, u // (2 * (ROLLS + 1)), u // (ROLLS + 1) % 2, u % (ROLLS + 1)

        def fill(head_work, h, slot):
            gram, lists_part, project = head_work
            if h + 1 < DHEADS:
                if slot % 2 == 0 and slot < 2 * PAIRS:
                    gram(h + 1, slot // 2)
                if 2 * PAIRS <= slot < 2 * PAIRS + 3:
                    lists_part(h + 1, slot - 2 * PAIRS)
            if h + 2 < DHEADS and slot % 2 == 1 and slot < 2 * YUNITS:
                project(h + 2, slot // 2)

        def prepare(head_work):
            gram, lists_part, project = head_work
            for u in range(YUNITS):
                project(0, u)
            for j in range(PAIRS):
                gram(0, j)
            for part in range(3):
                lists_part(0, part)
            for u in range(YUNITS):
                project(1, u)

        def nothing(*_):
            pass

        @block.sync
        def _(sp):
            first = at["roll"][0]
            sp.dma_start(W[:, 0:first], A["delta"][:, 0:first]).then_inc(s["w"], 16)
            sp.dma_start(W[:, first:], A["delta"][:, first:]).then_inc(s["roll"], 16)

        @block.gpsimd
        def _(pool):
            nc.gpsimd.memset(Z[:, :, :, :, 2 * SEQ:], 1.0).then_inc(s["ones"], 1)
            nc.gpsimd.memset(lists["At0"][:, :, :, 0:1], 0.0).then_inc(s["ones"], 1)
            nc.gpsimd.memset(lists["far"][:, :, :, 0:1], 0.0).then_inc(s["ones"], 1)
            n1.power(pool)
            pool.wait_ge(s["w"], 16)
            pool.wait_ge(s["roll"], 16)
            r = w("roll").rearrange("p (k h f) -> p k h f", k=2, h=DHEADS)
            for h in range(DHEADS):
                nc.gpsimd.tensor_tensor(r[:, :, h, :], r[:, :, h, :],
                                        w("sign").unsqueeze(1).broadcast_to([P, 2, (ROLLS + 1) * FEAT]),
                                        ALU.mult).then_inc(s["signed"], 1)

            def each(part, first=0):
                return w(part)[:, first:].unsqueeze(1).broadcast_to([P, PAIRS, SEQ - first])

            pool.wait_ge(s["v"], PAIRS)
            pool.wait_ge(s["ones"], 3)
            t = nc.gpsimd.tensor_tensor
            for h in range(DHEADS):
                lst = {k: lists[k][:, h % 2, :, :] for k in LISTS}
                pool.wait_ge(s["ga"], h + 1)
                t(lst["At0"][:, :, 1:], ga[:, :, :], each("near", 1), ALU.mult).then_inc(s["lists"], 1)
                t(lst["far"][:, :, 1:], ga[:, :, :], each("far", 1), ALU.mult).then_inc(s["lists"], 1)
                t(lst["rhs"], V[:, :, h, :], sumk[:, h % 2, :].unsqueeze(2).broadcast_to([P, PAIRS, DDIM]),
                  ALU.mult).then_inc(s["lists"], 1)
                pool.wait_ge(s["lists"], 4 * h + 1)
                t(lst["D1"], lst["At0"], each("eye"), ALU.add).then_inc(s["lists"], 1)
            n2.power(pool)

        @block.scalar
        def _(act):
            a = nc.scalar.activation
            act.wait_ge(s["xps"], 1)
            a(XT[:, :, :].rearrange("p b l -> p l b"),
              psGS[:, :, :].rearrange("p a k -> p (a k)").rearrange("p (l b) -> p l b", b=BATCH), ACT.Copy
              ).then_inc(s["xT"], 1)
            act.wait_ge(s["bps"], 1)
            a(beta[:, :, :], psGS[:, 0, 0:PAIRS * DHEADS].rearrange("p (j h) -> p j h", h=DHEADS), ACT.Sigmoid
              ).then_inc(s["beta"], 1)

            def project(h, u):
                n, m, kq, half, roll = unit(h, u)
                if roll == 0:
                    act.wait_ge(s["yps"], n + 1)
                    if m >= 2:
                        act.wait_ge(s["z"], (m - 1) * ROLLS)
                    a(Y0[:, m % 2, :], psY[:, n % 2, :], ACT.Relu).then_inc(s["y0"], 1)

            work = (nothing, nothing, project)
            prepare(work)
            for h in range(DHEADS):
                for k, (group, by) in enumerate(DSTEPS):
                    for chain in range(CHAINS):
                        if by == "scalar":
                            ready(act, h, k, chain)
                            a(mats[group][:, chain, :, :, :].rearrange("p n j t -> p (n j t)"),
                              bank(h, k, chain)[:, 0:len(group) * DMEMBERS * SEQ], ACT.Copy).then_inc(s["scalar"], 1)
                        fill(work, h, k * CHAINS + chain)
            for j in range(PAIRS):
                act.wait_ge(s["ops"], j + 1)
                a(OT[:, :, j * P:(j + 1) * P], psM[:, j % 2, :].rearrange("p (k t) -> p k t", t=P), ACT.Copy
                  ).then_inc(s["oT"], 1)
            act.wait_ge(s["aps"], 1)
            a(AT[:, :].rearrange("p (l b) -> p b l", b=BATCH),
              psGS[:, :, :].rearrange("p a k -> p (a k)").rearrange("p (b l) -> p b l", l=SEQ), ACT.Copy
              ).then_inc(s["aT"], 1)

        @block.vector
        def _(dve):
            v = nc.vector
            o = Order(dve, s["ord"])
            n1.statistics(o, c.H)
            n1.apply(dve, X, c.H).then_inc(s["x"], 1)
            for j in range(PAIRS):
                dve.wait_ge(s["vps"], j + 1)
                v.tensor_copy(V[:, j, :, :].rearrange("p h d -> p (h d)"), psY[:, j % 2, :]).then_inc(s["v"], 1)

            def project(h, u):
                n, m, kq, half, roll = unit(h, u)
                if roll > 0:
                    dve.wait_ge(s["yps"], n + 1)
                    dve.wait_ge(s["y0"], m + 1)
                    v.scalar_tensor_tensor(Z[:, h % ZBUFS, roll - 1, half * BATCH // 2:(half + 1) * BATCH // 2,
                                             kq * SEQ:(kq + 1) * SEQ],
                                           psY[:, n % 2, :].rearrange("p (b l) -> p b l", l=SEQ), 0.0,
                                           Y0[:, m % 2, :].rearrange("p (b l) -> p b l", l=SEQ), ALU.max, ALU.mult
                                           ).then_inc(s["z"], 1)

            def wide(a, n=DDIM):
                return a.unsqueeze(2).broadcast_to([P, a.shape[1], n])

            def lists_part(h, part):
                if part == 0:
                    dve.wait_ge(s["gs"], h + 1)
                    if h == 0:
                        dve.wait_ge(s["beta"], 1)
                    o.after(v.tensor_copy(sumk[:, h % 2, :], psGS[:, :, 2 * SEQ - 1]))
                    o.after(v.reciprocal(rk[:, :], sumk[:, h % 2, :]))
                    v.tensor_copy(lists["dl"][:, h % 2, :, DDIM], rk[:, :])
                    o.after(v.tensor_tensor(al[:, h % 2, :], rk[:, :], rk[:, :], ALU.mult))
                    o.after(v.tensor_tensor(al[:, h % 2, :], al[:, h % 2, :], beta[:, :, h], ALU.mult))
                    o.after(v.tensor_scalar_mul(nal[:, :], al[:, h % 2, :], -1.0))
                elif part == 1:
                    if h > 0:
                        dve.wait_ge(s["lists"], 4 * h)
                    v.tensor_tensor(ga[:, :, :], psGS[:, :, 0:SEQ - 1], wide(nal[:, :], SEQ - 1), ALU.mult
                                    ).then_inc(s["ga"], 1)
                else:
                    v.tensor_tensor(lists["S"][:, h % 2, :, :], psGS[:, :, SEQ - 1:2 * SEQ - 1],
                                    w("upto").unsqueeze(1).broadcast_to([P, PAIRS, SEQ]), ALU.mult
                                    ).then_inc(s["gsread"], 1)

            work = (nothing, lists_part, project)
            prepare(work)
            for h in range(DHEADS):
                for k, (group, by) in enumerate(DSTEPS):
                    for chain in range(CHAINS):
                        if by == "vector":
                            ready(dve, h, k, chain)
                            name, js = group[0], members(chain)
                            src = bank(h, k, chain)[:, 0:DMEMBERS * SEQ].rearrange("p (j t) -> p j t", t=SEQ)
                            if name == "dl":
                                ins = v.tensor_tensor(lists["dl"][:, h % 2, js, 0:DDIM], src,
                                                      wide(al[:, h % 2, js]), ALU.mult)
                            elif name == "O":
                                src = bank(h, k, chain)[:, 0:DMEMBERS * (DDIM + 1)].rearrange(
                                    "p (j d) -> p j d", d=DDIM + 1)
                                d = den[:, chain, :]
                                done(dve, h, STEP_OF["E1"], chain)
                                o.after(v.tensor_tensor(d, sumq[:, chain, :], src[:, :, DDIM], ALU.add))
                                o.after(v.reciprocal(d, d))
                                o.after(v.tensor_scalar_mul(d, d, DSCALE))
                                ins = v.tensor_tensor(O[:, js, h, :], src[:, :, 0:DDIM], wide(d), ALU.mult)
                            else:
                                dst = mats[group][:, chain, 0, :, :]
                                add = lists["D1"][:, h % 2, js, :] if name == "D2" else \
                                    mats[({"D3": "D2", "D4": "D3", "E1": "E0"}[name],)][:, chain, 0, :, :]
                                if name == "D2":
                                    dve.wait_ge(s["lists"], 4 * h + 4)
                                elif name == "E1":
                                    done(dve, h, STEP_OF["E0"], chain)
                                jj = QSUMS.index(name)
                                v.tensor_copy(sumq[:, chain, jj:jj + 1],
                                              bank(h, k, chain)[:, DMEMBERS * SEQ:DMEMBERS * SEQ + 1])
                                ins = v.tensor_tensor(dst, src, add, ALU.add)
                            ins.then_inc(s["vector"], 1)
                        fill(work, h, k * CHAINS + chain)
            dve.wait_ge(s["vector"], len(readers["vector"]) * DHEADS * CHAINS)
            dve.wait_ge(s["roll"], 16)
            dve.wait_ge(s["back"], 1)
            o.after(v.tensor_tensor(X[:, :, :], X[:, :, :], psY[:, :, :].rearrange("p a (i d) -> p (a i) d", d=P),
                                    ALU.add))
            n2.statistics(o, X)
            o.after(n2.apply(dve, X, X))
            o.after(v.tensor_tensor(X[:, :, :], X[:, :, :], w("g").unsqueeze(1).broadcast_to([P, TILES, P]),
                                    ALU.mult))
            o.after(v.tensor_tensor(X[:, :, :], X[:, :, :], w("b").unsqueeze(1).broadcast_to([P, TILES, P]),
                                    ALU.add))
            v.tensor_tensor(c.H[:, :, :], c.H[:, :, :], X[:, :, :], ALU.add)

        @block.tensor
        def _(pe):
            mm = nc.tensor.matmul
            tr = nc.tensor.transpose
            xt = XT[:, :, :].rearrange("p b l -> p (b l)")
            gs = psGS[:, :, :].rearrange("p a k -> p (a k)")
            pe.wait_ge(s["x"], 1)
            for i in range(TILES):
                ins = tr(gs[:, i * P:(i + 1) * P], X[:, i, :], c.ident[:, :])
            ins.then_inc(s["xps"], 1)
            pe.wait_ge(s["w"], 16)
            pe.wait_ge(s["xT"], 1)
            for j in range(PAIRS):
                ins = mm(gs[:, j * DHEADS:(j + 1) * DHEADS], xt[:, j * P:(j + 1) * P], w("beta"),
                         start=True, stop=True)
            ins.then_inc(s["bps"], 1)
            for j in range(PAIRS):
                if j >= 2:
                    pe.wait_ge(s["v"], j - 1)
                mm(psY[:, j % 2, :], xt[:, j * P:(j + 1) * P], w("v"), start=True, stop=True).then_inc(s["vps"], 1)
            def bank_read(h, u):
                n = unit(h, u)[0] - 2
                if n < 0:
                    pe.wait_ge(s["v"], PAIRS)
                    return
                _, m, _, _, roll = unit(n // YUNITS, n % YUNITS)
                if roll == 0:
                    pe.wait_ge(s["y0"], m + 1)
                else:
                    pe.wait_ge(s["z"], m * ROLLS + roll)

            def project(h, u):
                n, m, kq, half, roll = unit(h, u)
                bank_read(h, u)
                if u == 0:
                    pe.wait_ge(s["signed"], h + 1)
                col = at["roll"][0] + ((kq * DHEADS + h) * (ROLLS + 1) + roll) * FEAT
                mm(psY[:, n % 2, :], W[:, col:col + FEAT], xt[:, half * HALF:(half + 1) * HALF],
                   start=True, stop=True).then_inc(s["yps"], 1)

            def gram(h, j):
                if j == 0:
                    pe.wait_ge(s["z"], (h + 1) * 4 * ROLLS)
                    if h == 0:
                        pe.wait_ge(s["beta"], 1)
                        pe.wait_ge(s["ones"], 1)
                    else:
                        pe.wait_ge(s["gsread"], h)
                for r in range(ROLLS):
                    for b, rows in enumerate(lo_hi):
                        z = Z[:, h % ZBUFS, r, 2 * j + b, :]
                        ins = mm(psGS[rows, j, :], z[:, 0:SEQ], z[:, 1:], start=r == 0, stop=r == ROLLS - 1)
                if j == PAIRS - 1:
                    ins.then_inc(s["gs"], 1)

            work = (gram, nothing, project)
            prepare(work)
            for h in range(DHEADS):
                pe.wait_ge(s["lists"], 4 * h + 4)
                for k, (group, by) in enumerate(DSTEPS):
                    for chain in range(CHAINS):
                        if h > 0 or k > 1:
                            before = h * len(DSTEPS) + k - 2
                            done(pe, before // len(DSTEPS), before % len(DSTEPS), chain)
                        made_by = {STEP_OF[x] for name in group for x in OPERANDS[name] if x in STEP_OF and x != "O"}
                        for other in sorted(made_by):
                            done(pe, h, other, chain)
                        if group[0] == "O":
                            pe.wait_ge(s["gsread"], h + 1)
                        width = DDIM + 1 if group[0] == "O" else SEQ
                        for i, name in enumerate(group):
                            left, right = OPERANDS[name]
                            for jj in range(DMEMBERS):
                                col = (i * DMEMBERS + jj) * width
                                for rows in lo_hi:
                                    j = chain * DMEMBERS + jj
                                    lhs, rhs = matrix(left, h, j, rows), matrix(right, h, j, rows)
                                    dst = bank(h, k, chain)[rows, col:col + width]
                                    ins = mm(dst, lhs, rhs, start=True, stop=name != "dl")
                                    if name == "dl":
                                        ins = mm(dst, w("eye")[rows, :], rhs, start=False, stop=True)
                        if group[0] in QSUMS:
                            j = chain * DMEMBERS + QSUMS.index(group[0])
                            col = DMEMBERS * SEQ
                            for r in range(ROLLS):
                                for b, rows in enumerate(lo_hi):
                                    ins = mm(bank(h, k, chain)[rows, col:col + 1],
                                             Z[:, h % ZBUFS, r, 2 * j + b, SEQ:2 * SEQ], w("eps"),
                                             start=r == 0, stop=r == ROLLS - 1)
                        ins.then_inc(s["product"], 1)
                        fill(work, h, k * CHAINS + chain)
            for chain in range(CHAINS):
                done(pe, DHEADS - 1, STEP_OF["O"], chain)
            for j in range(PAIRS):
                if j >= 2:
                    pe.wait_ge(s["oT"], j - 1)
                flat = psM[:, j % 2, :]
                for k in range(4):
                    ins = tr(flat[:, k * P:(k + 1) * P],
                             O[:, j, 2 * k:2 * k + 2, :].rearrange("p h d -> p (h d)"), c.ident[:, :])
                ins.then_inc(s["ops"], 1)
            pe.wait_ge(s["oT"], PAIRS)
            pe.wait_ge(s["roll"], 16)
            for q in range(2):
                for k in range(4):
                    ins = mm(gs[:, q * HALF:(q + 1) * HALF], w("o")[:, k * P:(k + 1) * P],
                             OT[:, k, q * HALF:(q + 1) * HALF], start=k == 0, stop=k == 3)
            ins.then_inc(s["aps"], 1)
            pe.wait_ge(s["aT"], 1)
            for i in range(TILES):
                ins = tr(psY[:, i // 4, i % 4 * P:(i % 4 + 1) * P], AT[:, i * P:(i + 1) * P], c.ident[:, :])
            ins.then_inc(s["back"], 1)



GROUPS8, GHEADS, GDIM, LATENT = 8, 16, 128, 100
ZDIM = GROUPS8 * GHEADS * GDIM
FF2 = 2 * P
SPANS = P // 32
ROUNDS = GHEADS // 4
HALVES8 = GHEADS * PLACES // P
NORM_FLOOR = 1e-12
PRE_COLS = [("gamma", P), ("wk", GROUPS8 * P), ("bk", GROUPS8), ("aw1", GROUPS8 * LATENT), ("aw1_b", 1),
            ("aw2", LATENT), ("aw2_b", 1), ("aw2_row", LATENT), ("row", 2 * SPANS), ("same_row", P), ("span", SPANS),
            ("one", 1), ("w1_b", FF2), ("g2", FF2), ("w2", 2 * P), ("w2_b", P)]
GROUP_COLS = [("q", GHEADS * GDIM), ("k", GDIM), ("v", GDIM), ("bq", GHEADS), ("bk", 1), ("bv", 1),
              ("g1", GHEADS)]


def lay_grouped(np, x, A):
    g = {k[len("L3_ffn_"):]: v for k, v in x.items() if k.startswith("L3_ffn_")}
    wk, wv = g["Wkv_w"][:, :GROUPS8 * GDIM], g["Wkv_w"][:, GROUPS8 * GDIM:]
    bk, bv = g["Wkv_b"][:GROUPS8 * GDIM].reshape(GROUPS8, GDIM), g["Wkv_b"][GROUPS8 * GDIM:].reshape(GROUPS8, GDIM)
    t = np.arange(P)
    row = t // PLACES

    def tiled(a):
        return np.tile(a, (P, 1))

    A["g_pre"] = pack(np, PRE_COLS, {
        "gamma": tiled(g["gamma_norm"]), "bk": bk.T,
        "wk": np.transpose(wk.reshape(P, GROUPS8, GDIM), (2, 1, 0)).reshape(GDIM, GROUPS8 * P),
        "aw1": np.transpose(g["aw1_w"].reshape(GROUPS8, GDIM, LATENT), (1, 0, 2)).reshape(P, -1),
        "aw1_b": g["aw1_b"], "aw2": g["aw2_w"], "aw2_b": g["aw2_b"], "aw2_row": tiled(g["aw2_b"]),
        "row": (row[:, None] == np.arange(2 * SPANS)).astype(np.float32) * np.float32(GDIM ** -0.5),
        "same_row": (row[:, None] == row[None, :]).astype(np.float32),
        "span": (t[:, None] // 32 == np.arange(SPANS)).astype(np.float32), "one": np.ones((P, 1), np.float32),
        "w1_b": tiled(g["wz_b1"]), "g2": tiled(g["wz_g2"]),
        "w2": np.transpose(g["wz_w2"].reshape(2, P, P), (1, 0, 2)).reshape(P, 2 * P), "w2_b": tiled(g["wz_b2"])})
    per = []
    for i in range(GROUPS8):
        cols = slice(i * GHEADS * GDIM, (i + 1) * GHEADS * GDIM)
        per.append(pack(np, GROUP_COLS, {
            "q": g["Wq_w"][:, cols], "k": wk[:, i * GDIM:(i + 1) * GDIM], "v": wv[:, i * GDIM:(i + 1) * GDIM],
            "bq": g["Wq_b"][cols].reshape(GHEADS, GDIM).T, "bk": bk[i], "bv": bv[i],
            "g1": g["wz_g1"][cols].reshape(GHEADS, GDIM).T}))
    A["g_qkv"] = np.stack(per)
    A["g_w1"] = np.transpose(g["wz_w1"].reshape(GROUPS8, GHEADS, GDIM, FF2), (0, 2, 1, 3)).reshape(
        GROUPS8, P, GHEADS * FF2)


def grouped_attention(c, A):
    nc = c.nc
    at, n_pre = columns(PRE_COLS)
    gat, n_group = columns(GROUP_COLS)
    outer = ExitStack()
    with outer:
        W = c.sb("g_pre", [P, n_pre], outer)

        def w(part, rows=P):
            return W[0:rows, at[part][0]:at[part][1]]

        XT = c.sb("g_xT", [P, TOKENS], outer)
        wS = c.sb("g_wS", [P, TILES, 2, SPANS, LATENT], outer)
        wT = c.sb("g_wT", [LATENT, 2, ROWS, PLACES], outer)
        hacc = c.sb("g_hacc", [P, TILES, FF2], outer)
        dacc = c.sb("g_dacc", [P, TILES, 2 * PLACES], outer)
        G = c.sb("gh_qkv", [P, 2, n_group], outer)
        W1 = c.sb("gh_w1", [P, 2, GHEADS, FF2], outer)
        s_g = [c.sem(f"gh_qkv{i}") for i in range(2)]
        s_w = [c.sem(f"gh_w1_{i}") for i in range(2)]
        compress(c, A, W, w, XT, wS, wT, G, W1, s_g, s_w)
        heads(c, A, w, gat, G, W1, s_g, s_w, XT, wS, wT, hacc, dacc)
        project_out(c, w, hacc, dacc)


def compress(c, A, W, w, XT, wS, wT, G, W1, s_g, s_w):
    nc = c.nc
    with ExitStack() as st:
        def sb(name, shape):
            return c.sb("gc_" + name, shape, st)

        norm = Norm(c, "gc_n", st)
        X, sq = sb("x", [P, TILES, P]), sb("sq", [P, TILES, P])
        ss, rn = sb("ss", [P, TILES]), sb("rn", [P, TILES])
        M, m = sb("m", [P, LATENT]), sb("m_bias", [LATENT, 1])
        wcopy = sb("wcopy", [P, TILES, LATENT])
        A1 = sb("a1", [LATENT, TOKENS])
        wl, tk = sb("wl", [LATENT, ROWS, PLACES]), sb("tk", [P, TILES, LATENT])
        top, tot = sb("top", [P, TILES]), sb("tot", [P, TILES])
        topf, totf = sb("topf", [LATENT, ROWS]), sb("totf", [LATENT, ROWS])
        psT = c.ps("gc_psT", [P, TOKENS], st)
        psM = c.ps("gc_psM", [P, 2, HALF], st)
        psW = c.ps("gc_psW", [P, TOKENS], st)
        psX = c.ps("gc_psX", [P, 2, 4, P], st)
        names = ("w", "x", "ss", "rn", "xps", "xT", "mps", "m", "m_bias", "a1ps", "a1", "copied", "wps", "tok", "sub",
                 "exp",
                 "p1", "p1ps", "wl", "wlps", "lat", "sublat", "explat", "ord", "zero")
        s = {k: c.sem("gc_" + k) for k in names}
        block = st.enter_context(nc.Block())

        @block.sync
        def _(sp):
            sp.dma_start(W[:, :], A["g_pre"]).then_inc(s["w"], 16)
            for gg in range(2):
                sp.dma_start(G[:, gg, :], A["g_qkv"][gg, :, :]).then_inc(s_g[gg], 16)
                sp.dma_start(W1[:, gg, :, :].rearrange("p h f -> p (h f)"), A["g_w1"][gg, :, :]).then_inc(s_w[gg], 16)

        @block.gpsimd
        def _(pool):
            nc.gpsimd.memset(wT[:, :, :, :], 0.0).then_inc(s["zero"], 1)
            norm.power(pool)
            pool.wait_ge(s["ss"], 1)
            nc.gpsimd.tensor_tensor(rn[:, :], ss[:, :], c.half_neg[:, 0:TILES], ALU.pow).then_inc(s["rn"], 1)
            pool.wait_ge(s["copied"], 1)
            r = 2 * SPANS - 1
            nc.gpsimd.tensor_tensor(wS[:, :, r % 2, r // 2, :], wcopy[:, :, :],
                                    w("row")[:, r:r + 1].unsqueeze(2).broadcast_to([P, TILES, LATENT]), ALU.mult)

        @block.scalar
        def _(act):
            a = nc.scalar.activation
            act.wait_ge(s["xps"], 1)
            a(XT[:, :], psT[:, :], ACT.Copy).then_inc(s["xT"], 1)
            act.wait_ge(s["m_bias"], 1)
            act.wait_ge(s["a1ps"], 1)
            a(A1[:, :], psW[0:LATENT, :], ACT.Silu, bias=m[:, :]).then_inc(s["a1"], 1)
            act.wait_ge(s["wps"], 1)
            a(wl[:, :, :].rearrange("p b t -> p (b t)"), psT[0:LATENT, :], ACT.Identity, bias=w("aw2_b", LATENT)
              ).then_inc(s["lat"], 1)
            act.wait_ge(s["sub"], 1)
            a(tk[:, :, :], tk[:, :, :], ACT.Exp).then_inc(s["exp"], 1)
            act.wait_ge(s["sublat"], 1)
            a(wl[:, :, :], wl[:, :, :], ACT.Exp).then_inc(s["explat"], 1)
            act.wait_ge(s["copied"], 1)
            for r in range(4, 7):
                a(wS[:, :, r % 2, r // 2, :], wcopy[:, :, :], ACT.Identity, scale=w("row")[:, r:r + 1])

        @block.vector
        def _(dve):
            v = nc.vector
            o = Order(dve, s["ord"])
            norm.statistics(o, c.H)
            o.after(norm.apply(dve, X, c.H))
            o.after(v.tensor_tensor(sq[:, :, :], X[:, :, :], X[:, :, :], ALU.mult))
            o.after(v.tensor_reduce(ss[:, :], sq[:, :, :], AX, ALU.add))
            v.tensor_scalar_max(ss[:, :], ss[:, :], NORM_FLOOR ** 2).then_inc(s["ss"], 1)
            dve.wait_ge(s["w"], 16)
            dve.wait_ge(s["rn"], 1)
            for i in range(TILES):
                ins = v.tensor_scalar(X[:, i, :], X[:, i, :], rn[:, i:i + 1], float(P) ** 0.5, ALU.mult, ALU.mult)
            o.after(ins)
            v.tensor_tensor(X[:, :, :], X[:, :, :], w("gamma").unsqueeze(1).broadcast_to([P, TILES, P]), ALU.mult
                            ).then_inc(s["x"], 1)
            dve.wait_ge(s["mps"], 1)
            v.tensor_copy(M[:, :], psM[:, 0, 0:LATENT]).then_inc(s["m"], 1)
            v.tensor_tensor(m[:, :], psM[0:LATENT, 1, 0:1], w("aw1_b", LATENT), ALU.add).then_inc(s["m_bias"], 1)
            dve.wait_ge(s["wps"], 1)
            o.after(v.tensor_tensor(tk[:, :, :], psX[:, :, :, 0:LATENT].rearrange("p a i l -> p (a i) l"),
                                    w("aw2_row").unsqueeze(1).broadcast_to([P, TILES, LATENT]), ALU.add))
            o.after(v.tensor_reduce(top[:, :], tk[:, :, :], AX, ALU.max))
            v.tensor_tensor(tk[:, :, :], tk[:, :, :], top[:, :].unsqueeze(2).broadcast_to([P, TILES, LATENT]),
                            ALU.subtract).then_inc(s["sub"], 1)
            dve.wait_ge(s["lat"], 1)
            o.after(v.tensor_reduce(topf[:, :], wl[:, :, :], AX, ALU.max))
            v.tensor_tensor(wl[:, :, :], wl[:, :, :], topf[:, :].unsqueeze(2).broadcast_to([LATENT, ROWS, PLACES]),
                            ALU.subtract).then_inc(s["sublat"], 1)
            dve.wait_ge(s["exp"], 1)
            o.after(v.tensor_reduce(tot[:, :], tk[:, :, :], AX, ALU.add))
            o.after(v.reciprocal(tot[:, :], tot[:, :]))
            o.after(v.tensor_scalar_mul(tot[:, :], tot[:, :], 0.5 / PLACES))
            v.tensor_tensor(tk[:, :, :], tk[:, :, :], tot[:, :].unsqueeze(2).broadcast_to([P, TILES, LATENT]),
                            ALU.mult).then_inc(s["p1"], 1)
            dve.wait_ge(s["explat"], 1)
            o.after(v.tensor_reduce(totf[:, :], wl[:, :, :], AX, ALU.add))
            o.after(v.reciprocal(totf[:, :], totf[:, :]))
            o.after(v.tensor_scalar_mul(totf[:, :], totf[:, :], 0.5 / LATENT))
            o.after(v.tensor_tensor(wl[:, :, :], wl[:, :, :],
                                    totf[:, :].unsqueeze(2).broadcast_to([LATENT, ROWS, PLACES]), ALU.mult))
            dve.wait_ge(s["p1ps"], 1)
            v.tensor_tensor(wl[:, :, :].rearrange("p b t -> p (b t)"), wl[:, :, :].rearrange("p b t -> p (b t)"),
                            psW[0:LATENT, :], ALU.add).then_inc(s["wl"], 1)
            dve.wait_ge(s["wl"], 1)
            dve.wait_ge(s["zero"], 1)
            for par in range(2):
                rows = wl[:, :, :].rearrange("p (n r) t -> p n r t", r=2)[:, :, par, :]
                v.tensor_copy(wT[:, par, :, :].rearrange("p (n r) t -> p n r t", r=2)[:, :, par, :], rows)
            dve.wait_ge(s["wlps"], 1)
            v.tensor_copy(wcopy[:, :, :], psX[:, :, :, 0:LATENT].rearrange("p a i l -> p (a i) l")
                          ).then_inc(s["copied"], 1)
            dve.wait_ge(s["copied"], 1)
            for r in range(4):
                v.tensor_scalar_mul(wS[:, :, r % 2, r // 2, :], wcopy[:, :, :], w("row")[:, r:r + 1])

        @block.tensor
        def _(pe):
            mm, tr = nc.tensor.matmul, nc.tensor.transpose
            pe.wait_ge(s["w"], 16)
            for g in range(GROUPS8):
                aw1 = w("aw1")[:, g * LATENT:(g + 1) * LATENT]
                mm(psM[:, 0, 0:LATENT], w("wk")[:, g * P:(g + 1) * P], aw1, start=g == 0, stop=g == GROUPS8 - 1)
                ins = mm(psM[0:LATENT, 1, 0:1], aw1, w("bk")[:, g:g + 1], start=g == 0, stop=g == GROUPS8 - 1)
            ins.then_inc(s["mps"], 1)
            pe.wait_ge(s["x"], 1)
            transpose_tokens(c, psT, X).then_inc(s["xps"], 1)
            pe.wait_ge(s["m"], 1)
            pe.wait_ge(s["xT"], 1)
            for q in range(2):
                ins = mm(psW[0:LATENT, q * HALF:(q + 1) * HALF], M[:, :], XT[:, q * HALF:(q + 1) * HALF],
                         start=True, stop=True)
            ins.then_inc(s["a1ps"], 1)
            pe.wait_ge(s["a1"], 1)
            for q in range(2):
                mm(psT[0:LATENT, q * HALF:(q + 1) * HALF], w("aw2", LATENT), A1[:, q * HALF:(q + 1) * HALF],
                   start=True, stop=True)
            for i in range(TILES):
                ins = mm(psX[:, i // 4, i % 4, 0:LATENT], A1[:, i * P:(i + 1) * P], w("aw2", LATENT),
                         start=True, stop=True)
            ins.then_inc(s["wps"], 1)
            pe.wait_ge(s["p1"], 1)
            for i in range(TILES):
                ins = tr(psW[0:LATENT, i * P:(i + 1) * P], tk[:, i, :], c.ident[:, :])
            ins.then_inc(s["p1ps"], 1)
            pe.wait_ge(s["wl"], 1)
            flat = wl[:, :, :].rearrange("p b t -> p (b t)")
            for i in range(TILES):
                ins = tr(psX[:, i // 4, i % 4, 0:LATENT], flat[:, i * P:(i + 1) * P], c.ident[0:LATENT, 0:LATENT])
            ins.then_inc(s["wlps"], 1)


def heads(c, A, w, gat, G, W1, s_g, s_w, XT, wS, wT, hacc, dacc):
    nc = c.nc
    UNITS, TURN = GROUPS8 * TILES, 2 * TILES
    ROWCOLS = GHEADS * PLACES
    PREP = 8
    W1_PARTS = 4
    with ExitStack() as st:
        def sb(name, shape):
            return c.sb("gh_" + name, shape, st)

        KT, VT = sb("kT", [P, TOKENS]), sb("vT", [P, 2, TOKENS])
        V, VV = sb("v", [P, 2, TILES, GDIM]), sb("vv", [P, P])
        bqk = sb("bqk", [P, TILES, GHEADS])
        QT = sb("qT", [P, GHEADS, P])
        AT = sb("aT", [P, 2, ROWCOLS])
        PR = sb("p", [P, 2, 4, SPANS, LATENT])
        top, tot = sb("top", [P, 4, SPANS]), sb("tot", [P, 2, 4, SPANS])
        PT = sb("pT", [LATENT, SPANS, 2, ROWCOLS])
        BT = sb("bT", [P, 2, ROWCOLS])
        DD = sb("dd", [P, 2, ROWCOLS])
        dred = sb("dred", [P, 2, PLACES])
        zT = sb("zT", [P, GHEADS, 8, PLACES])
        psS = c.ps("gh_psS", [P, 4, HALF], st)
        psA = c.ps("gh_psA", [P, 2, ROWCOLS], st)
        psR = c.ps("gh_psR", [P, 2, HALF], st)
        psH = c.ps("gh_psH", [P, HALF], st)
        names = ("gzero", "round", "read", "aps", "aT", "sps", "max", "sub", "exp", "total", "inv", "norm", "vvps",
                 "vv", "bps", "bT", "zps", "zact", "zdve", "cps", "cread", "dred", "hps", "h", "w1s")
        s = {k: c.sem("gh_" + k) for k in names}
        block = st.enter_context(nc.Block())

        class Slot:

            def __init__(self, it, col):
                self.it, self.col = it, col
                known = isinstance(it, int)
                v = it * TURN + col if known else None
                self.opens = not known or v < UNITS
                self.mids = not known or 1 <= v <= UNITS
                self.closes = not known or 2 <= v
                self.later = not known or v >= 3
                self.preps = self.col % TILES == TILES - 1 and (not known or v < UNITS - 1)
                self.first = known and v == 0
                self.tile, self.group = col % TILES, col // TILES % 2
                self.mid_tile, self.mid_group = (col - 1) % TILES, (col - 1) // TILES % 2
                self.out_tile, self.out_group = (col - 2) % TILES, (col - 2) // TILES % 2
                self.base = PREP if self.first else 8 * col + 4 + PREP * (col // TILES)
                if known and v == UNITS:
                    self.base -= PREP

            def units(self, k):
                return self.it * TURN + (self.col + k)

            def rounds(self, k):
                return self.it * (8 * TURN + 2 * PREP) + (self.base + k)

            def loads(self, k):
                n = self.col // TILES + k
                return n % 2, self.it * 16 + (n // 2 + 1) * 16

        def slots(eng, body):
            for col in range(2):
                body(Slot(0, col))
            with eng.Fori(0, UNITS // TURN - 1) as it:
                for col in range(2, TURN + 2):
                    body(Slot(it, col))
            for col in range(2, TURN + 2):
                body(Slot(UNITS // TURN - 1, col))

        def g(gg, part):
            return G[:, gg, gat[part][0]:gat[part][1]]

        @block.sync
        def _(sp):
            with sp.Fori(1, GROUPS8 // 2) as it:
                for gg in range(2):
                    sp.wait_ge(s["aps"], it * TURN + (gg * TILES + TILES - TURN))
                    sp.wait_ge(s["w1s"], it * 2 * W1_PARTS + (gg + 1 - 2) * W1_PARTS)
                    sp.dma_start(G[:, gg, :], A["g_qkv"][bass.ds(it * 2 + gg, 1), :, :].rearrange("a p n -> (a p) n")
                                 ).then_inc(s_g[gg], 16)
                    sp.wait_ge(s["hps"], it * TURN + (gg * TILES + TILES - TURN))
                    sp.dma_start(W1[:, gg, :, :].rearrange("p h f -> p (h f)"),
                                 A["g_w1"][bass.ds(it * 2 + gg, 1), :, :].rearrange("a p n -> (a p) n")
                                 ).then_inc(s_w[gg], 16)

        @block.gpsimd
        def _(pool):
            def scale_w1(gg, part):
                hh = slice(part * GHEADS // W1_PARTS, (part + 1) * GHEADS // W1_PARTS)
                nc.gpsimd.tensor_tensor(W1[:, gg, hh, :], W1[:, gg, hh, :],
                                        g(gg, "g1")[:, hh].unsqueeze(2).broadcast_to([P, GHEADS // W1_PARTS, FF2]),
                                        ALU.mult).then_inc(s["w1s"], 1)

            nc.gpsimd.memset(hacc[:, :, :], 0.0).then_inc(s["gzero"], 1)
            nc.gpsimd.memset(dacc[:, :, :], 0.0).then_inc(s["gzero"], 1)

            def body(t):
                if t.first:
                    pool.wait_ge(s_g[0], 16)
                    pool.wait_ge(s_w[0], 16)
                    for part in range(W1_PARTS):
                        scale_w1(0, part)
                if t.opens:
                    pool.wait_ge(s["inv"], t.units(1))
                    b = t.col % 2
                    nc.gpsimd.tensor_tensor(PR[:, b, :, :, :], PR[:, b, :, :, :],
                                            tot[:, b, :, :].unsqueeze(3).broadcast_to([P, 4, SPANS, LATENT]),
                                            ALU.mult).then_inc(s["norm"], 1)
                part = t.tile - 3
                if 0 <= part < W1_PARTS and (not isinstance(t.it, int) or t.it * TURN + t.col < UNITS - TILES):
                    gg, loads = t.loads(1)
                    pool.wait_ge(s_g[gg], loads)
                    pool.wait_ge(s_w[gg], loads)
                    scale_w1(gg, part)

            slots(pool, body)

        @block.scalar
        def _(act):
            a = nc.scalar.activation

            def rounds(t, k, n, put):
                for r in range(n):
                    act.wait_ge(s["round"], t.rounds(k + r + 1))
                    put(r, psR[:, r % 2, :]).then_inc(s["read"], 1)

            def prep(t, k, gg):
                def put(r, bank):
                    q = r % 2
                    half = slice(q * HALF, (q + 1) * HALF)
                    if r < 2:
                        return a(KT[:, half], bank, ACT.Identity, bias=g(gg, "bk"))
                    if r < 4:
                        return a(VT[:, gg, half], bank, ACT.Identity, bias=g(gg, "bv"))
                    tiles = slice(q * TILES // 2, (q + 1) * TILES // 2)
                    if r < 6:
                        return a(bqk[:, tiles, :].rearrange("p i h -> p (i h)"), bank[:, 0:TILES // 2 * GHEADS],
                                 ACT.Copy)
                    return a(V[:, gg, tiles, :].rearrange("p i d -> p (i d)"), bank, ACT.Copy)
                rounds(t, k, PREP, put)

            def body(t):
                if t.first:
                    prep(t, -PREP, 0)
                k = 0
                if t.opens:
                    rounds(t, 0, ROUNDS, lambda r, bank: a(
                        QT[:, 4 * r:4 * r + 4, :].rearrange("p h t -> p (h t)"), bank, ACT.Copy))
                    k += ROUNDS
                if t.preps:
                    prep(t, k, 1 - t.group)
                    k += PREP
                if t.mids:
                    rounds(t, k, SPANS, lambda r, bank: a(
                        PT[:, r, :, :].rearrange("p a b -> p (a b)"), bank[0:LATENT, :], ACT.Copy))
                    act.wait_ge(s["bps"], t.units(0))
                    a(BT[:, :, :], psA[:, :, :], ACT.Copy).then_inc(s["bT"], 1)
                if t.opens:
                    act.wait_ge(s["sub"], t.units(1))
                    b = t.col % 2
                    a(PR[:, b, :, :, :], PR[:, b, :, :, :], ACT.Exp).then_inc(s["exp"], 1)
                if t.mids:
                    act.wait_ge(s["zps"], t.units(0))
                    for q in (0, 1):
                        ins = a(zT[:, :, 2 * q:2 * q + 2, :].rearrange("p h r t -> p r h t"),
                                psS[:, q, :].rearrange("p (r h t) -> p r h t", r=2, h=GHEADS), ACT.Copy)
                    ins.then_inc(s["zact"], 1)

            slots(act, body)

        @block.vector
        def _(dve):
            v = nc.vector

            def body(t):
                b = t.col % 2
                if t.opens:
                    dve.wait_ge(s["aps"], t.units(1))
                    v.tensor_tensor(AT[:, :, :].rearrange("p r (h t) -> p r h t", t=PLACES),
                                    psA[:, :, :].rearrange("p r (h t) -> p r h t", t=PLACES),
                                    bqk[:, t.tile, :].unsqueeze(1).unsqueeze(3)
                                    .broadcast_to([P, 2, GHEADS, PLACES]), ALU.add).then_inc(s["aT"], 1)
                    sc = psS[:, :, 0:SPANS * LATENT].rearrange("p j (q l) -> p j q l", l=LATENT)
                    dve.wait_ge(s["sps"], t.units(1))
                    v.tensor_reduce(top[:, :, :], sc, AX, ALU.max).then_inc(s["max"], 1)
                if t.mids:
                    dve.wait_ge(s["vvps"], t.units(0))
                    v.tensor_tensor(VV[:, :], psA[:, 0, 0:P], w("same_row"), ALU.mult).then_inc(s["vv"], 1)
                if t.opens:
                    dve.wait_ge(s["max"], t.units(1))
                    v.tensor_tensor(PR[:, b, :, :, :], sc,
                                    top[:, :, :].unsqueeze(3).broadcast_to([P, 4, SPANS, LATENT]), ALU.subtract
                                    ).then_inc(s["sub"], 1)
                    dve.wait_ge(s["exp"], t.units(1))
                    v.tensor_reduce(tot[:, b, :, :], PR[:, b, :, :, :], AX, ALU.add).then_inc(s["total"], 1)
                    dve.wait_ge(s["total"], t.units(1))
                    v.reciprocal(tot[:, b, :, :], tot[:, b, :, :]).then_inc(s["inv"], 1)
                if t.closes:
                    dve.wait_ge(s["hps"], t.units(-1))
                    v.tensor_tensor(hacc[:, t.out_tile, :], hacc[:, t.out_tile, :], psH[:, 0:FF2], ALU.add
                                    ).then_inc(s["h"], 1)
                if t.mids:
                    dve.wait_ge(s["zps"], t.units(0))
                    for q in (2, 3):
                        ins = v.tensor_copy(zT[:, :, 2 * q:2 * q + 2, :].rearrange("p h r t -> p r h t"),
                                            psS[:, q, :].rearrange("p (r h t) -> p r h t", r=2, h=GHEADS))
                    ins.then_inc(s["zdve"], 1)
                    dve.wait_ge(s["cps"], t.units(0))
                    v.tensor_tensor(DD[:, :, :], BT[:, :, :], psA[:, :, :], ALU.mult).then_inc(s["cread"], 1)
                    dve.wait_ge(s["cread"], t.units(0))
                    v.tensor_reduce(dred[:, :, :], DD[:, :, :].rearrange("p r (h t) -> p r t h", t=PLACES), AX,
                                    ALU.add).then_inc(s["dred"], 1)
                    dve.wait_ge(s["dred"], t.units(0))
                    v.tensor_tensor(dacc[:, t.mid_tile, :], dacc[:, t.mid_tile, :],
                                    dred[:, :, :].rearrange("p r t -> p (r t)"), ALU.add)

            dve.wait_ge(s["gzero"], 2)
            slots(dve, body)

        @block.tensor
        def _(pe):
            mm, tr = nc.tensor.matmul, nc.tensor.transpose

            def round_(t, k, r, put, first=False):
                if not (first and r < 2):
                    pe.wait_ge(s["read"], t.rounds(k + r - 1))
                put(r, psR[:, r % 2, :]).then_inc(s["round"], 1)

            def prep(t, k, gg, loads):
                pe.wait_ge(s_g[gg], loads)

                def put(r, bank):
                    q = r % 2
                    half = slice(q * HALF, (q + 1) * HALF)
                    if r < 4:
                        return mm(bank, g(gg, "kv"[r // 2]), XT[:, half], start=True, stop=True)
                    if r == 6:
                        pe.wait_ge(s["read"], t.rounds(k + 4))
                    if r == 4:
                        pe.wait_ge(s["read"], t.rounds(k + 3))
                    for j in range(TILES // 2):
                        i = q * TILES // 2 + j
                        if r < 6:
                            ins = mm(bank[:, j * GHEADS:(j + 1) * GHEADS], KT[:, i * P:(i + 1) * P], g(gg, "bq"),
                                     start=True, stop=True)
                        else:
                            ins = tr(bank[:, j * P:(j + 1) * P], VT[:, gg, i * P:(i + 1) * P], c.ident[:, :])
                    return ins

                for r in range(PREP):
                    round_(t, k, r, put, first=t.first)

            def body(t):
                pieces = [3, 3, 2, 3, 2, 3]
                done = [0]

                def out_heads():
                    if not t.closes:
                        return
                    if done[0] == 0:
                        pe.wait_ge(s["zact"], t.units(-1))
                        pe.wait_ge(s["zdve"], t.units(-1))
                        if t.later:
                            pe.wait_ge(s["h"], t.units(-2))
                        if t.out_tile == 0:
                            n = (t.col - 2) // TILES + 1
                            pe.wait_ge(s["w1s"], t.it * 2 * W1_PARTS + n * W1_PARTS)
                    for h in range(done[0], done[0] + pieces[0]):
                        ins = mm(psH[:, 0:FF2], zT[:, h, :, :].rearrange("p r t -> p (r t)"),
                                 W1[:, t.out_group, h, :], start=h == 0, stop=h == GHEADS - 1)
                    done[0] += pieces.pop(0)
                    if not pieces:
                        ins.then_inc(s["hps"], 1)

                if t.first:
                    prep(t, -PREP, 0, 16)
                k = 0
                if t.opens:
                    if t.tile == 0:
                        gg, loads = t.loads(0)
                        pe.wait_ge(s_g[gg], loads)

                    def queries(r, bank):
                        for h in range(4):
                            lo = gat["q"][0] + (4 * r + h) * GDIM
                            ins = mm(bank[:, h * P:(h + 1) * P], G[:, t.group, lo:lo + GDIM],
                                     XT[:, t.tile * P:(t.tile + 1) * P], start=True, stop=True)
                        return ins
                    for r in range(ROUNDS):
                        round_(t, 0, r, queries)
                    k += ROUNDS
                out_heads()
                if t.opens:
                    pe.wait_ge(s["read"], t.rounds(ROUNDS))
                    if t.closes:
                        pe.wait_ge(s["cread"], t.units(-1))
                    for q in range(SPANS):
                        lo = t.tile * P + q * 32
                        for par in range(2):
                            row = 2 * q + par
                            ins = mm(psA[q * 32:(q + 1) * 32, par, :], KT[:, lo:lo + 32],
                                     QT[:, :, row * PLACES:(row + 1) * PLACES], start=True, stop=True)
                    ins.then_inc(s["aps"], 1)
                out_heads()
                if t.opens:
                    pe.wait_ge(s["aT"], t.units(1))
                    for j in range(4):
                        par, hh = j // 2, j % 2
                        ins = mm(psS[:, j, 0:SPANS * LATENT], AT[:, par, hh * P:(hh + 1) * P],
                                 wS[:, t.tile, par, :, :].rearrange("p q l -> p (q l)"), start=True, stop=True)
                    ins.then_inc(s["sps"], 1)
                if t.preps:
                    gg, loads = t.loads(1)
                    prep(t, k, gg, loads)
                    k += PREP
                if t.mids:
                    if t.closes:
                        pe.wait_ge(s["cread"], t.units(-1))
                    mm(psA[:, 0, 0:P], VT[:, t.mid_group, t.mid_tile * P:(t.mid_tile + 1) * P],
                       VT[:, t.mid_group, t.mid_tile * P:(t.mid_tile + 1) * P], start=True, stop=True
                       ).then_inc(s["vvps"], 1)
                    pe.wait_ge(s["norm"], t.units(0))

                    def turned(q, bank):
                        for j in range(4):
                            ins = tr(bank[0:LATENT, j * P:(j + 1) * P], PR[:, (t.col - 1) % 2, j, q, :],
                                     c.ident[:, :])
                        return ins
                    for q in range(SPANS):
                        round_(t, k, q, turned)
                        if q in (1, 2):
                            out_heads()
                else:
                    out_heads()
                    out_heads()
                out_heads()
                if t.mids:
                    pe.wait_ge(s["read"], t.rounds(k + SPANS))
                    pe.wait_ge(s["vv"], t.units(0))
                    cols = wT[:, :, :, :].rearrange("p r b t -> p r (b t)")
                    for par in range(2):
                        for q in range(SPANS):
                            lo = t.mid_tile * P + q * 32
                            ins = mm(psA[q * 32:(q + 1) * 32, par, :], cols[:, par, lo:lo + 32], PT[:, q, par, :],
                                     start=True, stop=True)
                    ins.then_inc(s["bps"], 1)
                out_heads()
                if t.mids:
                    pe.wait_ge(s["bT"], t.units(0))
                    if t.opens:
                        pe.wait_ge(s["sub"], t.units(1))
                    for par in range(2):
                        for q in range(SPANS):
                            span = slice(q * 32, (q + 1) * 32)
                            ins = mm(psS[:, q, par * ROWCOLS:(par + 1) * ROWCOLS],
                                     V[span, t.mid_group, t.mid_tile, :], BT[span, par, :], start=True, stop=True)
                    ins.then_inc(s["zps"], 1)
                    mm(psA[:, :, :], VV[:, :], BT[:, :, :], start=True, stop=True).then_inc(s["cps"], 1)

            slots(pe, body)


def project_out(c, w, hacc, dacc):
    nc = c.nc
    with ExitStack() as st:
        def sb(name, shape):
            return c.sb("go_" + name, shape, st)

        E = sb("e", [P, TILES, SPANS, 2 * PLACES])
        n2, rz, ss, rh = (sb(n, [P, TILES]) for n in ("n2", "rz", "ss", "rh"))
        h1, sq = sb("h1", [P, TILES, FF2]), sb("sq", [P, TILES, FF2])
        hT = sb("hT", [P, 2, TOKENS])
        out = sb("out", [P, TILES, P])
        psN = c.ps("go_psN", [P, TILES], st)
        psT = c.ps("go_psT", [P, 2, TOKENS], st)
        psO = c.ps("go_psO", [P, TOKENS], st)
        names = ("e", "n2ps", "n2", "rz", "pre", "h1", "ss", "rh", "h1n", "tps", "hT", "ops", "sum", "silu", "ord")
        s = {k: c.sem("go_" + k) for k in names}
        block = st.enter_context(nc.Block())

        @block.gpsimd
        def _(pool):
            pool.wait_ge(s["n2"], 1)
            nc.gpsimd.tensor_tensor(rz[:, :], n2[:, :], c.half_neg[:, 0:TILES], ALU.pow).then_inc(s["rz"], 1)
            pool.wait_ge(s["ss"], 1)
            nc.gpsimd.tensor_tensor(rh[:, :], ss[:, :], c.half_neg[:, 0:TILES], ALU.pow).then_inc(s["rh"], 1)

        @block.scalar
        def _(act):
            a = nc.scalar.activation
            act.wait_ge(s["pre"], 1)
            a(h1[:, :, :], hacc[:, :, :], ACT.Silu).then_inc(s["h1"], 1)
            act.wait_ge(s["tps"], 1)
            a(hT[:, :, :], psT[:, :, :], ACT.Copy).then_inc(s["hT"], 1)
            act.wait_ge(s["sum"], 1)
            a(out[:, :, :], out[:, :, :], ACT.Silu).then_inc(s["silu"], 1)

        @block.vector
        def _(dve):
            v = nc.vector
            o = Order(dve, s["ord"])
            for i in range(TILES):
                ins = v.tensor_tensor(E[:, i, :, :], dacc[:, i, :].unsqueeze(1).broadcast_to([P, SPANS, 2 * PLACES]),
                                      w("span").unsqueeze(2).broadcast_to([P, SPANS, 2 * PLACES]), ALU.mult)
            ins.then_inc(s["e"], 1)
            dve.wait_ge(s["n2ps"], 1)
            v.tensor_scalar_max(n2[:, :], psN[:, :], NORM_FLOOR ** 2).then_inc(s["n2"], 1)
            dve.wait_ge(s["rz"], 1)
            for i in range(TILES):
                ins = v.tensor_scalar(hacc[:, i, :], hacc[:, i, :], rz[:, i:i + 1], float(ZDIM) ** 0.5,
                                      ALU.mult, ALU.mult)
            o.after(ins)
            v.tensor_tensor(hacc[:, :, :], hacc[:, :, :], w("w1_b").unsqueeze(1).broadcast_to([P, TILES, FF2]),
                            ALU.add).then_inc(s["pre"], 1)
            dve.wait_ge(s["h1"], 1)
            o.after(v.tensor_tensor(sq[:, :, :], h1[:, :, :], h1[:, :, :], ALU.mult))
            o.after(v.tensor_reduce(ss[:, :], sq[:, :, :], AX, ALU.add))
            v.tensor_scalar_max(ss[:, :], ss[:, :], NORM_FLOOR ** 2).then_inc(s["ss"], 1)
            dve.wait_ge(s["rh"], 1)
            for i in range(TILES):
                ins = v.tensor_scalar(h1[:, i, :], h1[:, i, :], rh[:, i:i + 1], float(FF2) ** 0.5,
                                      ALU.mult, ALU.mult)
            o.after(ins)
            v.tensor_tensor(h1[:, :, :], h1[:, :, :], w("g2").unsqueeze(1).broadcast_to([P, TILES, FF2]), ALU.mult
                            ).then_inc(s["h1n"], 1)
            dve.wait_ge(s["ops"], 1)
            v.tensor_tensor(out[:, :, :], psO[:, :].rearrange("p (i d) -> p i d", d=P),
                            w("w2_b").unsqueeze(1).broadcast_to([P, TILES, P]), ALU.add).then_inc(s["sum"], 1)
            dve.wait_ge(s["silu"], 1)
            v.tensor_tensor(c.H[:, :, :], c.H[:, :, :], out[:, :, :], ALU.add)

        @block.tensor
        def _(pe):
            mm, tr = nc.tensor.matmul, nc.tensor.transpose
            pe.wait_ge(s["e"], 1)
            for i in range(TILES):
                ins = mm(psN[:, i:i + 1], E[:, i, :, :].rearrange("p q t -> p (q t)"), w("one"),
                         start=True, stop=True)
            ins.then_inc(s["n2ps"], 1)
            pe.wait_ge(s["h1n"], 1)
            for k in range(2):
                for i in range(TILES):
                    ins = tr(psT[:, k, i * P:(i + 1) * P], h1[:, i, k * P:(k + 1) * P], c.ident[:, :])
            ins.then_inc(s["tps"], 1)
            pe.wait_ge(s["hT"], 1)
            for i in range(TILES):
                for k in range(2):
                    ins = mm(psO[:, i * P:(i + 1) * P], hT[:, k, i * P:(i + 1) * P], w("w2")[:, k * P:(k + 1) * P],
                             start=k == 0, stop=k == 1)
            ins.then_inc(s["ops"], 1)



def build(nc, A, out):
    layers = [token_embedding, mamba, switch_experts, delta_attention, lstm_experts, linear_attention,
              binned_experts, causal_attention, grouped_attention]
    with ExitStack() as stack:
        c = Chip(nc, stack)
        c.H = c.sb("stream", [P, TILES, P])
        c.ident = c.sb("ident", [P, P])
        c.half_neg = c.sb("half_neg", [P, 2 * TILES])
        for layer in layers:
            if layer is linear_attention:
                c.renew()
            layer(c, A)
        finish(c, out)
        c.sems.close()


def lay_out(x):
    import numpy as np
    A = {}
    w = np.transpose(x["L0_tok_weight"], (1, 0, 2)).reshape(GENES, EMB)
    A["genes"] = np.concatenate([w, x["L0_tok_mask"], np.transpose(x["x"])], axis=1).reshape(
        GENE_TILES, GENE_P, EMB_ROW)
    A["tok_bias"] = x["L0_tok_bias"].reshape(1, EMB)
    for lay in (lay_mamba, lay_switch, lay_delta, lay_lstm, lay_linear, lay_binned, lay_causal, lay_grouped):
        lay(np, x, A)
    return {k: np.ascontiguousarray(v) for k, v in A.items()}


def kernel(**inputs):
    import numpy as np
    import concourse.bacc as bacc
    from concourse.bass_utils import run_bass_kernel_spmd

    x = {k: np.asarray(v) for k, v in inputs.items()}
    arrays = lay_out(x)
    nc = bacc.Bacc("TRN2", target_bir_lowering=False, num_devices=1)
    A = {k: nc.dram_tensor("in_" + k, list(a.shape), F32, kind="ExternalInput").ap() for k, a in arrays.items()}
    feed = {"in_" + k: a for k, a in arrays.items()}
    out = nc.dram_tensor("out_0", [ROWS, PLACES, P], F32, kind="ExternalOutput").ap()
    build(nc, A, out)
    r = run_bass_kernel_spmd(nc, [feed], core_ids=[0])
    return r.results[0]["out_0"]
```
